# Optimizing a Trainium2 kernel written in Bass

```python
import numpy as np
import jax
import jax.numpy as jnp

def _softmax(x, axis=-1):
    return jax.nn.softmax(x, axis=axis)

def _gelu(x):
    return jax.nn.gelu(x, approximate=True)

def _silu(x):
    return jax.nn.silu(x)

def _sigmoid(x):
    return jax.nn.sigmoid(x)

def _layernorm(x, axis=-1, eps=1e-05):
    m = jnp.mean(x, axis=axis, keepdims=True)
    v = jnp.var(x, axis=axis, keepdims=True)
    return (x - m) / jnp.sqrt(v + eps)

def _scatter_add(tgt, idx, src, axis=0):
    return tgt.at[idx].add(src)

def _segment_sum(src, seg, n):
    return jax.ops.segment_sum(src, seg, n)
kernel_name = 'mk_gps_d1_gnn_r8_919e3d'

def setup_inputs(seed: int=0):
    np.random.seed(seed)
    _w = jnp.asarray

    def _rec_inputs():
        import jax
        import jax.numpy as jnp
        _gk = jax.random.key(seed)
        x = -0.0003713 + 1 * jax.random.normal(jax.random.fold_in(_gk, 1), (6250, 256), jnp.float32)
        _s = jax.random.randint(jax.random.fold_in(_gk, 2), (100000,), 0, 6250, jnp.int32)
        _d = jax.random.randint(jax.random.fold_in(_gk, 3), (100000,), 0, 6250, jnp.int32)
        _loop = jnp.arange(6250, dtype=jnp.int32)
        src = jnp.concatenate([_s, _d, _loop])
        dst = jnp.concatenate([_d, _s, _loop])
        _o = jnp.argsort(dst, stable=True)
        src = src[_o]
        dst = dst[_o]
        edge_weight = -7.32377e-05 + 0.176746 * jax.random.normal(jax.random.fold_in(_gk, 12), (206250,), jnp.float32)
        return (x, src, dst, edge_weight)
    x, src, dst, edge_weight = _rec_inputs()

    def _L0_gnn_setup():
        import jax, jax.numpy as jnp
        import numpy as np
        N_NODES = 6250
        NNZ = 200000
        D_FEAT = 256
        key = jax.random.key(seed)
        k_x, k_v, k_r, k_c = jax.random.split(key, 4)
        x = jax.random.normal(k_x, (N_NODES, D_FEAT), dtype=jnp.float32)
        std = 1.0 / np.sqrt(NNZ / N_NODES)
        values = jax.random.normal(k_v, (NNZ,), dtype=jnp.float32) * std
        row = jax.random.randint(k_r, (NNZ,), 0, N_NODES, dtype=jnp.int64)
        col = jax.random.randint(k_c, (NNZ,), 0, N_NODES, dtype=jnp.int64)
        return {'x': x, 'values': values, 'row': row, 'col': col}
    _L0_gnn_all = _L0_gnn_setup()
    _L0_gnn_in = {k: v for k, v in _L0_gnn_all.items() if k in ()}
    del _L0_gnn_all

    def _L0_mix_setup():
        import jax, jax.numpy as jnp
        import numpy as np
        N, F, C, H = (32, 512, 256, 8)
        D = C // H
        EPS_ATTN = 1e-06
        EPS_LN = 1e-05

        def layer_norm(x, g, b):
            mu = jnp.mean(x, axis=-1, keepdims=True)
            var = jnp.var(x, axis=-1, keepdims=True)
            return (x - mu) * jax.lax.rsqrt(var + EPS_LN) * g + b
        key = jax.random.key(seed)
        ks = jax.random.split(key, 8)
        s = 1.0 / np.sqrt(C)
        return {'x': jax.random.normal(ks[0], (N, F, C), jnp.float32), 'Wqkv': jax.random.uniform(ks[1], (3 * C, C), jnp.float32, -s, s), 'ln1_g': jnp.ones((C,), jnp.float32), 'ln1_b': jnp.zeros((C,), jnp.float32), 'W1': jax.random.uniform(ks[2], (C, C), jnp.float32, -s, s), 'b1': jax.random.uniform(ks[3], (C,), jnp.float32, -s, s), 'W2': jax.random.uniform(ks[4], (C, C), jnp.float32, -s, s), 'b2': jax.random.uniform(ks[5], (C,), jnp.float32, -s, s), 'ln2_g': jnp.ones((C,), jnp.float32), 'ln2_b': jnp.zeros((C,), jnp.float32)}
    _L0_mix_all = _L0_mix_setup()
    _L0_mix_in = {k: v for k, v in _L0_mix_all.items() if k in ('Wqkv', 'ln1_g', 'ln1_b', 'W1', 'b1', 'W2', 'b2', 'ln2_g', 'ln2_b')}
    del _L0_mix_all

    def _L0_ffn_setup():
        import jax, jax.numpy as jnp
        import numpy as np
        DIM = 256
        H = 8
        D = 64
        G = 64
        INNER = H * D
        SCALE = D ** (-0.5)
        key = jax.random.key(seed)
        ks = jax.random.split(key, 12)
        B, N = (4, 2048)
        x = jax.random.normal(ks[0], (B, N, DIM), dtype=jnp.float32)
        s = lambda fan_in: 1.0 / np.sqrt(fan_in)
        W_fx = jax.random.normal(ks[1], (DIM, INNER), dtype=jnp.float32) * s(DIM)
        b_fx = jnp.zeros((INNER,), dtype=jnp.float32)
        W_x = jax.random.normal(ks[2], (DIM, INNER), dtype=jnp.float32) * s(DIM)
        b_x = jnp.zeros((INNER,), dtype=jnp.float32)
        A = jax.random.normal(ks[3], (G, D), dtype=jnp.float32)
        Q, _ = jnp.linalg.qr(A.T)
        W_slice = Q[:, :G].astype(jnp.float32)
        b_slice = jnp.zeros((G,), dtype=jnp.float32)
        W_q = jax.random.normal(ks[4], (D, D), dtype=jnp.float32) * s(D)
        W_k = jax.random.normal(ks[5], (D, D), dtype=jnp.float32) * s(D)
        W_v = jax.random.normal(ks[6], (D, D), dtype=jnp.float32) * s(D)
        W_out = jax.random.normal(ks[7], (INNER, DIM), dtype=jnp.float32) * s(INNER)
        b_out = jnp.zeros((DIM,), dtype=jnp.float32)
        temperature = jnp.ones((1, H, 1, 1), dtype=jnp.float32) * 0.5
        return {'x': x, 'W_fx': W_fx, 'b_fx': b_fx, 'W_x': W_x, 'b_x': b_x, 'W_slice': W_slice, 'b_slice': b_slice, 'W_q': W_q, 'W_k': W_k, 'W_v': W_v, 'W_out': W_out, 'b_out': b_out, 'temperature': temperature}
    _L0_ffn_all = _L0_ffn_setup()
    _L0_ffn_in = {k: v for k, v in _L0_ffn_all.items() if k in ('W_fx', 'b_fx', 'W_x', 'b_x', 'W_slice', 'b_slice', 'W_q', 'W_k', 'W_v', 'W_out', 'b_out', 'temperature')}
    del _L0_ffn_all
    return {'x': x, 'src': src, 'dst': dst, 'edge_weight': edge_weight, 'L0_mix_Wqkv': _L0_mix_in['Wqkv'], 'L0_mix_ln1_g': _L0_mix_in['ln1_g'], 'L0_mix_ln1_b': _L0_mix_in['ln1_b'], 'L0_mix_W1': _L0_mix_in['W1'], 'L0_mix_b1': _L0_mix_in['b1'], 'L0_mix_W2': _L0_mix_in['W2'], 'L0_mix_b2': _L0_mix_in['b2'], 'L0_mix_ln2_g': _L0_mix_in['ln2_g'], 'L0_mix_ln2_b': _L0_mix_in['ln2_b'], 'L0_ffn_W_fx': _L0_ffn_in['W_fx'], 'L0_ffn_b_fx': _L0_ffn_in['b_fx'], 'L0_ffn_W_x': _L0_ffn_in['W_x'], 'L0_ffn_b_x': _L0_ffn_in['b_x'], 'L0_ffn_W_slice': _L0_ffn_in['W_slice'], 'L0_ffn_b_slice': _L0_ffn_in['b_slice'], 'L0_ffn_W_q': _L0_ffn_in['W_q'], 'L0_ffn_W_k': _L0_ffn_in['W_k'], 'L0_ffn_W_v': _L0_ffn_in['W_v'], 'L0_ffn_W_out': _L0_ffn_in['W_out'], 'L0_ffn_b_out': _L0_ffn_in['b_out'], 'L0_ffn_temperature': _L0_ffn_in['temperature']}

def reference(x, src, dst, edge_weight, L0_mix_Wqkv, L0_mix_ln1_g, L0_mix_ln1_b, L0_mix_W1, L0_mix_b1, L0_mix_W2, L0_mix_b2, L0_mix_ln2_g, L0_mix_ln2_b, L0_ffn_W_fx, L0_ffn_b_fx, L0_ffn_W_x, L0_ffn_b_x, L0_ffn_W_slice, L0_ffn_b_slice, L0_ffn_W_q, L0_ffn_W_k, L0_ffn_W_v, L0_ffn_W_out, L0_ffn_b_out, L0_ffn_temperature):
    import jax
    import jax.numpy as jnp

    def _L0_gnn_ref(x, values, row, col):
        import jax, jax.numpy as jnp
        import numpy as np
        N_NODES = 6250
        NNZ = 200000
        D_FEAT = 256
        msgs = values[:, None] * x[col]
        out = jax.ops.segment_sum(msgs, row, num_segments=N_NODES)
        return out

    def _L0_mix_ref(x, Wqkv, ln1_g, ln1_b, W1, b1, W2, b2, ln2_g, ln2_b):
        import jax, jax.numpy as jnp
        import numpy as np
        N, F, C, H = (32, 512, 256, 8)
        D = C // H
        EPS_ATTN = 1e-06
        EPS_LN = 1e-05

        def layer_norm(x, g, b):
            mu = jnp.mean(x, axis=-1, keepdims=True)
            var = jnp.var(x, axis=-1, keepdims=True)
            return (x - mu) * jax.lax.rsqrt(var + EPS_LN) * g + b
        n, f, c = x.shape
        qkv = jnp.einsum('nfc,oc->nfo', x, Wqkv)
        q, k, v = jnp.split(qkv, 3, axis=-1)
        q = q.reshape(n, f, H, D)
        k = k.reshape(n, f, H, D)
        v = v.reshape(n, f, H, D)
        q = jax.nn.elu(q) + 1.0
        k = jax.nn.elu(k) + 1.0
        kv = jnp.einsum('nshd,nshm->nhmd', k, v)
        ksum = jnp.sum(k, axis=1)
        z = 1.0 / (jnp.einsum('nlhd,nhd->nlh', q, ksum) + EPS_ATTN)
        t = jnp.einsum('nlhd,nhmd,nlh->nlhm', q, kv, z)
        t = t.reshape(n, f, c)
        x1 = layer_norm(t + x, ln1_g, ln1_b)
        h = jax.nn.gelu(jnp.einsum('nfc,oc->nfo', x1, W1) + b1, approximate=False)
        y = jnp.einsum('nfc,oc->nfo', h, W2) + b2
        return layer_norm(y + x1, ln2_g, ln2_b)

    def _L0_ffn_ref(x, W_fx, b_fx, W_x, b_x, W_slice, b_slice, W_q, W_k, W_v, W_out, b_out, temperature):
        import jax, jax.numpy as jnp
        import numpy as np
        DIM = 256
        H = 8
        D = 64
        G = 64
        INNER = H * D
        SCALE = D ** (-0.5)
        B, N, _ = x.shape
        fx_mid = (x @ W_fx + b_fx).reshape(B, N, H, D).transpose(0, 2, 1, 3)
        x_mid = (x @ W_x + b_x).reshape(B, N, H, D).transpose(0, 2, 1, 3)
        temp = jnp.clip(temperature, 0.1, 5.0)
        slice_weights = jax.nn.softmax((x_mid @ W_slice + b_slice) / temp, axis=-1)
        slice_norm = slice_weights.sum(axis=2)
        slice_token = jnp.einsum('bhnc,bhng->bhgc', fx_mid, slice_weights)
        slice_token = slice_token / (slice_norm[..., None] + 1e-05)
        q = slice_token @ W_q
        k = slice_token @ W_k
        v = slice_token @ W_v
        attn = jax.nn.softmax(jnp.einsum('bhgc,bhkc->bhgk', q, k) * SCALE, axis=-1)
        out_slice = jnp.einsum('bhgk,bhkc->bhgc', attn, v)
        out_x = jnp.einsum('bhgc,bhng->bhnc', out_slice, slice_weights)
        out_x = out_x.transpose(0, 2, 1, 3).reshape(B, N, INNER)
        return out_x @ W_out + b_out
    xn = _layernorm(x, axis=-1)
    x = x + _L0_gnn_ref(xn, edge_weight, src, dst) + _L0_mix_ref(xn[None], L0_mix_Wqkv, L0_mix_ln1_g, L0_mix_ln1_b, L0_mix_W1, L0_mix_b1, L0_mix_W2, L0_mix_b2, L0_mix_ln2_g, L0_mix_ln2_b)[0]
    x = x + _L0_ffn_ref(_layernorm(x, axis=-1)[None], L0_ffn_W_fx, L0_ffn_b_fx, L0_ffn_W_x, L0_ffn_b_x, L0_ffn_W_slice, L0_ffn_b_slice, L0_ffn_W_q, L0_ffn_W_k, L0_ffn_W_v, L0_ffn_W_out, L0_ffn_b_out, L0_ffn_temperature)[0]
    return x

_drawn_inputs = setup_inputs


def setup_inputs(seed=0):
    import zlib

    import numpy as np

    out = dict(_drawn_inputs(seed))
    spreads = {'L0_mix_ln1_g': (1.0, 0.2),
     'L0_mix_ln1_b': (0.0, 0.1),
     'L0_mix_ln2_g': (1.0, 0.2),
     'L0_mix_ln2_b': (0.0, 0.1),
     'L0_ffn_b_fx': (0.0, 0.1),
     'L0_ffn_b_x': (0.0, 0.8),
     'L0_ffn_b_slice': (0.0, 0.8),
     'L0_ffn_b_out': (0.0, 0.1),
     'L0_ffn_temperature': (0.5, 0.6)}
    factors = {'L0_mix_Wqkv': 8.0,
     'L0_mix_b1': 8.0,
     'L0_mix_b2': 3.329,
     'L0_ffn_W_x': 8.0,
     'L0_ffn_W_slice': 8.0,
     'L0_ffn_W_q': 8.0,
     'L0_ffn_W_k': 8.0}
    for name, (base, spread) in spreads.items():
        noise = np.random.default_rng([zlib.crc32(name.encode()), seed]).standard_normal(out[name].shape)
        drawn = base * np.exp(spread * noise) if base else spread * noise
        out[name] = jnp.asarray(drawn.astype(out[name].dtype))
    for name, factor in factors.items():
        out[name] = (out[name] * factor).astype(out[name].dtype)
    return out
```

```python
import concourse.bass as bass
from concourse import mybir
from contextlib import ExitStack

F32, I32, BF16 = mybir.dt.float32, mybir.dt.int32, mybir.dt.bfloat16
ALU = mybir.AluOpType
ACT = mybir.ActivationFunctionType
AX = mybir.AxisListType
ds = bass.ds

P = 128
N, C, E = 6250, 256, 206250
NT = (N + P - 1) // P
TAIL = N - (NT - 1) * P
COLS = 1620
LASTC = E - (P - 1) * COLS
SUPC = 60
NSUP = COLS // SUPC
BAT = 6
NBAT = SUPC // BAT
REC = 2
BLK = 8
BW = BLK * REC
NG8 = 8
GRP = 2 * P // BLK
NGRP = 896
NCHUNK = 2 * NGRP
RING = 12
HOT = 6
STEP = RING // 2
REST = NCHUNK - 3 * NT * RING
NBLK = NGRP * GRP
TRASH = NBLK
NREC = NBLK + NSUP * NG8 * P
assert NSUP * SUPC == COLS and (P * SUPC + NT * (BLK - 1)) <= NG8 * P * BLK
assert (E + NSUP * NT * (BLK - 1) + NT * (2 * P - BLK)) // (2 * P) <= NGRP
D2 = 64
INNER = 512
QN = 4
QW = COLS // QN
CW = NT * NSUP // 3


ARENA = NT * C + 3 * (NCHUNK + 4) + 5 * COLS


def wide(ap, shape, axis):
    names = list("abcd"[:len(ap.shape)])
    split, new = list(names), list(names)
    if axis == len(names):
        split[-1] = f"({names[-1]} z)"
    else:
        split[axis] = f"(z {names[axis]})"
    new.insert(axis, "z")
    return ap.rearrange(f"{' '.join(split)} -> {' '.join(new)}", z=1).broadcast_to(shape)


class Steps:

    def __init__(self, eng, sem):
        self.eng, self.sem, self.base, self.off, self.reg = eng, sem, 0, 0, 0

    def loop(self, i, per):
        self.reg, self.off, self.per = i * per, 0, per

    def leave(self, count):
        assert self.off == self.per, (self.off, self.per)
        self.base, self.reg, self.off = self.base + count * self.per, 0, 0

    def freeze(self):
        self.base, self.off = self.base + self.off, 0

    def __call__(self, ins):
        self.off += 1
        ins.then_inc(self.sem, 1)
        self.eng.wait_ge(self.sem, self.base + self.reg + self.off)


def program(nc, x, src, dst, edge_weight, Wqkv, ln1_g, ln1_b, W1, b1, W2, b2, ln2_g, ln2_b,
            W_fx, b_fx, W_x, b_x, W_slice, b_slice, W_q, W_k, W_v, W_out, b_out, temperature, out):
    ctx = ExitStack()
    with ctx:
        def sb(name, shape, dt=F32):
            return ctx.enter_context(nc.sbuf_tensor(name, shape, dt))

        def sem(name):
            return ctx.enter_context(nc.semaphore(name))

        rec = nc.dram_tensor("edge_records", (NREC, BW), F32).ap()
        xg = nc.dram_tensor("normed_rows", (N + 1, C), F32).ap()
        bucket_dram = nc.dram_tensor("group_buckets", (P, NGRP // P), I32).ap()

        ps = ctx.enter_context(nc.psum_tensor("ps", [P, 8, 512], F32))
        acc = sb("acc", [P, NT, C])
        iota = sb("iota", [P, P])
        identf = sb("identf", [P, P])
        identb = sb("identb", [P, P], BF16)
        before = sb("before", [P, P], BF16)
        onesb = sb("onesb", [P, P], BF16)
        zerob = sb("zerob", [P, QW + 3], BF16)
        block_no = sb("block_no", [P, NG8])
        group_no = sb("group_no", [P, NGRP // P])
        stats = sb("stats", [P, NT, 6])
        mean = sb("mean", [P, NT])
        half = sb("half", [P, NT])
        rstd = sb("rstd", [P, NT])
        arena = sb("arena", [P, ARENA])

        def view(at, shape, dt=F32):
            n = 1
            for d in shape:
                n *= d
            v = arena[:, at:at + n]
            if dt is not F32:
                v = v.bitcast(dt)
            if len(shape) == 2:
                v = v.rearrange("p (a b) -> p a b", b=shape[1])
            return v

        xn = view(0, [NT, C])
        tables = [NT, NSUP]
        tables_s = [NSUP, NT + 1]
        tw = NSUP * (NT + 1)
        tabi = view(0, [NT * NSUP], I32)
        nb = view(tw, tables)
        nbs = view(2 * tw, tables_s)
        rstb = view(3 * tw, tables_s)
        rsts = view(4 * tw, tables)
        gex = view(5 * tw, tables)
        ginc = view(6 * tw, tables)
        delta = view(7 * tw, tables_s)
        base = view(8 * tw, tables)
        gmat = view(9 * tw, [NGRP // P, NT])
        e0, ew = NT * C, NCHUNK + 4
        srci = view(e0, [COLS], I32)
        dsti = view(e0 + ew, [COLS], I32)
        loi = view(e0 + 2 * ew, [COLS], I32)
        posi = srci
        gidx = view(e0, [NCHUNK], I32)
        slo = view(e0 + ew, [NCHUNK + 4])
        sw = view(e0 + 2 * ew, [NCHUNK + 4])
        v0 = e0 + 3 * ew
        vals = view(v0, [COLS, REC])
        based = view(v0 + 2 * COLS, [COLS])
        gath = view(v0, [RING, C])
        onehot = view(v0 + RING * C, [HOT, P])
        w0 = v0 + 3 * COLS
        wraw = view(w0, [COLS])
        slotp = wraw
        restart = view(w0 + COLS, [NSUP, SUPC])
        slotc = view(w0 + COLS, [COLS])
        bench = sb("bench", [P, 3456])
        bucket, mask, running, ranked = (bench[:, k * COLS // 2:(k + 1) * COLS // 2].bitcast(BF16) for k in range(4))
        hot_part = bench[:, 0:2 * BAT * P].rearrange("p (h u a) -> p h u a", h=2, u=BAT)
        hot_col = bench[:, 2 * BAT * P:2 * BAT * P + BAT * 64].rearrange("p (u a) -> p u a", u=BAT)
        hot_rec = bench[:, 2 * BAT * P + BAT * 64:3456].rearrange("p (h u a v) -> p h u a v", h=2, u=BAT, v=REC)
        tabs = sb("tabs", [P, 4096])
        cnt = tabs[:, 0:NT * NSUP // 2 + 1].bitcast(BF16)[:, 0:NT * NSUP].rearrange("p (b s) -> p b s", s=NSUP)
        lstart = tabs[:, 672:672 + tw].rearrange("p (s b) -> p s b", s=NSUP)
        jump = tabs[:, 672 + tw:672 + 2 * tw].rearrange("p (s b) -> p s b", s=NSUP)
        gi = sb("gi", [P, NT], I32)
        gn = sb("gn", [P, NT])
        gst = sb("gst", [P, NT])
        gone = sb("gone", [P, NT])
        gbuck = sb("gbuck", [P, NGRP // P])
        gbucki = sb("gbucki", [P, NGRP // P], I32)
        group_bucket = sb("group_bucket", [1, NGRP], I32)
        passed = tabs[:, 672 + 2 * tw:672 + 2 * tw + NG8 * (NT + 1)].rearrange("p (g b) -> p g b", g=NG8)
        moved = sb("moved", [P, NG8])
        dest = sb("dest", [P, NG8], I32)
        raw_qkv = view(0, [6, C])
        raw_w1 = view(6 * C, [2, C])
        raw_w2 = view(8 * C, [2, C])
        zerof = view(5 * tw, [512])
        raw_wx = bench[:, 0:2 * INNER].rearrange("p (k o) -> p k o", o=INNER)
        wxT = bench[:, 2 * INNER:4 * INNER].rearrange("p (m c) -> p m c", c=C)
        xT = bench[:, 0:C].rearrange("p (k t) -> p k t", t=P)
        low = bench[:, C:2 * C]
        grown = bench[:, 2 * C:3 * C]
        feat = bench[:, 3 * C:4 * C]
        vone = bench[:, 4 * C:4 * C + 2 * (P + 1)].rearrange("p (g m) -> p g m", m=P + 1)
        tmp = bench[:, 5 * C + 4:6 * C + 4]
        zden = bench[:, 6 * C + 4:6 * C + 12].rearrange("p (g h) -> p g h", h=4)
        xcur = bench[:, 6 * C + 12:7 * C + 12]
        slcur = bench[:, 0:4 * INNER].rearrange("p (h m t) -> p h m t", h=4, t=P)
        wmix = sb("wmix", [P, 2824])
        wqkvT = wmix[:, 0:6 * C].rearrange("p (k o) -> p k o", o=3 * C)
        w1T = wmix[:, 6 * C:8 * C].rearrange("p (k o) -> p k o", o=C)
        w2T = wmix[:, 8 * C:10 * C].rearrange("p (k o) -> p k o", o=C)
        kvd = wmix[:, 10 * C:10 * C + 264].rearrange("p (g m) -> p g m", m=132)
        wout = wmix[0:D2, 0:8 * C].rearrange("p (h c) -> p h c", c=C)
        wc = tabs[:, 0:2 * INNER].rearrange("p (k o) -> p k o", o=INNER)
        mout = tabs[:, 0:4 * C].rearrange("p (m c) -> p m c", c=C)
        wfx = tabs[:, 2 * INNER:4 * INNER].rearrange("p (k o) -> p k o", o=INNER)
        rows = tabs[:, 4 * INNER:4 * INNER + 4 * C].rearrange("p (n c) -> p n c", c=C)
        small = tabs[:, 3072:4096]
        wslice = small[:, 0:64]
        wq, wk, wv = (small[0:D2, 64 + 64 * n:128 + 64 * n] for n in range(3))
        bxc = small[:, 256:260]
        b1c = small[:, 260:262]
        rtemp = small[:, 262:270]
        bsl = small[0:3, 270:334]
        spread, root, middle, off = (small[:, 880 + n:881 + n] for n in range(4))
        bfx = small[0:1, 350:862]
        biasf = arena[0:3, w0:w0 + 3 * INNER].rearrange("p (n c) -> p n c", c=INNER)
        bias_logit = sb("bias_logit", [3, INNER], BF16)
        bias2 = sb("bias2", [3, C], BF16)
        biaso = sb("biaso", [3, C], BF16)
        xs = bench[:, 0:2 * (C + 1)].rearrange("p (h c) -> p h c", c=C + 1)
        xsT = bench[:, 514:514 + 2 * C].rearrange("p (h k t) -> p h k t", h=2, t=P)
        lowered = bench[:, 1026:1026 + INNER]
        expd = bench[:, 1538:1538 + INNER]
        slices = bench[:, 2050:2050 + 2 * INNER].rearrange("p (h o) -> p h o", h=2)
        fmax = bench[:, 3074:3082]
        fsum = bench[:, 3082:3098].rearrange("p (h o) -> p h o", h=2)
        sliceT = view(0, [4, NT * P])
        token = bench[:, 0:4 * (C + 1)].rearrange("p (m c) -> p m c", c=C + 1)
        tokenT = bench[:, 1028:1028 + 2 * INNER].rearrange("p (k o) -> p k o", o=INNER)
        ratio = bench[0:1, 2052:2052 + INNER]
        tokf = bench[0:D2, 2564:2564 + INNER]
        tden = bench[:, 3076:3080]
        qk = tabs[0:D2, 4 * INNER:6 * INNER].rearrange("p (n o) -> p n o", o=INNER)
        vtok = bench[0:D2, 0:INNER]
        att = bench[0:D2, INNER:2 * INNER]
        attT = bench[0:D2, 1028:1028 + INNER]
        outT = bench[0:D2, 1540:1540 + INNER]
        amax = small[0:D2, 334:342]
        asum = small[0:D2, 342:350]
        local = sb("local", [P, NG8 * BW])
        back = sb("back", [P, 2, P * REC])
        geti = sb("geti", [P, P], I32)
        getl = sb("getl", [P, P], I32)
        iring = sb("iring", [P, 2, RING], I32)

        names = """row_var row_root scatter_done x_loaded src_loaded dst_loaded w_loaded consts pad_set zero_rows zeroed
            step_dve var_ready rstd_root rstd_ready normed xn_stored edges_ready prod_ready prod_used scan_ready
            count_copied count_sums sums_read based_ready based_used pos_read pair_ready col_hot sorted_batches
            local_sorted local_copied dest_ready super_zero
            bucket_ready bucket_stored bucket_loaded transposed unpacked w_copied
            raw_loaded trans_ps trans_sb rows_loaded wx_loaded wxT_ps wxT_sb wc_ps wc_sb late_loaded
            cur_sb sl_sb xt_ps xt_sb proj feat_low feat_exp feat_ready v_sb third res kv_start kv_done kv_diag bias_ready
            swept vone_set mixed f_norm f_logit f_low f_exp f_sum f_slice f_pair f_xT f_xsT f_sTsb tok_ps tok_sb out_ps out_sum
            ring_ready hot_ready multiplied added out_stored pace pace_sp pace_pe pace_act stepact""".split()
        S = {n: sem(n) for n in names}
        START_AT_ONE = """third proj xt_ps out_ps count_copied prod_used based_used pair_ready f_pair f_exp local_copied xt_sb feat_ready v_sb res f_sTsb out_sum scatter_done""".split()
        scattered = [sem(f"scattered{g}") for g in range(NG8)]
        gathered = [sem(f"gathered{g}") for g in range(RING)]
        loaded_back = [sem(f"loaded_back{g}") for g in range(2)]
        block = ctx.enter_context(nc.Block())

        @block.sync
        def _(sp):
            for name in START_AT_ONE:
                sp.sem_inc(S[name], 1)
            sp.dma_start(raw_qkv, Wqkv.rearrange("(o p) c -> p o c", p=P)).then_inc(S["raw_loaded"], 16)
            sp.dma_start(raw_w1, W1.rearrange("(o p) c -> p o c", p=P)).then_inc(S["raw_loaded"], 16)
            sp.dma_start(raw_w2, W2.rearrange("(o p) c -> p o c", p=P)).then_inc(S["raw_loaded"], 16)
            sp.wait_ge(S["pad_set"], 4)
            sp.dma_start(srci[0:112, :], src[0:112 * COLS].rearrange("(p c) -> p c", c=COLS)).then_inc(S["src_loaded"], 16)
            sp.dma_start(srci[112:127, :], src[112 * COLS:127 * COLS].rearrange("(p c) -> p c", c=COLS)).then_inc(S["src_loaded"], 16)
            sp.dma_start(srci[127:128, 0:LASTC], src[127 * COLS:E].rearrange("(p c) -> p c", p=1)).then_inc(S["src_loaded"], 16)
            sp.dma_start(dsti[0:112, :], dst[0:112 * COLS].rearrange("(p c) -> p c", c=COLS)).then_inc(S["dst_loaded"], 16)
            sp.dma_start(dsti[112:127, :], dst[112 * COLS:127 * COLS].rearrange("(p c) -> p c", c=COLS)).then_inc(S["dst_loaded"], 16)
            sp.dma_start(dsti[127:128, 0:LASTC], dst[127 * COLS:E].rearrange("(p c) -> p c", p=1)).then_inc(S["dst_loaded"], 16)
            sp.dma_start(wraw[0:112, :], edge_weight[0:112 * COLS].rearrange("(p c) -> p c", c=COLS)).then_inc(S["w_loaded"], 16)
            sp.dma_start(wraw[112:127, :], edge_weight[112 * COLS:127 * COLS].rearrange("(p c) -> p c", c=COLS)).then_inc(S["w_loaded"], 16)
            sp.dma_start(wraw[127:128, 0:LASTC], edge_weight[127 * COLS:E].rearrange("(p c) -> p c", p=1)).then_inc(S["w_loaded"], 16)
            sp.dma_start(acc[:, 0:NT - 1, :], x[0:(NT - 1) * P, :].rearrange("(t p) c -> p t c", p=P)).then_inc(S["x_loaded"], 16)
            sp.dma_start(acc[0:TAIL, NT - 1, :], x[(NT - 1) * P:N, :]).then_inc(S["x_loaded"], 16)
            sp.wait_ge(S["zero_rows"], 2)
            zr = NBLK * BW // (P * 512)
            for k in range(zr):
                sp.dma_start(rec[0:NBLK, :].rearrange("(k p a) w -> k p (a w)", k=zr, p=P)[k], zerof[:, :]).then_inc(S["zeroed"], 16)
            sp.dma_start(xg[0:1, :], zerof[0:1, 0:C]).then_inc(S["zeroed"], 16)
            sp.wait_ge(S["normed"], NT)
            sp.dma_start(xg[1:1 + (NT - 1) * P, :].rearrange("(t p) c -> p t c", p=P), xn[:, 0:NT - 1, :]).then_inc(S["xn_stored"], 16)
            sp.dma_start(xg[1 + (NT - 1) * P:N + 1, :], xn[0:TAIL, NT - 1, :]).then_inc(S["xn_stored"], 16)
            sp.wait_ge(S["bucket_ready"], 1)
            sp.dma_start(bucket_dram, gbucki[:, :]).then_inc(S["bucket_stored"], 16)
            sp.wait_ge(S["bucket_stored"], 16)
            sp.dma_start(group_bucket[0:1, :], bucket_dram.rearrange("p q -> (p q)").rearrange("(a n) -> a n", a=1)).then_inc(S["bucket_loaded"], 16)
            sp.wait_ge(S["local_sorted"], NSUP)
            sp.dma_start(raw_wx, W_x.rearrange("(k p) o -> p k o", p=P)).then_inc(S["wx_loaded"], 16)
            for g in range(NG8):
                sp.wait_ge(scattered[g], 16 * NSUP)
            recs = rec[0:NBLK, :].rearrange("(k p a) w -> k p (a w)", p=P, a=P // BLK)
            for k in range(NCHUNK // P):
                if k >= 2:
                    sp.wait_ge(S["transposed"], k - 1)
                sp.dma_start(back[:, k % 2, :], recs[k]).then_inc(loaded_back[k % 2], 16)
            sp.wait_ge(S["dest_ready"], NSUP)
            sp.dma_start(wfx, W_fx.rearrange("(k p) o -> p k o", p=P)).then_inc(S["rows_loaded"], 16)
            for n, v in enumerate((ln1_g, ln1_b, ln2_g, ln2_b)):
                sp.dma_start(rows[:, n, :], v.rearrange("(a c) -> a c", a=1).broadcast_to([P, C])).then_inc(S["rows_loaded"], 16)
            for h in range(2):
                sp.dma_start(wslice[h * D2:(h + 1) * D2, :], W_slice).then_inc(S["rows_loaded"], 16)
            for t, v in ((wq, W_q), (wk, W_k), (wv, W_v)):
                sp.dma_start(t, v).then_inc(S["rows_loaded"], 16)
            sp.dma_start(bxc, b_x.rearrange("(m p) -> p m", p=P), allow_slow_non_contiguous=True).then_inc(S["rows_loaded"], 16)
            sp.dma_start(b1c, b1.rearrange("(m p) -> p m", p=P), allow_slow_non_contiguous=True).then_inc(S["rows_loaded"], 16)
            sp.dma_start(rtemp, temperature.rearrange("a h b c -> (b c) (a h)").broadcast_to([P, 8])).then_inc(S["rows_loaded"], 16)
            sp.dma_start(bsl, b_slice.rearrange("(a c) -> a c", a=1).broadcast_to([3, D2])).then_inc(S["rows_loaded"], 16)
            sp.dma_start(bfx, b_fx.rearrange("(a c) -> a c", a=1)).then_inc(S["rows_loaded"], 16)
            sp.dma_start(biasf[:, 1, 0:C], b2.rearrange("(a c) -> a c", a=1).broadcast_to([3, C])).then_inc(S["rows_loaded"], 16)
            sp.dma_start(biasf[:, 1, C:2 * C], b_out.rearrange("(a c) -> a c", a=1).broadcast_to([3, C])).then_inc(S["rows_loaded"], 16)
            sp.wait_ge(S["third"], 3 * NT + 1)
            sp.dma_start(wout, W_out.rearrange("(h p) c -> p h c", p=D2)).then_inc(S["late_loaded"], 16)
            with sp.Fori(0, NT // 4) as i:
                sp.wait_ge(S["out_sum"], 4 * i + 5)
                sp.sem_inc(S["pace_sp"], 1)
                sp.dma_start(out[ds(i * 4 * P, 4 * P), :].rearrange("(t p) c -> p t c", p=P), acc[:, ds(i * 4, 4), :]).then_inc(S["out_stored"], 16)
            sp.wait_ge(S["out_sum"], NT + 1)
            sp.dma_start(out[(NT - 1) * P:N, :], acc[0:TAIL, NT - 1, :]).then_inc(S["out_stored"], 16)
            sp.wait_ge(S["out_stored"], 16 * (NT // 4 + 1))

        @block.gpsimd
        def _(pool):
            def seen(s, v):
                pool.wait_ge(s, v)
                pool.sem_inc(S["pace"], 1)
            pool.memset(identf[:, :], 0.0).then_inc(S["consts"], 1)
            pool.memset(identb[:, :], 0.0).then_inc(S["consts"], 1)
            pool.memset(onesb[:, :], 1.0).then_inc(S["consts"], 1)
            pool.memset(zerob[:, :], 0.0).then_inc(S["consts"], 1)
            pool.memset(zerof[:, :], 0.0).then_inc(S["zero_rows"], 2)
            pool.iota(iota[:, :], pattern=[[1, P]], base=0, channel_multiplier=0, allow_small_or_imprecise_dtypes=True).then_inc(S["consts"], 1)
            pool.iota(block_no[:, :], pattern=[[P, NG8]], base=0, channel_multiplier=1, allow_small_or_imprecise_dtypes=True).then_inc(S["consts"], 1)
            pool.iota(group_no[:, :], pattern=[[GRP, NGRP // P]], base=0, channel_multiplier=GRP * (NGRP // P), allow_small_or_imprecise_dtypes=True).then_inc(S["consts"], 1)
            pool.wait_ge(S["consts"], 7)
            pool.affine_select(out=identf[:, :], in_=identf[:, :], compare_op=ALU.not_equal, fill=1.0, base=0, pattern=[[-1, P]], channel_multiplier=1).then_inc(S["consts"], 1)
            pool.affine_select(out=identb[:, :], in_=identb[:, :], compare_op=ALU.not_equal, fill=1.0, base=0, pattern=[[-1, P]], channel_multiplier=1).then_inc(S["consts"], 1)
            pool.affine_select(out=before[:, :], in_=onesb[:, :], compare_op=ALU.is_gt, fill=0.0, base=0, pattern=[[1, P]], channel_multiplier=-1).then_inc(S["consts"], 1)
            pool.wait_ge(S["zeroed"], 16 * (NBLK * BW // (P * 512) + 1))
            with pool.Fori(0, NSUP) as i:
                pool.wait_ge(S["dest_ready"], i + 1)
                seen(S["local_copied"], i + 2)
                for g in range(NG8):
                    pool.indirect_dma_start(rec, bass.IndirectOffsetOnAxis(ap=dest[:, g:g + 1], axis=0), local[:, g * BW:(g + 1) * BW], None).then_inc(scattered[g], 16)
                for g in range(NG8):
                    pool.wait_ge(scattered[g], 16 * i + 16)
                pool.sem_inc(S["scatter_done"], 1)
            pool.wait_ge(S["xn_stored"], 32)
            pool.wait_ge(S["unpacked"], NCHUNK // P)

            PAIRS = NCHUNK // (2 * RING)
            with pool.Fori(0, PAIRS) as i:
                for h in range(2):
                    pool.tensor_copy(iring[:, h, :], gidx[:, ds((2 * i + h) * RING, RING)]).then_inc(S["ring_ready"], 1)
                    seen(S["ring_ready"], 2 * i + h + 1)
                    for j in range(RING):
                        seen(S["multiplied"], (2 * i + h) * RING + j + 1)
                        pool.indirect_dma_start(gath[:, j, :], None, xg, bass.IndirectOffsetOnAxis(ap=iring[:, h, j:j + 1], axis=0)).then_inc(gathered[j], 16)
            for k in range(2 * PAIRS, (NCHUNK + RING - 1) // RING):
                count = min(RING, NCHUNK - k * RING)
                pool.tensor_copy(iring[:, k % 2, 0:count], gidx[:, k * RING:k * RING + count]).then_inc(S["ring_ready"], 1)
                pool.wait_ge(S["ring_ready"], k + 1)
                for j in range(count):
                    pool.wait_ge(S["multiplied"], k * RING + j + 1)
                    pool.sem_inc(S["pace"], 1)
                    pool.indirect_dma_start(gath[:, j, :], None, xg, bass.IndirectOffsetOnAxis(ap=iring[:, k % 2, j:j + 1], axis=0)).then_inc(gathered[j], 16)

            def weigh(t, h):
                pool.wait_ge(S["f_pair"], t + 1)
                seen(S["f_sum"], t + 1)
                pool.tensor_tensor(slices[:, h, :].rearrange("p (n g) -> p n g", g=D2), expd[:, :].rearrange("p (n g) -> p n g", g=D2), wide(fsum[:, h, :], [P, 8, D2], 2), ALU.mult).then_inc(S["f_slice"], 1)
            with pool.Fori(0, NT // 2) as i:
                weigh(2 * i, 0)
                weigh(2 * i + 1, 1)
            weigh(NT - 1, 0)

        @block.scalar
        def _(act):
            def seen(s, v):
                act.wait_ge(s, v)
                act.sem_inc(S["pace_act"], 1)
            for k in range(10):
                act.wait_ge(S["trans_ps"], k + 1)
                to = wqkvT[:, :, k * P:(k + 1) * P] if k < 6 else (w1T if k < 8 else w2T)[:, :, k % 2 * P:k % 2 * P + P]
                act.copy(to, ps[:, 6 + k % 2, 0:2 * P].rearrange("p (k o) -> p k o", k=2)).then_inc(S["trans_sb"], 1)
            with act.Fori(0, NT) as b:
                seen(S["scan_ready"], b + 1)
                act.copy(cnt[:, ds(b, 1), :], running[:, SUPC - 1::SUPC].rearrange("p (a s) -> p a s", a=1)).then_inc(S["count_copied"], 1)
            act.wait_ge(S["var_ready"], 1)
            act.activation(rstd[:, :], rstd[:, :], ACT.Sqrt).then_inc(S["rstd_root"], 1)
            with act.Fori(0, NSUP) as i:
                act.wait_ge(S["scatter_done"], i + 1)
                seen(S["local_sorted"], i + 1)
                act.copy(local[:, :], ps[:, 7, 0:P]).then_inc(S["local_copied"], 1)
            for k in range(NCHUNK // P):
                act.wait_ge(S["transposed"], k + 1)
                act.copy(sw[:, k * P:(k + 1) * P], ps[:, 6 + k % 2, 0:P]).then_inc(S["w_copied"], 1)

            for m in range(4):
                act.wait_ge(S["wxT_ps"], m + 1)
                act.copy(wxT[:, m, :], ps[:, 2 + m % 2, 0:C]).then_inc(S["wxT_sb"], 1)

            tile = lambda a, t: a[:, ds(t, 1), :].rearrange("p a c -> p (a c)")

            def stage(n, t):
                seen(S["xt_ps"], n + 1)
                act.copy(xcur, tile(xn, t)).then_inc(S["cur_sb"], 1)

            def copy_xT(n):
                act.wait_ge(S["proj"], n + 1)
                seen(S["xt_ps"], n + 2)
                act.copy(xT[:, :, :], ps[:, 2, 0:C].rearrange("p (k t) -> p k t", k=2)).then_inc(S["xt_sb"], 1)

            def grow(n):
                seen(S["feat_low"], n + 1)
                act.activation(grown, low, ACT.Exp).then_inc(S["feat_exp"], 1)

            act.wait_ge(S["wc_ps"], 1)
            act.wait_ge(S["vone_set"], 1)
            with act.Fori(0, NT) as t:
                stage(t, t)
                copy_xT(t)
                act.wait_ge(S["third"], t + 1)
                seen(S["proj"], t + 2)
                act.copy(vone[:, :, 0:P], ps[:, 6, 0:C].rearrange("p (g m) -> p g m", g=2)).then_inc(S["v_sb"], 1)
                grow(t)
            with act.Fori(0, NT) as t:
                stage(t + NT, t)
                copy_xT(t + NT)
                grow(t + NT)
            act.wait_ge(S["var_ready"], 2)
            act.activation(rstd[:, :], rstd[:, :], ACT.Sqrt).then_inc(S["rstd_root"], 1)
            with act.Fori(0, NT) as t:
                n = t + 2 * NT
                act.wait_ge(S["mixed"], t + 1)
                stage(n, t)
                copy_xT(n)
                act.wait_ge(S["third"], n + 1)
                seen(S["proj"], n + 2)
                act.activation(feat[:, 0:P], ps[:, 3, 0:P], ACT.Gelu, bias=b1c[:, 0:1])
                act.activation(feat[:, P:2 * P], ps[:, 3, P:2 * P], ACT.Gelu, bias=b1c[:, 1:2]).then_inc(S["feat_ready"], 1)
                seen(S["row_var"], t + 1)
                act.activation(root, spread, ACT.Sqrt).then_inc(S["row_root"], 1)
            act.wait_ge(S["var_ready"], 3)
            act.activation(rstd[:, :], rstd[:, :], ACT.Sqrt).then_inc(S["rstd_root"], 1)

            def ffn_tile(t, h):
                seen(S["f_xT"], t + 1)
                act.wait_ge(S["f_logit"], t)
                act.copy(xsT[:, h, :, :], ps[:, 2, 0:C].rearrange("p (k t) -> p k t", k=2)).then_inc(S["f_xsT"], 1)
                act.wait_ge(S["f_slice"], t)
                seen(S["f_low"], t + 1)
                act.activation(expd, lowered, ACT.Exp).then_inc(S["f_exp"], 1)

            def keep_slices(t):
                seen(S["f_pair"], t + 3)
                act.copy(sliceT[:, :, ds(t * P, P)], ps[:, 3, 0:INNER].rearrange("p (m t) -> p m t", m=4)).then_inc(S["f_sTsb"], 1)
            ffn_tile(0, 0)
            with act.Fori(0, NT // 2) as i:
                ffn_tile(2 * i + 1, 1)
                keep_slices(2 * i)
                ffn_tile(2 * i + 2, 0)
                keep_slices(2 * i + 1)
            keep_slices(NT - 1)
            act.wait_ge(S["tok_sb"], 9)
            act.activation(att, att, ACT.Exp, scale=D2 ** -0.5).then_inc(S["tok_sb"], 1)
            act.wait_ge(S["tok_sb"], 14)

            def stage_slices(t, h):
                act.copy(slcur[:, h, :, :], sliceT[:, :, ds(t * P, P)]).then_inc(S["sl_sb"], 1)
            with act.Fori(0, NT // 4) as i:
                for h in range(4):
                    seen(S["out_ps"], 4 * i + 1)
                    stage_slices(4 * i + h, h)
            seen(S["out_ps"], NT - 1 + 1)
            stage_slices(NT - 1, 0)

        def split_bias(step, to, frm, width):
            dve = nc.vector
            hi, rest, mid = biasf[:, 0, 0:width], biasf[:, 2, 0:width], frm
            step(dve.tensor_copy(to[:, 0:width], frm))
            step(dve.tensor_copy(hi, to[:, 0:width]))
            step(dve.tensor_tensor(rest, frm, hi, ALU.subtract))
            step(dve.tensor_copy(to[:, 0:width], rest))
            step(dve.tensor_copy(mid, to[:, 0:width]))
            step(dve.tensor_tensor(rest, rest, mid, ALU.subtract))
            step(dve.tensor_scalar(hi, hi, identf[0:3, 0:1], None, ALU.mult))
            step(dve.scalar_tensor_tensor(hi, mid, identf[0:3, 1:2], hi, ALU.mult, ALU.add))
            step(dve.scalar_tensor_tensor(to[:, 0:width], rest, identf[0:3, 2:3], hi, ALU.mult, ALU.add))

        def var_of_stats(step):
            dve = nc.vector
            step(dve.tensor_tensor(mean[:, :], stats[:, :, 1], stats[:, :, 4], ALU.add))
            step(dve.tensor_scalar(mean[:, :], mean[:, :], 0.5, None, ALU.mult))
            step(dve.tensor_tensor(half[:, :], mean[:, :], stats[:, :, 1], ALU.subtract))
            step(dve.tensor_tensor(half[:, :], half[:, :], half[:, :], ALU.mult))
            step(dve.tensor_tensor(rstd[:, :], stats[:, :, 2], stats[:, :, 5], ALU.add))
            step(dve.scalar_tensor_tensor(rstd[:, :], rstd[:, :], 1.0 / C, half[:, :], ALU.mult, ALU.add))
            step(dve.tensor_scalar(rstd[:, :], rstd[:, :], 1e-5, None, ALU.add))

        @block.vector
        def _(dve):
            step = Steps(dve, S["step_dve"])
            dve.memset(srci[96:P, LASTC:COLS], NT * P).then_inc(S["pad_set"], 1)
            dve.memset(dsti[96:P, LASTC:COLS], -1).then_inc(S["pad_set"], 1)
            dve.memset(wraw[96:P, LASTC:COLS], 0.0).then_inc(S["pad_set"], 1)
            dve.memset(acc[96:P, NT - 1, :], 0.0).then_inc(S["pad_set"], 1)
            step(dve.memset(restart[:, :, :], 1.0))
            step(dve.memset(restart[:, :, 0:1], 0.0))
            dve.memset(rstb[:, :, :], 1.0)
            step(dve.memset(rsts[:, :, :], 1.0))
            dve.memset(rstb[:, :, 0:1], 0.0)
            step(dve.memset(rsts[:, :, 0:1], 0.0))
            dve.memset(gone[:, :], 1.0)
            dve.memset(slo[:, NCHUNK:], 0.0)
            dve.memset(sw[:, NCHUNK:], 0.0)
            step(dve.memset(nbs[:, :, :], 0.0))
            dve.wait_ge(S["consts"], 10)
            dve.wait_ge(S["src_loaded"], 48)
            dve.wait_ge(S["dst_loaded"], 48)
            dve.wait_ge(S["w_loaded"], 48)
            step(dve.tensor_scalar(loi[:, :], srci[:, :], 7, None, ALU.logical_shift_right))
            step(dve.tensor_copy(bucket[:, :], loi[:, :]))
            step(dve.tensor_scalar(loi[:, :], srci[:, :], P - 1, None, ALU.bitwise_and))
            step(dve.tensor_scalar(based[:, :], dsti[:, :], 1.0, float(P), ALU.add, ALU.mult))
            dve.tensor_tensor(vals[:, :, 0], based[:, :], loi[:, :], ALU.add)
            step(dve.tensor_copy(vals[:, :, 1], wraw[:, :]))
            step.freeze()
            with dve.Fori(0, NT) as b:
                step.loop(b, 1)
                step(dve.tensor_scalar(mask[:, :], bucket[:, :], iota[:, ds(b, 1)], None, ALU.is_equal))
                dve.wait_ge(S["count_copied"], b + 1)
                dve.tensor_tensor_scan(running[:, :], restart[:, :, :].rearrange("p s c -> p (s c)"), mask[:, :], 0.0, ALU.mult, ALU.add).then_inc(S["scan_ready"], 1)
                dve.wait_ge(S["scan_ready"], b + 1)
                dve.wait_ge(S["prod_used"], b + 1)
                dve.tensor_tensor(ranked[:, :], running[:, :], mask[:, :], ALU.mult).then_inc(S["prod_ready"], 1)
                dve.wait_ge(S["prod_ready"], b + 1)
            step.leave(NT)
            dve.wait_ge(S["zeroed"], 16 * (NBLK * BW // (P * 512) + 1))
            dve.wait_ge(S["trans_ps"], 10)
            dve.wait_ge(S["count_sums"], 1)
            step(dve.tensor_copy(base[:, :, :].rearrange("p b s -> p (b s)").rearrange("p (k c) -> p k c", k=3), ps[:, 4:7, 0:CW]))
            dve.engine_nop().then_inc(S["sums_read"], 1)
            dve.wait_ge(S["count_sums"], 2)
            step(dve.tensor_scalar(tabi[:, :].rearrange("p (k c) -> p k c", k=3), ps[:, 4:7, 0:CW], float(BLK - 1), None, ALU.add))
            step(dve.tensor_scalar(tabi[:, :], tabi[:, :], 3, None, ALU.logical_shift_right))
            step(dve.tensor_copy(nb[:, :, :].rearrange("p b s -> p (b s)"), tabi[:, :]))
            step(dve.tensor_copy(nbs[:, :, 0:NT].rearrange("p s b -> p b s"), nb[:, :, :]))
            flat = lambda t: t[:, :, :].rearrange("p a b -> p (a b)")
            step(dve.tensor_tensor_scan(flat(lstart), flat(rstb), flat(nbs), 0.0, ALU.mult, ALU.add))
            step(dve.tensor_tensor(flat(lstart), flat(lstart), flat(nbs), ALU.subtract))
            step(dve.tensor_tensor_scan(flat(ginc), flat(rsts), flat(nb), 0.0, ALU.mult, ALU.add))
            step(dve.tensor_tensor(flat(gex), flat(ginc), flat(nb), ALU.subtract))
            step(dve.tensor_scalar(gi[:, :], ginc[:, :, NSUP - 1], float(GRP - 1), None, ALU.add))
            step(dve.tensor_scalar(gi[:, :], gi[:, :], 5, 5, ALU.logical_shift_right, ALU.logical_shift_left))
            step(dve.tensor_copy(gn[:, :], gi[:, :]))
            step(dve.tensor_tensor_scan(gst[:, :], gone[:, :], gn[:, :], 0.0, ALU.mult, ALU.add))
            step(dve.tensor_tensor(gst[:, :], gst[:, :], gn[:, :], ALU.subtract))
            step(dve.tensor_tensor(gex[:, :, :], gex[:, :, :], gst[:, :].rearrange("p (b s) -> p b s", s=1).broadcast_to([P, NT, NSUP]), ALU.add))
            step(dve.tensor_tensor(delta[:, :, 0:NT].rearrange("p s b -> p b s"), gex[:, :, :], lstart[:, :, 0:NT].rearrange("p s b -> p b s"), ALU.subtract))
            step(dve.tensor_scalar(delta[:, :, NT], iota[:, 0:NSUP], float(NG8 * P), float(TRASH), ALU.mult, ALU.add))
            step(dve.tensor_tensor(jump[:, :, 1:NT + 1], delta[:, :, 1:NT + 1], delta[:, :, 0:NT], ALU.subtract))
            step(dve.tensor_copy(jump[:, :, 0:1], delta[:, :, 0:1]))
            step(dve.scalar_tensor_tensor(base[:, :, :], lstart[:, :, 0:NT].rearrange("p s b -> p b s"), float(BLK), base[:, :, :], ALU.mult, ALU.add))
            step(dve.tensor_scalar(flat(base), flat(base), 1.0, None, ALU.subtract))
            step(dve.tensor_tensor(gmat[:, :, :], group_no[:, :].rearrange("p (q b) -> p q b", b=1).broadcast_to([P, NGRP // P, NT]), gst[:, :].rearrange("p (q b) -> p q b", q=1).broadcast_to([P, NGRP // P, NT]), ALU.is_ge))
            step(dve.tensor_reduce(gbuck[:, :], gmat[:, :, :], AX.X, ALU.add))
            dve.tensor_scalar(gbucki[:, :], gbuck[:, :], 1.0, None, ALU.subtract).then_inc(S["bucket_ready"], 1)
            step.freeze()
            with dve.Fori(0, NT) as b:
                step.loop(b, 1)
                step(dve.tensor_scalar(mask[:, :], bucket[:, :], iota[:, ds(b, 1)], None, ALU.is_equal))
                dve.wait_ge(S["based_used"], b + 1)
                dve.tensor_tensor(based[:, :].rearrange("p (s c) -> p s c", c=SUPC), mask[:, :].rearrange("p (s c) -> p s c", c=SUPC), base[:, ds(b, 1), :].rearrange("p a s -> p s a").broadcast_to([P, NSUP, SUPC]), ALU.mult).then_inc(S["based_ready"], 1)
                dve.wait_ge(S["based_ready"], b + 1)
            step.leave(NT)
            dve.wait_ge(S["based_used"], NT + 2)
            step(dve.tensor_copy(posi[:, :].rearrange("p (k c) -> p k c", k=QN), ps[:, 0:QN, 0:QW]))
            step(dve.tensor_scalar(loi[:, :], posi[:, :], 3, P - 1, ALU.logical_shift_right, ALU.bitwise_and))
            step(dve.tensor_copy(slotp[:, :], loi[:, :]))
            step(dve.tensor_scalar(loi[:, :], posi[:, :], 10, 3, ALU.logical_shift_right, ALU.logical_shift_left))
            step(dve.tensor_scalar(dsti[:, :], posi[:, :], BLK - 1, None, ALU.bitwise_and))
            step(dve.tensor_tensor(loi[:, :], loi[:, :], dsti[:, :], ALU.bitwise_or))
            step(dve.tensor_copy(slotc[:, :], loi[:, :]))
            dve.wait_ge(S["x_loaded"], 32)
            step.freeze()
            with dve.Fori(0, NT) as t:
                step.loop(t, 1)
                step(dve.bn_stats(stats[:, ds(t, 1), :].rearrange("p a c -> p (a c)"), acc[:, ds(t, 1), :].rearrange("p a c -> p (a c)")))
            step.leave(NT)
            var_of_stats(step)
            dve.wait_ge(S["x_loaded"], 32)
            dve.engine_nop().then_inc(S["var_ready"], 1)
            dve.wait_ge(S["rstd_root"], 1)
            step(dve.reciprocal(rstd[:, :], rstd[:, :]))
            with dve.Fori(0, NT) as t:
                dve.tensor_scalar(xn[:, ds(t, 1), :], acc[:, ds(t, 1), :], mean[:, ds(t, 1)], rstd[:, ds(t, 1)], ALU.subtract, ALU.mult).then_inc(S["normed"], 1)
            step.freeze()
            with dve.Fori(0, NSUP) as i:
                with dve.Fori(0, NBAT // 2) as j:
                    for h in range(2):
                        q = i * NBAT + j * 2 + h
                        c = ds(i * SUPC + j * (2 * BAT) + h * BAT, BAT)
                        dve.wait_ge(S["sorted_batches"], q + 1)
                        dve.tensor_tensor(hot_part[:, h, :, :], wide(iota[:, :], [P, BAT, P], 1), wide(slotp[:, c], [P, BAT, P], 2), ALU.is_equal)
                        dve.wait_ge(S["pair_ready"], q + 1)
                        dve.tensor_tensor(hot_col[:, :, :], wide(iota[:, 0:64], [P, BAT, 64], 1), wide(slotc[:, c], [P, BAT, 64], 2), ALU.is_equal).then_inc(S["col_hot"], 1)
                        dve.wait_ge(S["col_hot"], q + 1)
                        dve.tensor_tensor(hot_rec[:, h, :, :, :], wide(hot_col[:, :, :], [P, BAT, 64, REC], 3), wide(vals[:, c, :], [P, BAT, 64, REC], 2), ALU.mult).then_inc(S["pair_ready"], 1)
                dve.wait_ge(S["scatter_done"], i + 1)
                step.loop(i, 3)
                shape = [P, NG8, NT + 1]
                step(dve.tensor_tensor(passed[:, :, :], block_no[:, :].rearrange("p (g b) -> p g b", b=1).broadcast_to(shape), lstart[:, ds(i, 1), :].broadcast_to(shape), ALU.is_ge))
                step(dve.tensor_tensor(passed[:, :, :], passed[:, :, :], jump[:, ds(i, 1), :].broadcast_to(shape), ALU.mult))
                step(dve.tensor_reduce(moved[:, :], passed[:, :, :], AX.X, ALU.add))
                dve.tensor_tensor(dest[:, :], moved[:, :], block_no[:, :], ALU.add).then_inc(S["dest_ready"], 1)
            step.leave(NSUP)
            for k in range(NCHUNK // P):
                dve.wait_ge(S["transposed"], k + 1)
                step(dve.tensor_copy(geti[:, :], ps[:, 4 + k % 2, 0:P]))
                step(dve.tensor_scalar(getl[:, :], geti[:, :], P - 1, None, ALU.bitwise_and))
                dve.tensor_scalar(gidx[:, k * P:(k + 1) * P], geti[:, :], 7, None, ALU.logical_shift_right)
                step(dve.tensor_copy(slo[:, k * P:(k + 1) * P], getl[:, :]))
                dve.engine_nop().then_inc(S["unpacked"], 1)
            step.freeze()
            dve.wait_ge(S["rows_loaded"], 16 * 17)
            step(dve.tensor_scalar(rtemp, rtemp, 0.1, 5.0, ALU.max, ALU.min))
            step(dve.reciprocal(rtemp, rtemp))
            dve.wait_ge(S["wc_ps"], 1)
            parity = lambda a, e: a.rearrange("p (m e g) -> p e m g", e=2, g=D2)[:, e]
            for e in range(2):
                for k in range(2):
                    dve.tensor_tensor(parity(wc[:, k, :], e), parity(ps[:, 2 + k + 2 * e, :], e), wide(rtemp.rearrange("p (m e) -> p e m", e=2)[:, e, :], [P, 4, D2], 2), ALU.mult)
            three = lambda a: a.rearrange("p (n g) -> p n g", g=D2)
            split_bias(step, bias2[:, :], biasf[:, 1, 0:C], C)
            split_bias(step, biaso[:, :], biasf[:, 1, C:2 * C], C)
            for e in range(2):
                step(dve.tensor_tensor(parity(biasf[:, 1, :], e), parity(ps[0:3, 6 + e, :], e), wide(bsl, [3, 4, D2], 1), ALU.add))
            step(dve.tensor_tensor(three(biasf[:, 1, :]), three(biasf[:, 1, :]), wide(rtemp[0:3, :], [3, 8, D2], 2), ALU.mult))
            split_bias(step, bias_logit[:, :], biasf[:, 1, :], INNER)
            step(dve.memset(vone[:, :, P:P + 1], 1.0))
            step(dve.memset(kvd[:, :, :], 0.0))
            dve.engine_nop().then_inc(S["vone_set"], 1)
            dve.engine_nop().then_inc(S["wc_sb"], 1)

            def low_part(n):
                dve.wait_ge(S["proj"], n + 2)
                dve.tensor_scalar(low, ps[:, 3, 0:C], 0.0, None, ALU.min).then_inc(S["feat_low"], 1)

            def high_part(n):
                dve.wait_ge(S["third"], n + 1)
                dve.wait_ge(S["feat_exp"], n + 1)
                dve.scalar_tensor_tensor(feat, ps[:, 3, 0:C], 0.0, grown, ALU.max, ALU.add).then_inc(S["feat_ready"], 1)

            tile = lambda a, t: a[:, ds(t, 1), :].rearrange("p a c -> p (a c)")
            dve.wait_ge(S["w_copied"], NCHUNK // P)
            dve.wait_ge(S["bucket_loaded"], 16)
            dve.sem_inc(S["added"], 2)

            def hot(q, u):
                dve.wait_ge(S["multiplied"], q + RING + 1 - HOT)
                dve.tensor_scalar(onehot[:, u, :], iota[:, :], slo[:, ds(q, 1)], sw[:, ds(q, 1)], ALU.is_equal, ALU.mult).then_inc(S["hot_ready"], 1)

            def buckets(n, count=STEP):
                return nc.values_load_multi_w_load_instructions(
                    group_bucket[0:1, ds(n * STEP, count)], engines=[mybir.EngineType.DVE], min_val=0, max_val=NT - 1,
                    skip_runtime_bounds_check_because="a count of NT comparisons less one, the first of which holds")[1]

            def groups(n, at, *js):
                for j in js:
                    g = n * STEP + j
                    for u in range(2):
                        hot(2 * g + 4 + u, (2 * j + 4 + u) % HOT)
                    b = at[j]
                    dve.wait_ge(S["multiplied"], RING + 2 * g + 2)
                    dve.wait_ge(S["added"], 2 + g)
                    dve.tensor_tensor(tile(acc, b), tile(acc, b), ps[:, j % 2, 0:C], ALU.add).then_inc(S["added"], 1)
            for q in range(4):
                hot(q, q)
            step.freeze()
            with dve.Fori(0, NT) as t:
                at = buckets(t)
                groups(t, at, 0, 1)
                low_part(t)
                groups(t, at, 2)
                high_part(t)
                groups(t, at, 3, 4, 5)
            dve.wait_ge(S["kv_done"], 1)
            for g in range(2):
                for h in range(4):
                    rr = slice(32 * h, 32 * h + 32)
                    dve.tensor_copy(kvd[rr, g, 32 * h:32 * h + 32], ps[rr, 4 + g, 32 * h:32 * h + 32])
                    last = dve.tensor_copy(kvd[rr, g, P + h:P + h + 1], ps[rr, 4 + g, P:P + 1])
            step(last)
            dve.engine_nop().then_inc(S["kv_diag"], 1)
            step.freeze()
            with dve.Fori(0, NT) as t:
                step.loop(t, 4)
                at = buckets(t + NT)
                groups(t + NT, at, 0, 1)
                low_part(t + NT)
                groups(t + NT, at, 2)
                high_part(t + NT)
                groups(t + NT, at, 3, 4)
                dve.wait_ge(S["third"], t + NT + 2)
                heads = ps[:, 6:8, 0:132]
                step(dve.tensor_scalar(zden, heads[:, :, P:P + 4], 1e-6, None, ALU.add))
                step(dve.reciprocal(zden, zden))
                dve.tensor_tensor(tmp.rearrange("p (g h m) -> p g h m", g=2, h=4), heads[:, :, 0:P].rearrange("p g (h m) -> p g h m", h=4), wide(zden, [P, 2, 4, 32], 3), ALU.mult).then_inc(S["res"], 1)
                dve.wait_ge(S["res"], t + 2)
                step(dve.tensor_tensor(tile(xn, t), tmp, tile(xn, t), ALU.add))
                step(dve.bn_stats(tile(stats, t), tile(xn, t)))
                groups(t + NT, at, 5)
            step.leave(NT)
            var_of_stats(step)
            dve.engine_nop().then_inc(S["var_ready"], 1)
            dve.wait_ge(S["rstd_root"], 2)
            step(dve.reciprocal(rstd[:, :], rstd[:, :]))

            def affine(t, n, to, center, scale):
                step(dve.scalar_tensor_tensor(tmp, tile(xn, t), center, rows[:, n, :], ALU.subtract, ALU.mult))
                return dve.scalar_tensor_tensor(to, tmp, scale, rows[:, n + 1, :], ALU.mult, ALU.add)
            step.freeze()
            def second(t):
                affine(t, 0, tile(xn, t), mean[:, ds(t, 1)], rstd[:, ds(t, 1)]).then_inc(S["mixed"], 1)

            def last_norm(t, more):
                n = t + 2 * NT
                at = buckets(n)
                groups(n, at, 0, 1, 2)
                if more:
                    second(t + 1)
                groups(n, at, 3)
                dve.wait_ge(S["third"], n + 2)
                dve.tensor_tensor(tile(xn, t), ps[:, 6, 0:C], tile(xn, t), ALU.add).then_inc(S["res"], 1)
                dve.wait_ge(S["res"], NT + t + 2)
                step(dve.bn_stats(tile(stats, t), tile(xn, t)))
                col = lambda k: tile(stats, t)[:, k:k + 1]
                step(dve.tensor_tensor(middle, col(1), col(4), ALU.add))
                step(dve.tensor_scalar(middle, middle, 0.5, None, ALU.mult))
                step(dve.tensor_tensor(off, middle, col(1), ALU.subtract))
                step(dve.tensor_tensor(off, off, off, ALU.mult))
                step(dve.tensor_tensor(spread, col(2), col(5), ALU.add))
                step(dve.scalar_tensor_tensor(spread, spread, 1.0 / C, off, ALU.mult, ALU.add))
                dve.tensor_scalar(spread, spread, 1e-5, None, ALU.add).then_inc(S["row_var"], 1)
                groups(n, at, 4)
                dve.wait_ge(S["row_root"], t + 1)
                step(dve.reciprocal(root, root))
                step(affine(t, 2, tile(xn, t), middle, root))
                groups(n, at, 5)
                dve.wait_ge(S["added"], 2 + n * STEP + STEP)
                step(dve.tensor_tensor(tile(acc, t), tile(acc, t), tile(xn, t), ALU.add))
            second(0)
            step.freeze()
            with dve.Fori(0, NT - 1) as t:
                step.loop(t, 12)
                last_norm(t, True)
            step.leave(NT - 1)
            last_norm(NT - 1, False)
            step.freeze()
            for k in range((REST + RING - 1) // RING):
                count = min(STEP, REST // 2 - k * STEP)
                groups(3 * NT + k, buckets(3 * NT + k, count), *range(count))
            dve.wait_ge(S["added"], 2 + NGRP)
            step.freeze()
            with dve.Fori(0, NT) as t:
                step.loop(t, 1)
                step(dve.bn_stats(tile(stats, t), tile(acc, t)))
            step.leave(NT)
            var_of_stats(step)
            dve.engine_nop().then_inc(S["var_ready"], 1)
            dve.wait_ge(S["rstd_root"], 3)
            step(dve.reciprocal(rstd[:, :], rstd[:, :]))
            step(dve.memset(xs[:, :, C:C + 1], 1.0))

            def normed(t, h):
                dve.wait_ge(S["f_pair"], t + 1)
                dve.tensor_scalar(xs[:, h, 0:C], tile(acc, t), mean[:, ds(t, 1)], rstd[:, ds(t, 1)], ALU.subtract, ALU.mult).then_inc(S["f_norm"], 1)

            def soften(t, h):
                step.loop(t, 2)
                dve.wait_ge(S["f_logit"], t + 1)
                step(dve.tensor_reduce(fmax, three(ps[:, h, :]), AX.X, ALU.max))
                dve.wait_ge(S["f_exp"], t + 1)
                dve.tensor_tensor(three(lowered), three(ps[:, h, :]), wide(fmax, [P, 8, D2], 2), ALU.subtract).then_inc(S["f_low"], 1)
                dve.wait_ge(S["f_exp"], t + 2)
                step(dve.tensor_reduce(fsum[:, h, :], three(expd), AX.X, ALU.add))
                dve.reciprocal(fsum[:, h, :], fsum[:, h, :]).then_inc(S["f_sum"], 1)
            step.freeze()
            normed(0, 0)
            with dve.Fori(0, NT // 2) as i:
                normed(2 * i + 1, 1)
                soften(2 * i, 0)
                normed(2 * i + 2, 0)
                soften(2 * i + 1, 1)
            soften(NT - 1, 0)
            step.leave(NT)
            dve.wait_ge(S["tok_ps"], 1)
            step(dve.tensor_scalar(tden, ps[:, 4:8, C], 1e-5, None, ALU.add))
            step(dve.reciprocal(tden, tden))
            step(dve.tensor_tensor(token[:, :, :], ps[:, 4:8, 0:C + 1], wide(tden, [P, 4, C + 1], 2), ALU.mult))
            dve.engine_nop().then_inc(S["tok_sb"], 1)
            dve.wait_ge(S["tok_ps"], 2)
            dve.tensor_copy(tokenT[:, 0, :], ps[:, 0, :])
            dve.tensor_copy(tokenT[:, 1, :], ps[:, 1, :])
            step(dve.tensor_copy(ratio, ps[0:1, 2, :]))
            dve.engine_nop().then_inc(S["tok_sb"], 1)
            dve.wait_ge(S["tok_ps"], 3)
            step(dve.tensor_copy(tokf, ps[0:D2, 3, :]))
            dve.engine_nop().then_inc(S["tok_sb"], 1)
            dve.wait_ge(S["tok_ps"], 4)
            dve.tensor_copy(qk[:, 0, :], ps[0:D2, 0, :])
            dve.tensor_copy(qk[:, 1, :], ps[0:D2, 1, :])
            step(dve.tensor_copy(vtok, ps[0:D2, 2, :]))
            dve.engine_nop().then_inc(S["tok_sb"], 1)
            dve.wait_ge(S["tok_ps"], 5)
            step(dve.tensor_reduce(amax, three(ps[0:D2, 3, :]), AX.X, ALU.max))
            step(dve.tensor_tensor(three(att), three(ps[0:D2, 3, :]), wide(amax, [D2, 8, D2], 2), ALU.subtract))
            for k in range(5):
                dve.engine_nop().then_inc(S["tok_sb"], 1)
            dve.wait_ge(S["tok_sb"], 10)
            step(dve.tensor_reduce(asum, three(att), AX.X, ALU.add))
            step(dve.reciprocal(asum, asum))
            step(dve.tensor_tensor(three(att), three(att), wide(asum, [D2, 8, D2], 2), ALU.mult))
            dve.engine_nop().then_inc(S["tok_sb"], 1)
            dve.wait_ge(S["tok_ps"], 6)
            step(dve.tensor_copy(attT, ps[0:D2, 0, :]))
            dve.engine_nop().then_inc(S["tok_sb"], 1)
            dve.wait_ge(S["tok_ps"], 7)
            step(dve.tensor_copy(outT, ps[0:D2, 1, :]))
            dve.engine_nop().then_inc(S["tok_sb"], 1)
            dve.wait_ge(S["tok_ps"], 8)
            for m in range(4):
                last = dve.tensor_copy(mout[:, m, :], ps[:, 4 + m, 0:C])
            step(last)
            dve.engine_nop().then_inc(S["tok_sb"], 1)

            def add_out(t, h):
                dve.wait_ge(S["out_ps"], t + 2)
                dve.tensor_tensor(tile(acc, t), tile(acc, t), ps[:, h, 0:C], ALU.add).then_inc(S["out_sum"], 1)
            with dve.Fori(0, NT // 4) as i:
                for h in range(4):
                    add_out(4 * i + h, h)
            add_out(NT - 1, 0)

        @block.tensor
        def _(pe):
            def seen(s, v):
                pe.wait_ge(s, v)
                pe.sem_inc(S["pace_pe"], 1)
            pe.wait_ge(S["consts"], 10)
            mm = pe.matmul
            for k in range(QN):
                mm(ps[:, k, 0:QW], zerob[:, 0:P], zerob[:, 0:QW], start=True, stop=False)
            pe.wait_ge(S["raw_loaded"], 48)
            for k in range(10):
                raw = raw_qkv[:, k, :] if k < 6 else (raw_w1 if k < 8 else raw_w2)[:, k % 2, :]
                if k >= 2:
                    pe.wait_ge(S["trans_sb"], k - 1)
                for c in range(2):
                    last = pe.transpose(ps[:, 6 + k % 2, c * P:(c + 1) * P], raw[:, c * P:(c + 1) * P], identf[:, :])
                last.then_inc(S["trans_ps"], 1)
            pe.wait_ge(S["trans_sb"], 10)
            with pe.Fori(0, NT) as b:
                seen(S["prod_ready"], b + 1)
                for k in range(QN):
                    last = mm(ps[:, k, 0:QW], identb[:, :], ranked[:, k * QW:(k + 1) * QW], start=False, stop=False)
                last.then_inc(S["prod_used"], 1)
            pe.wait_ge(S["count_copied"], NT + 1)
            flat = cnt[:, :, :].rearrange("p b s -> p (b s)")
            for k in range(3):
                last = mm(ps[:, 4 + k, 0:CW], before[:, :], flat[:, k * CW:(k + 1) * CW], start=True, stop=True)
            last.then_inc(S["count_sums"], 1)
            pe.wait_ge(S["sums_read"], 1)
            for k in range(3):
                last = mm(ps[:, 4 + k, 0:CW], onesb[:, :], flat[:, k * CW:(k + 1) * CW], start=True, stop=True)
            last.then_inc(S["count_sums"], 1)
            with pe.Fori(0, NT) as b:
                seen(S["based_ready"], b + 1)
                for k in range(QN):
                    last = mm(ps[:, k, 0:QW], identf[:, :], based[:, k * QW:(k + 1) * QW], start=False, stop=False)
                last.then_inc(S["based_used"], 1)
            for k in range(QN):
                last = mm(ps[:, k, 0:QW], zerob[:, 0:P], zerob[:, 0:QW], start=False, stop=True)
            last.then_inc(S["based_used"], 1)
            pe.sem_inc(S["sorted_batches"], 2)
            with pe.Fori(0, NSUP) as i:
                seen(S["local_copied"], i + 1)
                mm(ps[:, 7, 0:P], zerob[:, 0:P], zerob[:, 0:P], start=True, stop=False)
                with pe.Fori(0, NBAT // 2) as j:
                    for h in range(2):
                        seen(S["pair_ready"], i * NBAT + j * 2 + h + 2)
                        for u in range(BAT):
                            last = mm(ps[:, 7, 0:P], hot_part[:, h, u, :], hot_rec[:, h, u, :, :].rearrange("p a v -> p (a v)"), start=False, stop=False)
                        last.then_inc(S["sorted_batches"], 1)
                mm(ps[:, 7, 0:P], zerob[:, 0:P], zerob[:, 0:P], start=False, stop=True).then_inc(S["local_sorted"], 1)
            for k in range(NCHUNK // P):
                pe.wait_ge(loaded_back[k % 2], 16 * (k // 2 + 1))
                if k >= 2:
                    pe.wait_ge(S["unpacked"], k - 1)
                    pe.wait_ge(S["w_copied"], k - 1)
                for v in range(REC):
                    last = pe.transpose(ps[:, 4 + 2 * v + k % 2, 0:P], back[:, k % 2, v::REC], identf[:, :])
                last.then_inc(S["transposed"], 1)

            pe.wait_ge(S["wx_loaded"], 16)
            for m in range(4):
                if m >= 2:
                    pe.wait_ge(S["wxT_sb"], m - 1)
                for c in range(2):
                    last = pe.transpose(ps[:, 2 + m % 2, c * P:(c + 1) * P], raw_wx[:, c, m * P:(m + 1) * P], identf[:, :])
                last.then_inc(S["wxT_ps"], 1)
            pe.wait_ge(S["wxT_sb"], 4)
            pe.wait_ge(S["unpacked"], NCHUNK // P)
            pe.wait_ge(S["w_copied"], NCHUNK // P)
            pe.wait_ge(S["rows_loaded"], 16 * 17)
            for h in range(8):
                half_of = slice(h % 2 * D2, h % 2 * D2 + D2)
                for k in range(2):
                    mm(ps[:, 2 + k + 2 * (h % 2), h * D2:(h + 1) * D2], wxT[half_of, h // 2, k * P:(k + 1) * P], wslice[half_of, :], start=True, stop=True)
                last = mm(ps[0:3, 6 + h % 2, h * D2:(h + 1) * D2], bxc[half_of, h // 2:h // 2 + 1].broadcast_to([D2, 3]), wslice[half_of, :], start=True, stop=True)
            last.then_inc(S["wc_ps"], 1)
            pe.wait_ge(S["wc_sb"], 1)
            pe.sem_inc(S["multiplied"], RING)

            def groups(n, *js):
                for j in js:
                    for u in range(2):
                        q = 2 * j + u
                        seen(gathered[q], 16 * n + 16)
                        seen(S["hot_ready"], RING * n + q + 1)
                        if u == 0:
                            seen(S["added"], n * STEP + j + 1)
                        mm(ps[:, j % 2, 0:C], onehot[:, q % HOT, :], gath[:, q, :], start=u == 0, stop=u == 1).then_inc(S["multiplied"], 1)

            def turn(n, t):
                seen(S["xt_sb"], n + 1)
                seen(S["cur_sb"], n + 1)
                for c in range(2):
                    last = pe.transpose(ps[:, 2, c * P:(c + 1) * P], xcur[:, c * P:(c + 1) * P], identf[:, :])
                last.then_inc(S["xt_ps"], 1)

            tile = lambda a, t: a[:, ds(t, 1), :].rearrange("p a c -> p (a c)")
            for g in range(2):
                mm(ps[:, 4 + g, 0:P + 1], zerob[:, 0:P], zerob[:, 0:P + 1], start=True, stop=False)

            def kv_tile(t, edge):
                turn(t, t)
                groups(t, 0, 1)
                seen(S["feat_ready"], t + 1)
                seen(S["v_sb"], t + 1)
                seen(S["xt_sb"], t + 2)
                for v in range(2):
                    for c in range(2):
                        last = mm(ps[:, 3 + 3 * v, 0:C], xT[:, c, :], wqkvT[:, c, C * (1 + v):C * (2 + v)], start=c == 0, stop=c == 1)
                last.then_inc(S["proj"], 1)
                groups(t, 2, 3)
                seen(S["feat_ready"], t + 2)
                seen(S["v_sb"], t + 2)
                r = TAIL if edge else P
                for g in range(2):
                    last = mm(ps[:, 4 + g, 0:P + 1], feat[0:r, g * P:(g + 1) * P], vone[0:r, g, :], start=False, stop=edge)
                last.then_inc(S["third"], 1)
                groups(t, 4, 5)
            with pe.Fori(0, NT - 1) as t:
                kv_tile(t, False)
            kv_tile(NT - 1, True)
            pe.wait_ge(S["third"], NT + 1)
            pe.sem_inc(S["kv_done"], 1)
            pe.wait_ge(S["kv_diag"], 1)
            with pe.Fori(0, NT) as t:
                turn(t + NT, t)
                groups(t + NT, 0, 1)
                seen(S["feat_ready"], t + NT + 1)
                seen(S["xt_sb"], t + NT + 2)
                for g in range(2):
                    for c in range(2):
                        last = mm(ps[:, 3, g * P:(g + 1) * P], wqkvT[:, c, g * P:(g + 1) * P], xT[:, c, :], start=c == 0, stop=c == 1)
                last.then_inc(S["proj"], 1)
                groups(t + NT, 2, 3)
                seen(S["res"], t + 1)
                seen(S["feat_ready"], t + NT + 2)
                for g in range(2):
                    last = mm(ps[:, 6 + g, 0:132], feat[:, g * P:(g + 1) * P], kvd[:, g, :], start=True, stop=True)
                last.then_inc(S["third"], 1)
                groups(t + NT, 4, 5)
            with pe.Fori(0, NT) as t:
                n = t + 2 * NT
                turn(n, t)
                groups(n, 0, 1)
                seen(S["feat_ready"], n + 1)
                seen(S["xt_sb"], n + 2)
                for g in range(2):
                    for c in range(2):
                        last = mm(ps[:, 3, g * P:(g + 1) * P], w1T[:, c, g * P:(g + 1) * P], xT[:, c, :], start=c == 0, stop=c == 1)
                last.then_inc(S["proj"], 1)
                groups(n, 2, 3)
                seen(S["res"], t + NT + 1)
                seen(S["feat_ready"], n + 2)
                for g in range(2):
                    mm(ps[:, 6, 0:C], feat[:, g * P:(g + 1) * P], w2T[:, g, :], start=g == 0, stop=False)
                mm(ps[:, 6, 0:C], onesb[0:3, :], bias2[:, :], start=False, stop=True).then_inc(S["third"], 1)
                groups(n, 4, 5)
            for k in range((REST + RING - 1) // RING):
                groups(3 * NT + k, *range(min(STEP, REST // 2 - k * STEP)))

            def logit(t, h):
                seen(S["f_norm"], t + 1)
                seen(S["f_xsT"], t)
                for c in range(2):
                    last = pe.transpose(ps[:, 2, c * P:(c + 1) * P], xs[:, h, c * P:(c + 1) * P], identf[:, :])
                last.then_inc(S["f_xT"], 1)
                seen(S["f_xsT"], t + 1)
                for c in range(2):
                    mm(ps[:, h, :], xsT[:, h, c, :], wc[:, c, :], start=c == 0, stop=False)
                mm(ps[:, h, :], onesb[0:3, :], bias_logit[:, :], start=False, stop=True).then_inc(S["f_logit"], 1)

            def gather_slices(t, h, edge):
                seen(S["f_slice"], t + 1)
                r = TAIL if edge else P
                for m in range(4):
                    last = mm(ps[:, 4 + m, 0:C + 1], slices[0:r, h, m * P:(m + 1) * P], xs[0:r, h, :], start=False, stop=edge)
                seen(S["f_sTsb"], t + 1)
                for m in range(4):
                    last = pe.transpose(ps[:, 3, m * P:(m + 1) * P], slices[:, h, m * P:(m + 1) * P], identf[:, :])
                last.then_inc(S["f_pair"], 1)
            pe.wait_ge(S["rstd_root"], 3)
            for m in range(4):
                mm(ps[:, 4 + m, 0:C + 1], zerob[:, 0:P], zerob[:, 0:C + 1], start=True, stop=False)
            pe.sem_inc(S["f_pair"], 1)
            logit(0, 0)
            with pe.Fori(0, NT // 2) as i:
                logit(2 * i + 1, 1)
                gather_slices(2 * i, 0, False)
                logit(2 * i + 2, 0)
                gather_slices(2 * i + 1, 1, False)
            gather_slices(NT - 1, 0, True)
            pe.wait_ge(S["f_pair"], NT + 2)
            pe.sem_inc(S["tok_ps"], 1)
            pe.wait_ge(S["tok_sb"], 1)
            pe.wait_ge(S["late_loaded"], 16)
            for m in range(4):
                for c in range(2):
                    pe.transpose(ps[:, c, m * P:(m + 1) * P], token[:, m, c * P:(c + 1) * P], identf[:, :])
                last = pe.transpose(ps[0:1, 2, m * P:(m + 1) * P], token[:, m, C:C + 1], identf[:, :])
            last.then_inc(S["tok_ps"], 1)
            pe.wait_ge(S["tok_sb"], 2)
            pe.wait_ge(S["f_sTsb"], NT + 1)
            for h in range(8):
                hh = slice(h * D2, (h + 1) * D2)
                for c in range(2):
                    mm(ps[0:D2, 3, hh], wfx[:, c, hh], tokenT[:, c, hh], start=c == 0, stop=False)
                last = mm(ps[0:D2, 3, hh], bfx[:, hh], ratio[:, hh], start=False, stop=True)
            last.then_inc(S["tok_ps"], 1)
            pe.wait_ge(S["tok_sb"], 3)
            mm(ps[0:D2, 0, :], wq, tokf, start=True, stop=True)
            mm(ps[0:D2, 1, :], wk, tokf, start=True, stop=True)
            for h in range(8):
                hh = slice(h * D2, (h + 1) * D2)
                last = mm(ps[0:D2, 2, hh], tokf[:, hh], wv, start=True, stop=True)
            last.then_inc(S["tok_ps"], 1)
            pe.wait_ge(S["tok_sb"], 4)
            for h in range(8):
                hh = slice(h * D2, (h + 1) * D2)
                last = mm(ps[0:D2, 3, hh], qk[:, 0, hh], qk[:, 1, hh], start=True, stop=True)
            last.then_inc(S["tok_ps"], 1)
            pe.wait_ge(S["tok_sb"], 11)
            for h in range(8):
                hh = slice(h * D2, (h + 1) * D2)
                last = pe.transpose(ps[0:D2, 0, hh], att[:, hh], identf[0:D2, 0:D2])
            last.then_inc(S["tok_ps"], 1)
            pe.wait_ge(S["tok_sb"], 12)
            for h in range(8):
                hh = slice(h * D2, (h + 1) * D2)
                last = mm(ps[0:D2, 1, hh], vtok[:, hh], attT[:, hh], start=True, stop=True)
            last.then_inc(S["tok_ps"], 1)
            pe.wait_ge(S["tok_sb"], 13)
            for h in range(8):
                last = mm(ps[h % 2 * D2:h % 2 * D2 + D2, 4 + h // 2, 0:C], outT[:, h * D2:(h + 1) * D2], wout[:, h, :], start=True, stop=True)
            last.then_inc(S["tok_ps"], 1)
            pe.wait_ge(S["tok_sb"], 14)

            def project(t, h):
                seen(S["sl_sb"], t + 1)
                for m in range(4):
                    mm(ps[:, h, 0:C], slcur[:, h, m, :], mout[:, m, :], start=m == 0, stop=False)
                mm(ps[:, h, 0:C], onesb[0:3, :], biaso[:, :], start=False, stop=True).then_inc(S["out_ps"], 1)
            with pe.Fori(0, NT // 4) as i:
                for h in range(4):
                    seen(S["out_sum"], 4 * i + 1)
                    project(4 * i + h, h)
            seen(S["out_sum"], NT - 1 + 1)
            project(NT - 1, 0)


_INS = ["x", "src", "dst", "edge_weight", "L0_mix_Wqkv", "L0_mix_ln1_g", "L0_mix_ln1_b", "L0_mix_W1", "L0_mix_b1",
        "L0_mix_W2", "L0_mix_b2", "L0_mix_ln2_g", "L0_mix_ln2_b", "L0_ffn_W_fx", "L0_ffn_b_fx", "L0_ffn_W_x",
        "L0_ffn_b_x", "L0_ffn_W_slice", "L0_ffn_b_slice", "L0_ffn_W_q", "L0_ffn_W_k", "L0_ffn_W_v", "L0_ffn_W_out",
        "L0_ffn_b_out", "L0_ffn_temperature"]


def kernel(**inputs):
    import numpy as np
    import concourse.bacc as bacc
    from concourse.bass_utils import run_bass_kernel_spmd

    nc = bacc.Bacc("TRN2", target_bir_lowering=False, num_devices=1)
    arrays, args = {}, []
    for name in _INS:
        a = np.ascontiguousarray(inputs[name])
        arrays[f"in_{name}"] = a
        args.append(nc.dram_tensor(f"in_{name}", a.shape, mybir.dt.from_np(a.dtype), kind="ExternalInput").ap())
    args.append(nc.dram_tensor("out_rows", (N, C), F32, kind="ExternalOutput").ap())
    program(nc, *args)
    result = run_bass_kernel_spmd(nc, [arrays], core_ids=[0])
    return result.results[0]["out_rows"]
```

```python
import concourse.bass as bass
from concourse import mybir
from contextlib import ExitStack

F32, I32, BF16 = mybir.dt.float32, mybir.dt.int32, mybir.dt.bfloat16
ALU = mybir.AluOpType
ACT = mybir.ActivationFunctionType
AX = mybir.AxisListType
ds = bass.ds

P = 128
N, C, E = 6250, 256, 206250
NT = (N + P - 1) // P
TAIL = N - (NT - 1) * P
COLS = 1620
LASTC = E - (P - 1) * COLS
SUPC = 60
NSUP = COLS // SUPC
BAT = 6
NBAT = SUPC // BAT
REC = 2
BLK = 8
BW = BLK * REC
NG8 = 8
GRP = 2 * P // BLK
NGRP = 896
NCHUNK = 2 * NGRP
RING = 12
HOT = 6
STEP = RING // 2
REST = NCHUNK - 3 * NT * RING
NBLK = NGRP * GRP
TRASH = NBLK
NREC = NBLK + NSUP * NG8 * P
assert NSUP * SUPC == COLS and (P * SUPC + NT * (BLK - 1)) <= NG8 * P * BLK
assert (E + NSUP * NT * (BLK - 1) + NT * (2 * P - BLK)) // (2 * P) <= NGRP
PIPE = (NT - 4) // 4
D2 = 64
INNER = 512
QN = 4
QW = -(-NSUP // QN) * SUPC
BANKS = [(k, k * QW, min(COLS, (k + 1) * QW)) for k in range(QN)]
WB = 3
WHOLE = WB * QW // SUPC
CW = NT * NSUP // 3


ARENA = NT * C + 3 * (NCHUNK + 4) + 5 * COLS


def wide(ap, shape, axis):
    names = list("abcd"[:len(ap.shape)])
    split, new = list(names), list(names)
    if axis == len(names):
        split[-1] = f"({names[-1]} z)"
    else:
        split[axis] = f"(z {names[axis]})"
    new.insert(axis, "z")
    return ap.rearrange(f"{' '.join(split)} -> {' '.join(new)}", z=1).broadcast_to(shape)


class Steps:

    def __init__(self, eng, sem):
        self.eng, self.sem, self.base, self.off, self.reg = eng, sem, 0, 0, 0

    def loop(self, i, per):
        self.reg, self.off, self.per = i * per, 0, per

    def leave(self, count):
        assert self.off == self.per, (self.off, self.per)
        self.base, self.reg, self.off = self.base + count * self.per, 0, 0

    def freeze(self):
        self.base, self.off = self.base + self.off, 0

    def __call__(self, ins):
        self.off += 1
        ins.then_inc(self.sem, 1)
        self.eng.wait_ge(self.sem, self.base + self.reg + self.off)


def pipeline(eng, body, steps=None, per=0):
    for t in range(2):
        body(t, t)
    if steps:
        steps.freeze()
    with eng.Fori(0, PIPE) as i:
        if steps:
            steps.loop(i, 4 * per)
        for u in range(4):
            body(4 * i + 2 + u, (2 + u) % 4)
    if steps:
        steps.leave(PIPE)
    for t in range(2 + 4 * PIPE, NT + 2):
        body(t, t % 4)


def live(t, back):
    return not isinstance(t, int) or 0 <= t - back < NT


def program(nc, x, src, dst, edge_weight, Wqkv, ln1_g, ln1_b, W1, b1, W2, b2, ln2_g, ln2_b,
            W_fx, b_fx, W_x, b_x, W_slice, b_slice, W_q, W_k, W_v, W_out, b_out, temperature, out):
    ctx = ExitStack()
    with ctx:
        def sb(name, shape, dt=F32):
            return ctx.enter_context(nc.sbuf_tensor(name, shape, dt))

        def sem(name):
            return ctx.enter_context(nc.semaphore(name))

        rec = nc.dram_tensor("edge_records", (NREC, BW), F32).ap()
        xg = nc.dram_tensor("normed_rows", (N + 1, C), F32).ap()
        bucket_dram = nc.dram_tensor("group_buckets", (P, NGRP // P), I32).ap()

        ps = ctx.enter_context(nc.psum_tensor("ps", [P, 8, 512], F32))
        acc = sb("acc", [P, NT, C])
        iota = sb("iota", [P, P])
        identf = sb("identf", [P, P])
        identb = sb("identb", [P, P], BF16)
        before = sb("before", [P, P], BF16)
        onesb = sb("onesb", [P, P], BF16)
        zerob = sb("zerob", [P, QW], BF16)
        block_no = sb("block_no", [P, NG8])
        group_no = sb("group_no", [P, NGRP // P])
        stats = sb("stats", [P, NT, 6])
        mean = sb("mean", [P, NT])
        half = sb("half", [P, NT])
        rstd = sb("rstd", [P, NT])
        arena = sb("arena", [P, ARENA])
        bench = sb("bench", [P, 3456])

        def view(at, shape, dt=F32):
            n = 1
            for d in shape:
                n *= d
            v = arena[:, at:at + n]
            if dt is not F32:
                v = v.bitcast(dt)
            if len(shape) == 2:
                v = v.rearrange("p (a b) -> p a b", b=shape[1])
            return v

        xn = view(0, [NT, C])
        tables = [NT, NSUP]
        tables_s = [NSUP, NT + 1]
        tw = NSUP * (NT + 1)
        tabi = view(0, [NT * NSUP], I32)
        nbi = view(tw, [NT * NSUP], I32)
        nb = view(tw, tables)
        nbs = view(2 * tw, tables_s)
        rstb = view(3 * tw, tables_s)
        rsts = view(4 * tw, tables)
        gex = view(5 * tw, tables)
        ginc = view(6 * tw, tables)
        delta = view(7 * tw, tables_s)
        base = view(8 * tw, tables)
        base_part = [view((5 + n) * tw, [NT * (NSUP - WHOLE) // 2 + 1]).bitcast(BF16)[:, 0:NT * (NSUP - WHOLE)].rearrange("p (b s) -> p b s", b=NT) for n in range(2)]
        gmat = view(9 * tw, [NGRP // P, NT])
        e0, ew = NT * C, NCHUNK + 4
        srci = view(e0, [COLS], I32)
        dsti = view(e0 + ew, [COLS], I32)
        loi = view(e0 + 2 * ew, [COLS], I32)
        posi = srci
        gidx = view(e0, [NCHUNK], I32)
        slo = view(e0 + ew, [NCHUNK + 4])
        sw = view(e0 + 2 * ew, [NCHUNK + 4])
        v0 = e0 + 3 * ew
        vals = view(v0, [COLS, REC])
        based_at = (view(v0 + 2 * COLS, [COLS]), bench[:, COLS // 2:COLS // 2 + COLS])
        base_float = view(v0 + 2 * COLS, [COLS])
        based = [a[:, 0:WB * QW] for a in based_at]
        based_part = [a[:, WB * QW:COLS].bitcast(BF16).rearrange("p (n c) -> p n c", n=2) for a in based_at]
        gath = view(v0, [RING, C])
        onehot = view(v0 + RING * C, [HOT, P])
        w0 = v0 + 3 * COLS
        wraw = view(w0, [COLS])
        slotp = wraw
        restart = view(w0 + COLS, [NSUP, SUPC])
        slotc = view(w0 + COLS, [COLS])
        bucket, mask0, running, ranked0 = (bench[:, k * COLS // 2:(k + 1) * COLS // 2].bitcast(BF16) for k in range(4))
        hot_part = bench[:, 0:2 * BAT * P].rearrange("p (h u a) -> p h u a", h=2, u=BAT)
        hot_col = bench[:, 2 * BAT * P:2 * BAT * P + BAT * 64].rearrange("p (u a) -> p u a", u=BAT)
        hot_rec = bench[:, 2 * BAT * P + BAT * 64:3456].rearrange("p (h u a v) -> p h u a v", h=2, u=BAT, v=REC)
        tabs = sb("tabs", [P, 4096])
        cnt = tabs[:, 0:NT * NSUP // 2 + 1].bitcast(BF16)[:, 0:NT * NSUP].rearrange("p (b s) -> p b s", s=NSUP)
        lstart = tabs[:, 672:672 + tw].rearrange("p (s b) -> p s b", s=NSUP)
        jump = tabs[:, 672 + tw:672 + 2 * tw].rearrange("p (s b) -> p s b", s=NSUP)
        mask1, ranked1 = (tabs[:, 672 + k * COLS // 2:672 + (k + 1) * COLS // 2].bitcast(BF16) for k in range(2))
        mask, ranked = (mask0, mask1), (ranked0, ranked1)
        gi = sb("gi", [P, NT], I32)
        gn = sb("gn", [P, NT])
        gst = sb("gst", [P, NT])
        gone = sb("gone", [P, NT])
        gbuck = sb("gbuck", [P, NGRP // P])
        gbucki = sb("gbucki", [P, NGRP // P], I32)
        group_bucket = sb("group_bucket", [1, NGRP], I32)
        passed = tabs[:, 672 + 2 * tw:672 + 2 * tw + NG8 * (NT + 1)].rearrange("p (g b) -> p g b", g=NG8)
        moved = sb("moved", [P, NG8])
        dest = sb("dest", [P, NG8], I32)
        raw_qkv = view(0, [6, C])
        raw_w1 = view(6 * C, [2, C])
        raw_w2 = view(8 * C, [2, C])
        zerof = view(5 * tw, [512])
        raw_wx = bench[:, 0:2 * INNER].rearrange("p (k o) -> p k o", o=INNER)
        wxT = bench[:, 2 * INNER:4 * INNER].rearrange("p (m c) -> p m c", c=C)
        xT = bench[:, 0:C].rearrange("p (k t) -> p k t", t=P)
        low = bench[:, C:2 * C]
        grown = bench[:, 2 * C:3 * C]
        feat = bench[:, 3 * C:4 * C]
        vone = bench[:, 4 * C:4 * C + 2 * (P + 1)].rearrange("p (g m) -> p g m", m=P + 1)
        tmp = bench[:, 5 * C + 4:6 * C + 4]
        zden = bench[:, 6 * C + 4:6 * C + 12].rearrange("p (g h) -> p g h", h=4)
        xcur = bench[:, 6 * C + 12:7 * C + 12]
        slcur = bench[:, 0:4 * INNER].rearrange("p (h m t) -> p h m t", h=4, t=P)
        wmix = sb("wmix", [P, 2824])
        wqkvT = wmix[:, 0:6 * C].rearrange("p (k o) -> p k o", o=3 * C)
        w1T = wmix[:, 6 * C:8 * C].rearrange("p (k o) -> p k o", o=C)
        w2T = wmix[:, 8 * C:10 * C].rearrange("p (k o) -> p k o", o=C)
        kvd = wmix[:, 10 * C:10 * C + 264].rearrange("p (g m) -> p g m", m=132)
        wout = wmix[0:D2, 0:8 * C].rearrange("p (h c) -> p h c", c=C)
        wc = tabs[:, 0:2 * INNER].rearrange("p (k o) -> p k o", o=INNER)
        mout = tabs[:, 0:4 * C].rearrange("p (m c) -> p m c", c=C)
        wfx = tabs[:, 2 * INNER:4 * INNER].rearrange("p (k o) -> p k o", o=INNER)
        rows = tabs[:, 4 * INNER:4 * INNER + 4 * C].rearrange("p (n c) -> p n c", c=C)
        small = tabs[:, 3072:4096]
        wslice = small[:, 0:64]
        wq, wk, wv = (small[0:D2, 64 + 64 * n:128 + 64 * n] for n in range(3))
        bxc = small[:, 256:260]
        b1c = small[:, 260:262]
        rtemp = small[:, 262:270]
        bsl = small[0:3, 270:334]
        spread, root, middle, off = (small[:, 880 + n:881 + n] for n in range(4))
        bfx = small[0:1, 350:862]
        biasf = arena[0:3, w0:w0 + 3 * INNER].rearrange("p (n c) -> p n c", c=INNER)
        bias_logit = sb("bias_logit", [3, INNER], BF16)
        bias2 = sb("bias2", [3, C], BF16)
        biaso = sb("biaso", [3, C], BF16)
        xs = bench[:, 0:4 * (C + 1)].rearrange("p (h c) -> p h c", c=C + 1)
        xsT = bench[:, 1028:1028 + C].rearrange("p (k t) -> p k t", t=P)
        slices = bench[:, 1284:1284 + 4 * INNER].rearrange("p (h o) -> p h o", h=4)
        fmax = bench[:, 3332:3348].rearrange("p (h o) -> p h o", h=2)
        fsum = bench[:, 3348:3380].rearrange("p (h o) -> p h o", h=4)
        sliceT = view(0, [4, NT * P])
        token = bench[:, 0:4 * (C + 1)].rearrange("p (m c) -> p m c", c=C + 1)
        tokenT = bench[:, 1028:1028 + 2 * INNER].rearrange("p (k o) -> p k o", o=INNER)
        ratio = bench[0:1, 2052:2052 + INNER]
        tokf = bench[0:D2, 2564:2564 + INNER]
        tden = bench[:, 3076:3080]
        qk = tabs[0:D2, 4 * INNER:6 * INNER].rearrange("p (n o) -> p n o", o=INNER)
        vtok = bench[0:D2, 0:INNER]
        att = bench[0:D2, INNER:2 * INNER]
        attT = bench[0:D2, 1028:1028 + INNER]
        outT = bench[0:D2, 1540:1540 + INNER]
        amax = small[0:D2, 334:342]
        asum = small[0:D2, 342:350]
        local = sb("local", [P, NG8 * BW])
        back = sb("back", [P, 2, P * REC])
        geti = sb("geti", [P, P], I32)
        getl = sb("getl", [P, P], I32)
        iring = sb("iring", [P, 2, RING], I32)

        names = """row_stats masked row_var row_root scatter_done x_loaded src_loaded dst_loaded w_loaded consts pad_set zero_rows zeroed
            step_dve var_ready rstd_root rstd_ready normed xn_stored edges_ready prod_ready prod_used scan_ready
            count_copied count_sums sums_read based_ready based_used pos_read pair_ready col_hot sorted_batches
            local_sorted local_copied dest_ready super_zero
            bucket_ready bucket_stored bucket_loaded transposed unpacked w_copied
            raw_loaded trans_ps trans_sb rows_loaded wx_loaded wxT_ps wxT_sb wc_ps wc_sb late_loaded
            cur_sb sl_sb xt_ps xt_sb proj feat_low feat_exp feat_ready v_sb third res kv_start kv_done kv_diag bias_ready
            swept vone_set mixed f_norm f_logit f_low f_exp f_sum f_slice f_pair f_xT f_xsT f_sTsb tok_ps tok_sb out_ps out_sum
            ring_ready hot_ready multiplied added out_stored pace pace_sp pace_pe pace_act stepact""".split()
        S = {n: sem(n) for n in names}
        START_AT_ONE = """third proj xt_ps out_ps count_copied prod_used based_used pair_ready f_pair f_exp local_copied xt_sb feat_ready v_sb res f_sTsb out_sum scatter_done""".split()
        scattered = [sem(f"scattered{g}") for g in range(NG8)]
        gathered = [sem(f"gathered{g}") for g in range(RING)]
        loaded_back = [sem(f"loaded_back{g}") for g in range(2)]
        block = ctx.enter_context(nc.Block())

        @block.sync
        def _(sp):
            for name in START_AT_ONE:
                sp.sem_inc(S[name], 1)
            sp.sem_inc(S["out_ps"], 3)
            sp.sem_inc(S["out_sum"], 3)
            sp.dma_start(raw_qkv, Wqkv.rearrange("(o p) c -> p o c", p=P)).then_inc(S["raw_loaded"], 16)
            sp.dma_start(raw_w1, W1.rearrange("(o p) c -> p o c", p=P)).then_inc(S["raw_loaded"], 16)
            sp.dma_start(raw_w2, W2.rearrange("(o p) c -> p o c", p=P)).then_inc(S["raw_loaded"], 16)
            sp.wait_ge(S["pad_set"], 4)
            sp.dma_start(srci[0:112, :], src[0:112 * COLS].rearrange("(p c) -> p c", c=COLS)).then_inc(S["src_loaded"], 16)
            sp.dma_start(srci[112:127, :], src[112 * COLS:127 * COLS].rearrange("(p c) -> p c", c=COLS)).then_inc(S["src_loaded"], 16)
            sp.dma_start(srci[127:128, 0:LASTC], src[127 * COLS:E].rearrange("(p c) -> p c", p=1)).then_inc(S["src_loaded"], 16)
            sp.dma_start(dsti[0:112, :], dst[0:112 * COLS].rearrange("(p c) -> p c", c=COLS)).then_inc(S["dst_loaded"], 16)
            sp.dma_start(dsti[112:127, :], dst[112 * COLS:127 * COLS].rearrange("(p c) -> p c", c=COLS)).then_inc(S["dst_loaded"], 16)
            sp.dma_start(dsti[127:128, 0:LASTC], dst[127 * COLS:E].rearrange("(p c) -> p c", p=1)).then_inc(S["dst_loaded"], 16)
            sp.dma_start(wraw[0:112, :], edge_weight[0:112 * COLS].rearrange("(p c) -> p c", c=COLS)).then_inc(S["w_loaded"], 16)
            sp.dma_start(wraw[112:127, :], edge_weight[112 * COLS:127 * COLS].rearrange("(p c) -> p c", c=COLS)).then_inc(S["w_loaded"], 16)
            sp.dma_start(wraw[127:128, 0:LASTC], edge_weight[127 * COLS:E].rearrange("(p c) -> p c", p=1)).then_inc(S["w_loaded"], 16)
            sp.dma_start(acc[:, 0:NT - 1, :], x[0:(NT - 1) * P, :].rearrange("(t p) c -> p t c", p=P)).then_inc(S["x_loaded"], 16)
            sp.dma_start(acc[0:TAIL, NT - 1, :], x[(NT - 1) * P:N, :]).then_inc(S["x_loaded"], 16)
            sp.wait_ge(S["zero_rows"], 2)
            zr = NBLK * BW // (P * 512)
            for k in range(zr):
                sp.dma_start(rec[0:NBLK, :].rearrange("(k p a) w -> k p (a w)", k=zr, p=P)[k], zerof[:, :]).then_inc(S["zeroed"], 16)
            sp.dma_start(xg[0:1, :], zerof[0:1, 0:C]).then_inc(S["zeroed"], 16)
            sp.wait_ge(S["normed"], NT)
            sp.dma_start(xg[1:1 + (NT - 1) * P, :].rearrange("(t p) c -> p t c", p=P), xn[:, 0:NT - 1, :]).then_inc(S["xn_stored"], 16)
            sp.dma_start(xg[1 + (NT - 1) * P:N + 1, :], xn[0:TAIL, NT - 1, :]).then_inc(S["xn_stored"], 16)
            sp.wait_ge(S["bucket_ready"], 1)
            sp.dma_start(bucket_dram, gbucki[:, :]).then_inc(S["bucket_stored"], 16)
            sp.wait_ge(S["bucket_stored"], 16)
            sp.dma_start(group_bucket[0:1, :], bucket_dram.rearrange("p q -> (p q)").rearrange("(a n) -> a n", a=1)).then_inc(S["bucket_loaded"], 16)
            sp.wait_ge(S["local_sorted"], NSUP)
            sp.dma_start(raw_wx, W_x.rearrange("(k p) o -> p k o", p=P)).then_inc(S["wx_loaded"], 16)
            for g in range(NG8):
                sp.wait_ge(scattered[g], 16 * NSUP)
            recs = rec[0:NBLK, :].rearrange("(k p a) w -> k p (a w)", p=P, a=P // BLK)
            for k in range(NCHUNK // P):
                if k >= 2:
                    sp.wait_ge(S["transposed"], k - 1)
                sp.dma_start(back[:, k % 2, :], recs[k]).then_inc(loaded_back[k % 2], 16)
            sp.wait_ge(S["dest_ready"], NSUP)
            sp.dma_start(wfx, W_fx.rearrange("(k p) o -> p k o", p=P)).then_inc(S["rows_loaded"], 16)
            for n, v in enumerate((ln1_g, ln1_b, ln2_g, ln2_b)):
                sp.dma_start(rows[:, n, :], v.rearrange("(a c) -> a c", a=1).broadcast_to([P, C])).then_inc(S["rows_loaded"], 16)
            for h in range(2):
                sp.dma_start(wslice[h * D2:(h + 1) * D2, :], W_slice).then_inc(S["rows_loaded"], 16)
            for t, v in ((wq, W_q), (wk, W_k), (wv, W_v)):
                sp.dma_start(t, v).then_inc(S["rows_loaded"], 16)
            sp.dma_start(bxc, b_x.rearrange("(m p) -> p m", p=P), allow_slow_non_contiguous=True).then_inc(S["rows_loaded"], 16)
            sp.dma_start(b1c, b1.rearrange("(m p) -> p m", p=P), allow_slow_non_contiguous=True).then_inc(S["rows_loaded"], 16)
            sp.dma_start(rtemp, temperature.rearrange("a h b c -> (b c) (a h)").broadcast_to([P, 8])).then_inc(S["rows_loaded"], 16)
            sp.dma_start(bsl, b_slice.rearrange("(a c) -> a c", a=1).broadcast_to([3, D2])).then_inc(S["rows_loaded"], 16)
            sp.dma_start(bfx, b_fx.rearrange("(a c) -> a c", a=1)).then_inc(S["rows_loaded"], 16)
            sp.dma_start(biasf[:, 1, 0:C], b2.rearrange("(a c) -> a c", a=1).broadcast_to([3, C])).then_inc(S["rows_loaded"], 16)
            sp.dma_start(biasf[:, 1, C:2 * C], b_out.rearrange("(a c) -> a c", a=1).broadcast_to([3, C])).then_inc(S["rows_loaded"], 16)
            sp.wait_ge(S["third"], 3 * NT + 1)
            sp.dma_start(wout, W_out.rearrange("(h p) c -> p h c", p=D2)).then_inc(S["late_loaded"], 16)
            with sp.Fori(0, NT // 4) as i:
                sp.wait_ge(S["out_sum"], 4 * i + 8)
                sp.sem_inc(S["pace_sp"], 1)
                sp.dma_start(out[ds(i * 4 * P, 4 * P), :].rearrange("(t p) c -> p t c", p=P), acc[:, ds(i * 4, 4), :]).then_inc(S["out_stored"], 16)
            sp.wait_ge(S["out_sum"], NT + 4)
            sp.dma_start(out[(NT - 1) * P:N, :], acc[0:TAIL, NT - 1, :]).then_inc(S["out_stored"], 16)
            sp.wait_ge(S["out_stored"], 16 * (NT // 4 + 1))

        @block.gpsimd
        def _(pool):
            def seen(s, v):
                pool.wait_ge(s, v)
                pool.sem_inc(S["pace"], 1)
            pool.memset(identf[:, :], 0.0).then_inc(S["consts"], 1)
            pool.memset(identb[:, :], 0.0).then_inc(S["consts"], 1)
            pool.memset(onesb[:, :], 1.0).then_inc(S["consts"], 1)
            pool.memset(zerob[:, :], 0.0).then_inc(S["consts"], 1)
            pool.memset(zerof[:, :], 0.0).then_inc(S["zero_rows"], 2)
            pool.iota(iota[:, :], pattern=[[1, P]], base=0, channel_multiplier=0, allow_small_or_imprecise_dtypes=True).then_inc(S["consts"], 1)
            pool.iota(block_no[:, :], pattern=[[P, NG8]], base=0, channel_multiplier=1, allow_small_or_imprecise_dtypes=True).then_inc(S["consts"], 1)
            pool.iota(group_no[:, :], pattern=[[GRP, NGRP // P]], base=0, channel_multiplier=GRP * (NGRP // P), allow_small_or_imprecise_dtypes=True).then_inc(S["consts"], 1)
            pool.wait_ge(S["consts"], 7)
            pool.affine_select(out=identf[:, :], in_=identf[:, :], compare_op=ALU.not_equal, fill=1.0, base=0, pattern=[[-1, P]], channel_multiplier=1).then_inc(S["consts"], 1)
            pool.affine_select(out=identb[:, :], in_=identb[:, :], compare_op=ALU.not_equal, fill=1.0, base=0, pattern=[[-1, P]], channel_multiplier=1).then_inc(S["consts"], 1)
            pool.affine_select(out=before[:, :], in_=onesb[:, :], compare_op=ALU.is_gt, fill=0.0, base=0, pattern=[[1, P]], channel_multiplier=-1).then_inc(S["consts"], 1)
            pool.wait_ge(S["zeroed"], 16 * (NBLK * BW // (P * 512) + 1))
            with pool.Fori(0, NSUP) as i:
                pool.wait_ge(S["dest_ready"], i + 1)
                seen(S["local_copied"], i + 2)
                for g in range(NG8):
                    pool.indirect_dma_start(rec, bass.IndirectOffsetOnAxis(ap=dest[:, g:g + 1], axis=0), local[:, g * BW:(g + 1) * BW], None).then_inc(scattered[g], 16)
                for g in range(NG8):
                    pool.wait_ge(scattered[g], 16 * i + 16)
                pool.sem_inc(S["scatter_done"], 1)
            pool.wait_ge(S["xn_stored"], 32)
            pool.wait_ge(S["unpacked"], NCHUNK // P)

            PAIRS = NCHUNK // (2 * RING)
            with pool.Fori(0, PAIRS) as i:
                for h in range(2):
                    pool.tensor_copy(iring[:, h, :], gidx[:, ds((2 * i + h) * RING, RING)]).then_inc(S["ring_ready"], 1)
                    seen(S["ring_ready"], 2 * i + h + 1)
                    for j in range(RING):
                        seen(S["multiplied"], (2 * i + h) * RING + j + 1)
                        pool.indirect_dma_start(gath[:, j, :], None, xg, bass.IndirectOffsetOnAxis(ap=iring[:, h, j:j + 1], axis=0)).then_inc(gathered[j], 16)
            for k in range(2 * PAIRS, (NCHUNK + RING - 1) // RING):
                count = min(RING, NCHUNK - k * RING)
                pool.tensor_copy(iring[:, k % 2, 0:count], gidx[:, k * RING:k * RING + count]).then_inc(S["ring_ready"], 1)
                pool.wait_ge(S["ring_ready"], k + 1)
                for j in range(count):
                    pool.wait_ge(S["multiplied"], k * RING + j + 1)
                    pool.sem_inc(S["pace"], 1)
                    pool.indirect_dma_start(gath[:, j, :], None, xg, bass.IndirectOffsetOnAxis(ap=iring[:, k % 2, j:j + 1], axis=0)).then_inc(gathered[j], 16)

            def weigh(t, h):
                if live(t, 1):
                    seen(S["f_sum"], t)
                    k = (h - 1) % 4
                    pool.tensor_tensor(slices[:, k, :].rearrange("p (n g) -> p n g", g=D2), slices[:, k, :].rearrange("p (n g) -> p n g", g=D2), wide(fsum[:, k, :], [P, 8, D2], 2), ALU.mult).then_inc(S["f_slice"], 1)
            pipeline(pool, weigh)

        @block.scalar
        def _(act):
            def seen(s, v):
                act.wait_ge(s, v)
                act.sem_inc(S["pace_act"], 1)
            for k in range(10):
                act.wait_ge(S["trans_ps"], k + 1)
                to = wqkvT[:, :, k * P:(k + 1) * P] if k < 6 else (w1T if k < 8 else w2T)[:, :, k % 2 * P:k % 2 * P + P]
                act.copy(to, ps[:, 6 + k % 2, 0:2 * P].rearrange("p (k o) -> p k o", k=2)).then_inc(S["trans_sb"], 1)
            with act.Fori(0, NT) as b:
                seen(S["scan_ready"], b + 1)
                act.copy(cnt[:, ds(b, 1), :], running[:, SUPC - 1::SUPC].rearrange("p (a s) -> p a s", a=1)).then_inc(S["count_copied"], 1)
            act.wait_ge(S["var_ready"], 1)
            act.activation(rstd[:, :], rstd[:, :], ACT.Sqrt).then_inc(S["rstd_root"], 1)
            with act.Fori(0, NSUP) as i:
                act.wait_ge(S["scatter_done"], i + 1)
                seen(S["local_sorted"], i + 1)
                act.copy(local[:, :], ps[:, 7, 0:P]).then_inc(S["local_copied"], 1)
            for k in range(NCHUNK // P):
                act.wait_ge(S["transposed"], k + 1)
                act.copy(sw[:, k * P:(k + 1) * P], ps[:, 6 + k % 2, 0:P]).then_inc(S["w_copied"], 1)

            for m in range(4):
                act.wait_ge(S["wxT_ps"], m + 1)
                act.copy(wxT[:, m, :], ps[:, 2 + m % 2, 0:C]).then_inc(S["wxT_sb"], 1)

            tile = lambda a, t: a[:, ds(t, 1), :].rearrange("p a c -> p (a c)")

            def stage(n, t):
                seen(S["xt_ps"], n + 1)
                act.copy(xcur, tile(xn, t)).then_inc(S["cur_sb"], 1)

            def copy_xT(n):
                act.wait_ge(S["proj"], n + 1)
                seen(S["xt_ps"], n + 2)
                act.copy(xT[:, :, :], ps[:, 2, 0:C].rearrange("p (k t) -> p k t", k=2)).then_inc(S["xt_sb"], 1)

            def grow(n):
                seen(S["feat_low"], n + 1)
                act.activation(grown, low, ACT.Exp).then_inc(S["feat_exp"], 1)

            act.wait_ge(S["wc_ps"], 1)
            act.wait_ge(S["vone_set"], 1)
            with act.Fori(0, NT) as t:
                stage(t, t)
                copy_xT(t)
                act.wait_ge(S["third"], t + 1)
                seen(S["proj"], t + 2)
                act.copy(vone[:, :, 0:P], ps[:, 6, 0:C].rearrange("p (g m) -> p g m", g=2)).then_inc(S["v_sb"], 1)
                grow(t)
            with act.Fori(0, NT) as t:
                stage(t + NT, t)
                copy_xT(t + NT)
                grow(t + NT)
            act.wait_ge(S["var_ready"], 2)
            act.activation(rstd[:, :], rstd[:, :], ACT.Sqrt).then_inc(S["rstd_root"], 1)
            with act.Fori(0, NT) as t:
                n = t + 2 * NT
                act.wait_ge(S["mixed"], t + 1)
                stage(n, t)
                copy_xT(n)
                act.wait_ge(S["third"], n + 1)
                seen(S["proj"], n + 2)
                act.activation(feat[:, 0:P], ps[:, 3, 0:P], ACT.Gelu, bias=b1c[:, 0:1])
                act.activation(feat[:, P:2 * P], ps[:, 3, P:2 * P], ACT.Gelu, bias=b1c[:, 1:2]).then_inc(S["feat_ready"], 1)
                seen(S["row_var"], t + 1)
                act.activation(root, spread, ACT.Sqrt).then_inc(S["row_root"], 1)
            act.wait_ge(S["var_ready"], 3)
            act.activation(rstd[:, :], rstd[:, :], ACT.Sqrt).then_inc(S["rstd_root"], 1)

            def ffn_step(t, h):
                if live(t, 0):
                    if live(t, 1):
                        act.wait_ge(S["f_logit"], t)
                    seen(S["f_xT"], t + 1)
                    act.copy(xsT[:, :, :], ps[:, 2, 0:C].rearrange("p (k t) -> p k t", k=2)).then_inc(S["f_xsT"], 1)
                if live(t, 1):
                    seen(S["f_low"], t)
                    k = (h - 1) % 4
                    act.activation(slices[:, k, :], slices[:, k, :], ACT.Exp).then_inc(S["f_exp"], 1)
                if live(t, 2):
                    seen(S["f_pair"], t + 1)
                    act.copy(sliceT[:, :, ds((t - 2) * P, P)], ps[:, 3, 0:INNER].rearrange("p (m t) -> p m t", m=4)).then_inc(S["f_sTsb"], 1)
            pipeline(act, ffn_step)
            act.wait_ge(S["tok_sb"], 9)
            act.activation(att, att, ACT.Exp, scale=D2 ** -0.5).then_inc(S["tok_sb"], 1)
            act.wait_ge(S["tok_sb"], 14)

            def stage_slices(t, h):
                act.copy(slcur[:, h, :, :], sliceT[:, :, ds(t * P, P)]).then_inc(S["sl_sb"], 1)
            with act.Fori(0, NT // 4) as i:
                for h in range(4):
                    seen(S["out_ps"], 4 * i + h + 1)
                    stage_slices(4 * i + h, h)
            seen(S["out_ps"], NT)
            stage_slices(NT - 1, 0)

        def split_bias(step, to, frm, width):
            dve = nc.vector
            hi, rest, mid = biasf[:, 0, 0:width], biasf[:, 2, 0:width], frm
            step(dve.tensor_copy(to[:, 0:width], frm))
            step(dve.tensor_copy(hi, to[:, 0:width]))
            step(dve.tensor_tensor(rest, frm, hi, ALU.subtract))
            step(dve.tensor_copy(to[:, 0:width], rest))
            step(dve.tensor_copy(mid, to[:, 0:width]))
            step(dve.tensor_tensor(rest, rest, mid, ALU.subtract))
            step(dve.tensor_scalar(hi, hi, identf[0:3, 0:1], None, ALU.mult))
            step(dve.scalar_tensor_tensor(hi, mid, identf[0:3, 1:2], hi, ALU.mult, ALU.add))
            step(dve.scalar_tensor_tensor(to[:, 0:width], rest, identf[0:3, 2:3], hi, ALU.mult, ALU.add))

        def var_of_stats(step):
            dve = nc.vector
            step(dve.tensor_tensor(mean[:, :], stats[:, :, 1], stats[:, :, 4], ALU.add))
            step(dve.tensor_scalar(mean[:, :], mean[:, :], 0.5, None, ALU.mult))
            step(dve.tensor_tensor(half[:, :], mean[:, :], stats[:, :, 1], ALU.subtract))
            step(dve.tensor_tensor(half[:, :], half[:, :], half[:, :], ALU.mult))
            step(dve.tensor_tensor(rstd[:, :], stats[:, :, 2], stats[:, :, 5], ALU.add))
            step(dve.scalar_tensor_tensor(rstd[:, :], rstd[:, :], 1.0 / C, half[:, :], ALU.mult, ALU.add))
            step(dve.tensor_scalar(rstd[:, :], rstd[:, :], 1e-5, None, ALU.add))

        @block.vector
        def _(dve):
            step = Steps(dve, S["step_dve"])
            dve.memset(srci[96:P, LASTC:COLS], NT * P).then_inc(S["pad_set"], 1)
            dve.memset(dsti[96:P, LASTC:COLS], -1).then_inc(S["pad_set"], 1)
            dve.memset(wraw[96:P, LASTC:COLS], 0.0).then_inc(S["pad_set"], 1)
            dve.memset(acc[96:P, NT - 1, :], 0.0).then_inc(S["pad_set"], 1)
            step(dve.memset(restart[:, :, :], 1.0))
            step(dve.memset(restart[:, :, 0:1], 0.0))
            dve.memset(rstb[:, :, :], 1.0)
            step(dve.memset(rsts[:, :, :], 1.0))
            dve.memset(rstb[:, :, 0:1], 0.0)
            step(dve.memset(rsts[:, :, 0:1], 0.0))
            dve.memset(gone[:, :], 1.0)
            dve.memset(slo[:, NCHUNK:], 0.0)
            dve.memset(sw[:, NCHUNK:], 0.0)
            step(dve.memset(nbs[:, :, :], 0.0))
            dve.wait_ge(S["consts"], 10)
            dve.wait_ge(S["src_loaded"], 48)
            dve.wait_ge(S["dst_loaded"], 48)
            dve.wait_ge(S["w_loaded"], 48)
            step(dve.tensor_scalar(loi[:, :], srci[:, :], 7, None, ALU.logical_shift_right))
            step(dve.tensor_copy(bucket[:, :], loi[:, :]))
            step(dve.tensor_scalar(loi[:, :], srci[:, :], P - 1, None, ALU.bitwise_and))
            step(dve.tensor_scalar(base_float[:, :], dsti[:, :], 1.0, float(P), ALU.add, ALU.mult))
            dve.tensor_tensor(vals[:, :, 0], base_float[:, :], loi[:, :], ALU.add)
            step(dve.tensor_copy(vals[:, :, 1], wraw[:, :]))

            def find(b, h):
                dve.tensor_scalar(mask[h][:, :], bucket[:, :], iota[:, ds(b, 1)], None, ALU.is_equal).then_inc(S["masked"], 1)

            def count(b, h, more):
                dve.wait_ge(S["masked"], b + 1)
                dve.wait_ge(S["prod_ready"], b + 1)
                dve.wait_ge(S["count_copied"], b + 1)
                dve.tensor_tensor_scan(running[:, :], restart[:, :, :].rearrange("p s c -> p (s c)"), mask[h][:, :], 0.0, ALU.mult, ALU.add).then_inc(S["scan_ready"], 1)
                if more:
                    find(b + 1, 1 - h)
                dve.wait_ge(S["scan_ready"], b + 1)
                dve.wait_ge(S["prod_used"], b + 1)
                dve.tensor_tensor(ranked[h][:, :], running[:, :], mask[h][:, :], ALU.mult).then_inc(S["prod_ready"], 1)
            dve.sem_inc(S["prod_used"], 1)
            dve.sem_inc(S["prod_ready"], 1)
            find(0, 0)
            with dve.Fori(0, NT // 2) as i:
                for h in range(2):
                    count(2 * i + h, h, True)
            count(NT - 1, 0, False)
            dve.wait_ge(S["prod_used"], NT + 2)
            dve.wait_ge(S["zeroed"], 16 * (NBLK * BW // (P * 512) + 1))
            dve.wait_ge(S["trans_ps"], 10)
            dve.wait_ge(S["count_sums"], 1)
            step(dve.tensor_copy(base[:, :, :].rearrange("p b s -> p (b s)").rearrange("p (k c) -> p k c", k=3), ps[:, 4:7, 0:CW]))
            dve.engine_nop().then_inc(S["sums_read"], 1)
            dve.wait_ge(S["count_sums"], 2)
            step(dve.tensor_scalar(tabi[:, :].rearrange("p (k c) -> p k c", k=3), ps[:, 4:7, 0:CW], float(BLK - 1), None, ALU.add))
            step(dve.tensor_scalar(tabi[:, :], tabi[:, :], 3, None, ALU.logical_shift_right))
            step(dve.tensor_copy(nb[:, :, :].rearrange("p b s -> p (b s)"), tabi[:, :]))
            step(dve.tensor_copy(nbs[:, :, 0:NT].rearrange("p s b -> p b s"), nb[:, :, :]))
            flat = lambda t: t[:, :, :].rearrange("p a b -> p (a b)")
            step(dve.tensor_tensor_scan(flat(lstart), flat(rstb), flat(nbs), 0.0, ALU.mult, ALU.add))
            step(dve.tensor_tensor(flat(lstart), flat(lstart), flat(nbs), ALU.subtract))
            step(dve.tensor_tensor_scan(flat(ginc), flat(rsts), flat(nb), 0.0, ALU.mult, ALU.add))
            step(dve.tensor_tensor(flat(gex), flat(ginc), flat(nb), ALU.subtract))
            step(dve.tensor_scalar(gi[:, :], ginc[:, :, NSUP - 1], float(GRP - 1), None, ALU.add))
            step(dve.tensor_scalar(gi[:, :], gi[:, :], 5, 5, ALU.logical_shift_right, ALU.logical_shift_left))
            step(dve.tensor_copy(gn[:, :], gi[:, :]))
            step(dve.tensor_tensor_scan(gst[:, :], gone[:, :], gn[:, :], 0.0, ALU.mult, ALU.add))
            step(dve.tensor_tensor(gst[:, :], gst[:, :], gn[:, :], ALU.subtract))
            step(dve.tensor_tensor(gex[:, :, :], gex[:, :, :], gst[:, :].rearrange("p (b s) -> p b s", s=1).broadcast_to([P, NT, NSUP]), ALU.add))
            step(dve.tensor_tensor(delta[:, :, 0:NT].rearrange("p s b -> p b s"), gex[:, :, :], lstart[:, :, 0:NT].rearrange("p s b -> p b s"), ALU.subtract))
            step(dve.tensor_scalar(delta[:, :, NT], iota[:, 0:NSUP], float(NG8 * P), float(TRASH), ALU.mult, ALU.add))
            step(dve.tensor_tensor(jump[:, :, 1:NT + 1], delta[:, :, 1:NT + 1], delta[:, :, 0:NT], ALU.subtract))
            step(dve.tensor_copy(jump[:, :, 0:1], delta[:, :, 0:1]))
            step(dve.scalar_tensor_tensor(base[:, :, :], lstart[:, :, 0:NT].rearrange("p s b -> p b s"), float(BLK), base[:, :, :], ALU.mult, ALU.add))
            step(dve.tensor_copy(tabi[:, :], flat(base)))
            step(dve.tensor_scalar(nbi[:, :], tabi[:, :], 7, 7, ALU.logical_shift_right, ALU.logical_shift_left))
            step(dve.tensor_copy(base_part[0], nbi[:, :].rearrange("p (b s) -> p b s", b=NT)[:, :, WHOLE:]))
            step(dve.tensor_scalar(nbi[:, :], tabi[:, :], P - 1, None, ALU.bitwise_and))
            step(dve.tensor_copy(base_part[1], nbi[:, :].rearrange("p (b s) -> p b s", b=NT)[:, :, WHOLE:]))
            step(dve.tensor_tensor(gmat[:, :, :], group_no[:, :].rearrange("p (q b) -> p q b", b=1).broadcast_to([P, NGRP // P, NT]), gst[:, :].rearrange("p (q b) -> p q b", q=1).broadcast_to([P, NGRP // P, NT]), ALU.is_ge))
            step(dve.tensor_reduce(gbuck[:, :], gmat[:, :, :], AX.X, ALU.add))
            dve.tensor_scalar(gbucki[:, :], gbuck[:, :], 1.0, None, ALU.subtract).then_inc(S["bucket_ready"], 1)
            by_super = lambda a: a.rearrange("p (s c) -> p s c", c=SUPC)

            def add_base(b, h):
                dve.wait_ge(S["based_used"], b + 1)
                for n in range(2):
                    cols = slice(WHOLE * SUPC, COLS)
                    dve.scalar_tensor_tensor(by_super(based_part[h][:, n, :]), by_super(bucket[:, cols]), iota[:, ds(b, 1)], base_part[n][:, ds(b, 1), :].rearrange("p a s -> p s a").broadcast_to([P, NSUP - WHOLE, SUPC]), ALU.is_equal, ALU.mult)
                dve.scalar_tensor_tensor(by_super(based[h]), by_super(bucket[:, 0:WHOLE * SUPC]), iota[:, ds(b, 1)], base[:, ds(b, 1), 0:WHOLE].rearrange("p a s -> p s a").broadcast_to([P, WHOLE, SUPC]), ALU.is_equal, ALU.mult).then_inc(S["based_ready"], 1)
            dve.sem_inc(S["based_used"], 1)
            with dve.Fori(0, NT // 2) as i:
                for h in range(2):
                    add_base(2 * i + h, h)
            add_base(NT - 1, 0)
            dve.wait_ge(S["based_used"], NT + 3)
            for k, c0, c1 in BANKS:
                last = dve.tensor_scalar(posi[:, c0:c1], ps[:, k, 0:c1 - c0], 1.0, None, ALU.subtract)
            step(last)
            step(dve.tensor_scalar(loi[:, :], posi[:, :], 3, P - 1, ALU.logical_shift_right, ALU.bitwise_and))
            step(dve.tensor_copy(slotp[:, :], loi[:, :]))
            step(dve.tensor_scalar(loi[:, :], posi[:, :], 10, 3, ALU.logical_shift_right, ALU.logical_shift_left))
            step(dve.tensor_scalar(dsti[:, :], posi[:, :], BLK - 1, None, ALU.bitwise_and))
            step(dve.tensor_tensor(loi[:, :], loi[:, :], dsti[:, :], ALU.bitwise_or))
            step(dve.tensor_copy(slotc[:, :], loi[:, :]))
            dve.wait_ge(S["x_loaded"], 32)
            tile = lambda a, t: a[:, ds(t, 1), :].rearrange("p a c -> p (a c)")
            with dve.Fori(0, NT) as t:
                dve.bn_stats(tile(stats, t), tile(acc, t)).then_inc(S["row_stats"], 1)
            dve.wait_ge(S["row_stats"], NT)
            var_of_stats(step)
            dve.wait_ge(S["x_loaded"], 32)
            dve.engine_nop().then_inc(S["var_ready"], 1)
            dve.wait_ge(S["rstd_root"], 1)
            step(dve.reciprocal(rstd[:, :], rstd[:, :]))
            with dve.Fori(0, NT) as t:
                dve.tensor_scalar(xn[:, ds(t, 1), :], acc[:, ds(t, 1), :], mean[:, ds(t, 1)], rstd[:, ds(t, 1)], ALU.subtract, ALU.mult).then_inc(S["normed"], 1)
            step.freeze()
            with dve.Fori(0, NSUP) as i:
                with dve.Fori(0, NBAT // 2) as j:
                    for h in range(2):
                        q = i * NBAT + j * 2 + h
                        c = ds(i * SUPC + j * (2 * BAT) + h * BAT, BAT)
                        dve.wait_ge(S["sorted_batches"], q + 1)
                        dve.tensor_tensor(hot_part[:, h, :, :], wide(iota[:, :], [P, BAT, P], 1), wide(slotp[:, c], [P, BAT, P], 2), ALU.is_equal)
                        dve.wait_ge(S["pair_ready"], q + 1)
                        dve.tensor_tensor(hot_col[:, :, :], wide(iota[:, 0:64], [P, BAT, 64], 1), wide(slotc[:, c], [P, BAT, 64], 2), ALU.is_equal).then_inc(S["col_hot"], 1)
                        dve.wait_ge(S["col_hot"], q + 1)
                        dve.tensor_tensor(hot_rec[:, h, :, :, :], wide(hot_col[:, :, :], [P, BAT, 64, REC], 3), wide(vals[:, c, :], [P, BAT, 64, REC], 2), ALU.mult).then_inc(S["pair_ready"], 1)
                dve.wait_ge(S["scatter_done"], i + 1)
                step.loop(i, 3)
                shape = [P, NG8, NT + 1]
                step(dve.tensor_tensor(passed[:, :, :], block_no[:, :].rearrange("p (g b) -> p g b", b=1).broadcast_to(shape), lstart[:, ds(i, 1), :].broadcast_to(shape), ALU.is_ge))
                step(dve.tensor_tensor(passed[:, :, :], passed[:, :, :], jump[:, ds(i, 1), :].broadcast_to(shape), ALU.mult))
                step(dve.tensor_reduce(moved[:, :], passed[:, :, :], AX.X, ALU.add))
                dve.tensor_tensor(dest[:, :], moved[:, :], block_no[:, :], ALU.add).then_inc(S["dest_ready"], 1)
            step.leave(NSUP)
            for k in range(NCHUNK // P):
                dve.wait_ge(S["transposed"], k + 1)
                step(dve.tensor_copy(geti[:, :], ps[:, 4 + k % 2, 0:P]))
                step(dve.tensor_scalar(getl[:, :], geti[:, :], P - 1, None, ALU.bitwise_and))
                dve.tensor_scalar(gidx[:, k * P:(k + 1) * P], geti[:, :], 7, None, ALU.logical_shift_right)
                step(dve.tensor_copy(slo[:, k * P:(k + 1) * P], getl[:, :]))
                dve.engine_nop().then_inc(S["unpacked"], 1)
            step.freeze()
            dve.wait_ge(S["rows_loaded"], 16 * 17)
            step(dve.tensor_scalar(rtemp, rtemp, 0.1, 5.0, ALU.max, ALU.min))
            step(dve.reciprocal(rtemp, rtemp))
            dve.wait_ge(S["wc_ps"], 1)
            parity = lambda a, e: a.rearrange("p (m e g) -> p e m g", e=2, g=D2)[:, e]
            for e in range(2):
                for k in range(2):
                    dve.tensor_tensor(parity(wc[:, k, :], e), parity(ps[:, 2 + k + 2 * e, :], e), wide(rtemp.rearrange("p (m e) -> p e m", e=2)[:, e, :], [P, 4, D2], 2), ALU.mult)
            three = lambda a: a.rearrange("p (n g) -> p n g", g=D2)
            split_bias(step, bias2[:, :], biasf[:, 1, 0:C], C)
            split_bias(step, biaso[:, :], biasf[:, 1, C:2 * C], C)
            for e in range(2):
                step(dve.tensor_tensor(parity(biasf[:, 1, :], e), parity(ps[0:3, 6 + e, :], e), wide(bsl, [3, 4, D2], 1), ALU.add))
            step(dve.tensor_tensor(three(biasf[:, 1, :]), three(biasf[:, 1, :]), wide(rtemp[0:3, :], [3, 8, D2], 2), ALU.mult))
            split_bias(step, bias_logit[:, :], biasf[:, 1, :], INNER)
            step(dve.memset(vone[:, :, P:P + 1], 1.0))
            step(dve.memset(kvd[:, :, :], 0.0))
            dve.engine_nop().then_inc(S["vone_set"], 1)
            dve.engine_nop().then_inc(S["wc_sb"], 1)

            def low_part(n):
                dve.wait_ge(S["proj"], n + 2)
                dve.tensor_scalar(low, ps[:, 3, 0:C], 0.0, None, ALU.min).then_inc(S["feat_low"], 1)

            def high_part(n):
                dve.wait_ge(S["third"], n + 1)
                dve.wait_ge(S["feat_exp"], n + 1)
                dve.scalar_tensor_tensor(feat, ps[:, 3, 0:C], 0.0, grown, ALU.max, ALU.add).then_inc(S["feat_ready"], 1)

            tile = lambda a, t: a[:, ds(t, 1), :].rearrange("p a c -> p (a c)")
            dve.wait_ge(S["w_copied"], NCHUNK // P)
            dve.wait_ge(S["bucket_loaded"], 16)
            dve.sem_inc(S["added"], 2)

            def hot(q, u):
                dve.wait_ge(S["multiplied"], q + RING + 1 - HOT)
                dve.tensor_scalar(onehot[:, u, :], iota[:, :], slo[:, ds(q, 1)], sw[:, ds(q, 1)], ALU.is_equal, ALU.mult).then_inc(S["hot_ready"], 1)

            def buckets(n, count=STEP):
                return nc.values_load_multi_w_load_instructions(
                    group_bucket[0:1, ds(n * STEP, count)], engines=[mybir.EngineType.DVE], min_val=0, max_val=NT - 1,
                    skip_runtime_bounds_check_because="a count of NT comparisons less one, the first of which holds")[1]

            def groups(n, at, *js):
                for j in js:
                    g = n * STEP + j
                    for u in range(2):
                        hot(2 * g + 4 + u, (2 * j + 4 + u) % HOT)
                    b = at[j]
                    dve.wait_ge(S["multiplied"], RING + 2 * g + 2)
                    dve.wait_ge(S["added"], 2 + g)
                    dve.tensor_tensor(tile(acc, b), tile(acc, b), ps[:, j % 2, 0:C], ALU.add).then_inc(S["added"], 1)
            for q in range(4):
                hot(q, q)
            step.freeze()
            with dve.Fori(0, NT) as t:
                at = buckets(t)
                groups(t, at, 0, 1)
                low_part(t)
                groups(t, at, 2)
                high_part(t)
                groups(t, at, 3, 4, 5)
            dve.wait_ge(S["kv_done"], 1)
            for g in range(2):
                for h in range(4):
                    rr = slice(32 * h, 32 * h + 32)
                    dve.tensor_copy(kvd[rr, g, 32 * h:32 * h + 32], ps[rr, 4 + g, 32 * h:32 * h + 32])
                    last = dve.tensor_copy(kvd[rr, g, P + h:P + h + 1], ps[rr, 4 + g, P:P + 1])
            step(last)
            dve.engine_nop().then_inc(S["kv_diag"], 1)
            step.freeze()
            with dve.Fori(0, NT) as t:
                step.loop(t, 4)
                at = buckets(t + NT)
                groups(t + NT, at, 0, 1)
                low_part(t + NT)
                groups(t + NT, at, 2)
                high_part(t + NT)
                groups(t + NT, at, 3, 4)
                dve.wait_ge(S["third"], t + NT + 2)
                heads = ps[:, 6:8, 0:132]
                step(dve.tensor_scalar(zden, heads[:, :, P:P + 4], 1e-6, None, ALU.add))
                step(dve.reciprocal(zden, zden))
                dve.tensor_tensor(tmp.rearrange("p (g h m) -> p g h m", g=2, h=4), heads[:, :, 0:P].rearrange("p g (h m) -> p g h m", h=4), wide(zden, [P, 2, 4, 32], 3), ALU.mult).then_inc(S["res"], 1)
                dve.wait_ge(S["res"], t + 2)
                step(dve.tensor_tensor(tile(xn, t), tmp, tile(xn, t), ALU.add))
                step(dve.bn_stats(tile(stats, t), tile(xn, t)))
                groups(t + NT, at, 5)
            step.leave(NT)
            var_of_stats(step)
            dve.engine_nop().then_inc(S["var_ready"], 1)
            dve.wait_ge(S["rstd_root"], 2)
            step(dve.reciprocal(rstd[:, :], rstd[:, :]))

            def affine(t, n, to, center, scale):
                step(dve.scalar_tensor_tensor(tmp, tile(xn, t), center, rows[:, n, :], ALU.subtract, ALU.mult))
                return dve.scalar_tensor_tensor(to, tmp, scale, rows[:, n + 1, :], ALU.mult, ALU.add)
            step.freeze()
            def second(t):
                affine(t, 0, tile(xn, t), mean[:, ds(t, 1)], rstd[:, ds(t, 1)]).then_inc(S["mixed"], 1)

            def last_norm(t, more):
                n = t + 2 * NT
                at = buckets(n)
                groups(n, at, 0, 1, 2)
                if more:
                    second(t + 1)
                groups(n, at, 3)
                dve.wait_ge(S["third"], n + 2)
                dve.tensor_tensor(tile(xn, t), ps[:, 6, 0:C], tile(xn, t), ALU.add).then_inc(S["res"], 1)
                dve.wait_ge(S["res"], NT + t + 2)
                step(dve.bn_stats(tile(stats, t), tile(xn, t)))
                col = lambda k: tile(stats, t)[:, k:k + 1]
                step(dve.tensor_tensor(middle, col(1), col(4), ALU.add))
                step(dve.tensor_scalar(middle, middle, 0.5, None, ALU.mult))
                step(dve.tensor_tensor(off, middle, col(1), ALU.subtract))
                step(dve.tensor_tensor(off, off, off, ALU.mult))
                step(dve.tensor_tensor(spread, col(2), col(5), ALU.add))
                step(dve.scalar_tensor_tensor(spread, spread, 1.0 / C, off, ALU.mult, ALU.add))
                dve.tensor_scalar(spread, spread, 1e-5, None, ALU.add).then_inc(S["row_var"], 1)
                groups(n, at, 4)
                dve.wait_ge(S["row_root"], t + 1)
                step(dve.reciprocal(root, root))
                step(affine(t, 2, tile(xn, t), middle, root))
                groups(n, at, 5)
                dve.wait_ge(S["added"], 2 + n * STEP + STEP)
                step(dve.tensor_tensor(tile(acc, t), tile(acc, t), tile(xn, t), ALU.add))
            second(0)
            step.freeze()
            with dve.Fori(0, NT - 1) as t:
                step.loop(t, 12)
                last_norm(t, True)
            step.leave(NT - 1)
            last_norm(NT - 1, False)
            step.freeze()
            for k in range((REST + RING - 1) // RING):
                count = min(STEP, REST // 2 - k * STEP)
                groups(3 * NT + k, buckets(3 * NT + k, count), *range(count))
            dve.wait_ge(S["added"], 2 + NGRP)
            with dve.Fori(0, NT) as t:
                dve.bn_stats(tile(stats, t), tile(acc, t)).then_inc(S["row_stats"], 1)
            dve.wait_ge(S["row_stats"], 2 * NT)
            var_of_stats(step)
            dve.engine_nop().then_inc(S["var_ready"], 1)
            dve.wait_ge(S["rstd_root"], 3)
            step(dve.reciprocal(rstd[:, :], rstd[:, :]))
            step(dve.memset(xs[:, :, C:C + 1], 1.0))

            def normed(t, h):
                dve.tensor_scalar(xs[:, h, 0:C], tile(acc, t), mean[:, ds(t, 1)], rstd[:, ds(t, 1)], ALU.subtract, ALU.mult).then_inc(S["f_norm"], 1)

            def soften(t, h):
                if live(t, 1):
                    k = (h - 1) % 4
                    dve.wait_ge(S["f_exp"], t + 1)
                    step(dve.tensor_reduce(fsum[:, k, :], three(slices[:, k, :]), AX.X, ALU.add))
                    dve.reciprocal(fsum[:, k, :], fsum[:, k, :]).then_inc(S["f_sum"], 1)
                if live(t, 0):
                    dve.wait_ge(S["f_logit"], t + 1)
                    step(dve.tensor_reduce(fmax[:, h % 2, :], three(ps[:, h % 2, :]), AX.X, ALU.max))
                    dve.tensor_tensor(three(slices[:, h, :]), three(ps[:, h % 2, :]), wide(fmax[:, h % 2, :], [P, 8, D2], 2), ALU.subtract).then_inc(S["f_low"], 1)
                if live(t, -2):
                    if live(t, 2):
                        dve.wait_ge(S["f_pair"], t + 1)
                    normed(t + 2, (h + 2) % 4)
            step.freeze()
            normed(0, 0)
            normed(1, 1)
            pipeline(dve, soften, step, 2)
            dve.wait_ge(S["tok_ps"], 1)
            step(dve.tensor_scalar(tden, ps[:, 4:8, C], 1e-5, None, ALU.add))
            step(dve.reciprocal(tden, tden))
            step(dve.tensor_tensor(token[:, :, :], ps[:, 4:8, 0:C + 1], wide(tden, [P, 4, C + 1], 2), ALU.mult))
            dve.engine_nop().then_inc(S["tok_sb"], 1)
            dve.wait_ge(S["tok_ps"], 2)
            dve.tensor_copy(tokenT[:, 0, :], ps[:, 0, :])
            dve.tensor_copy(tokenT[:, 1, :], ps[:, 1, :])
            step(dve.tensor_copy(ratio, ps[0:1, 2, :]))
            dve.engine_nop().then_inc(S["tok_sb"], 1)
            dve.wait_ge(S["tok_ps"], 3)
            step(dve.tensor_copy(tokf, ps[0:D2, 3, :]))
            dve.engine_nop().then_inc(S["tok_sb"], 1)
            dve.wait_ge(S["tok_ps"], 4)
            dve.tensor_copy(qk[:, 0, :], ps[0:D2, 0, :])
            dve.tensor_copy(qk[:, 1, :], ps[0:D2, 1, :])
            step(dve.tensor_copy(vtok, ps[0:D2, 2, :]))
            dve.engine_nop().then_inc(S["tok_sb"], 1)
            dve.wait_ge(S["tok_ps"], 5)
            step(dve.tensor_reduce(amax, three(ps[0:D2, 3, :]), AX.X, ALU.max))
            step(dve.tensor_tensor(three(att), three(ps[0:D2, 3, :]), wide(amax, [D2, 8, D2], 2), ALU.subtract))
            for k in range(5):
                dve.engine_nop().then_inc(S["tok_sb"], 1)
            dve.wait_ge(S["tok_sb"], 10)
            step(dve.tensor_reduce(asum, three(att), AX.X, ALU.add))
            step(dve.reciprocal(asum, asum))
            step(dve.tensor_tensor(three(att), three(att), wide(asum, [D2, 8, D2], 2), ALU.mult))
            dve.engine_nop().then_inc(S["tok_sb"], 1)
            dve.wait_ge(S["tok_ps"], 6)
            step(dve.tensor_copy(attT, ps[0:D2, 0, :]))
            dve.engine_nop().then_inc(S["tok_sb"], 1)
            dve.wait_ge(S["tok_ps"], 7)
            step(dve.tensor_copy(outT, ps[0:D2, 1, :]))
            dve.engine_nop().then_inc(S["tok_sb"], 1)
            dve.wait_ge(S["tok_ps"], 8)
            for m in range(4):
                last = dve.tensor_copy(mout[:, m, :], ps[:, 4 + m, 0:C])
            step(last)
            dve.engine_nop().then_inc(S["tok_sb"], 1)

            def add_out(t, h):
                dve.wait_ge(S["out_ps"], t + 5)
                dve.tensor_tensor(tile(acc, t), tile(acc, t), ps[:, h, 0:C], ALU.add).then_inc(S["out_sum"], 1)
            with dve.Fori(0, NT // 4) as i:
                for h in range(4):
                    add_out(4 * i + h, h)
            add_out(NT - 1, 0)

        @block.tensor
        def _(pe):
            def seen(s, v):
                pe.wait_ge(s, v)
                pe.sem_inc(S["pace_pe"], 1)
            pe.wait_ge(S["consts"], 10)
            mm = pe.matmul
            for k in range(QN):
                mm(ps[:, k, 0:QW], zerob[:, 0:P], zerob[:, :], start=True, stop=False)
            pe.wait_ge(S["raw_loaded"], 48)
            for k in range(10):
                raw = raw_qkv[:, k, :] if k < 6 else (raw_w1 if k < 8 else raw_w2)[:, k % 2, :]
                if k >= 2:
                    pe.wait_ge(S["trans_sb"], k - 1)
                for c in range(2):
                    last = pe.transpose(ps[:, 6 + k % 2, c * P:(c + 1) * P], raw[:, c * P:(c + 1) * P], identf[:, :])
                last.then_inc(S["trans_ps"], 1)
            pe.wait_ge(S["trans_sb"], 10)

            def add_ranks(b, h):
                seen(S["prod_ready"], b + 2)
                for k, c0, c1 in BANKS:
                    last = mm(ps[:, k, 0:c1 - c0], identb[:, :], ranked[h][:, c0:c1], start=False, stop=False)
                last.then_inc(S["prod_used"], 1)
            with pe.Fori(0, NT // 2) as i:
                for h in range(2):
                    add_ranks(2 * i + h, h)
            add_ranks(NT - 1, 0)
            pe.wait_ge(S["count_copied"], NT + 1)
            flat = cnt[:, :, :].rearrange("p b s -> p (b s)")
            for k in range(3):
                last = mm(ps[:, 4 + k, 0:CW], before[:, :], flat[:, k * CW:(k + 1) * CW], start=True, stop=True)
            last.then_inc(S["count_sums"], 1)
            pe.wait_ge(S["sums_read"], 1)
            for k in range(3):
                last = mm(ps[:, 4 + k, 0:CW], onesb[:, :], flat[:, k * CW:(k + 1) * CW], start=True, stop=True)
            last.then_inc(S["count_sums"], 1)

            def add_bases(b, h):
                seen(S["based_ready"], b + 1)
                for k, c0, c1 in BANKS[0:WB]:
                    mm(ps[:, k, 0:c1 - c0], identf[:, :], based[h][:, c0:c1], start=False, stop=False)
                for k, c0, c1 in BANKS[WB:]:
                    for n in range(2):
                        last = mm(ps[:, k, 0:c1 - c0], identb[:, :], based_part[h][:, n, c0 - WB * QW:c1 - WB * QW], start=False, stop=False)
                last.then_inc(S["based_used"], 1)
            with pe.Fori(0, NT // 2) as i:
                for h in range(2):
                    add_bases(2 * i + h, h)
            add_bases(NT - 1, 0)
            for k, c0, c1 in BANKS:
                last = mm(ps[:, k, 0:c1 - c0], zerob[:, 0:P], zerob[:, 0:c1 - c0], start=False, stop=True)
            last.then_inc(S["based_used"], 1)
            pe.sem_inc(S["sorted_batches"], 2)
            with pe.Fori(0, NSUP) as i:
                seen(S["local_copied"], i + 1)
                mm(ps[:, 7, 0:P], zerob[:, 0:P], zerob[:, 0:P], start=True, stop=False)
                with pe.Fori(0, NBAT // 2) as j:
                    for h in range(2):
                        seen(S["pair_ready"], i * NBAT + j * 2 + h + 2)
                        for u in range(BAT):
                            last = mm(ps[:, 7, 0:P], hot_part[:, h, u, :], hot_rec[:, h, u, :, :].rearrange("p a v -> p (a v)"), start=False, stop=False)
                        last.then_inc(S["sorted_batches"], 1)
                mm(ps[:, 7, 0:P], zerob[:, 0:P], zerob[:, 0:P], start=False, stop=True).then_inc(S["local_sorted"], 1)
            for k in range(NCHUNK // P):
                pe.wait_ge(loaded_back[k % 2], 16 * (k // 2 + 1))
                if k >= 2:
                    pe.wait_ge(S["unpacked"], k - 1)
                    pe.wait_ge(S["w_copied"], k - 1)
                for v in range(REC):
                    last = pe.transpose(ps[:, 4 + 2 * v + k % 2, 0:P], back[:, k % 2, v::REC], identf[:, :])
                last.then_inc(S["transposed"], 1)

            pe.wait_ge(S["wx_loaded"], 16)
            for m in range(4):
                if m >= 2:
                    pe.wait_ge(S["wxT_sb"], m - 1)
                for c in range(2):
                    last = pe.transpose(ps[:, 2 + m % 2, c * P:(c + 1) * P], raw_wx[:, c, m * P:(m + 1) * P], identf[:, :])
                last.then_inc(S["wxT_ps"], 1)
            pe.wait_ge(S["wxT_sb"], 4)
            pe.wait_ge(S["unpacked"], NCHUNK // P)
            pe.wait_ge(S["w_copied"], NCHUNK // P)
            pe.wait_ge(S["rows_loaded"], 16 * 17)
            for h in range(8):
                half_of = slice(h % 2 * D2, h % 2 * D2 + D2)
                for k in range(2):
                    mm(ps[:, 2 + k + 2 * (h % 2), h * D2:(h + 1) * D2], wxT[half_of, h // 2, k * P:(k + 1) * P], wslice[half_of, :], start=True, stop=True)
                last = mm(ps[0:3, 6 + h % 2, h * D2:(h + 1) * D2], bxc[half_of, h // 2:h // 2 + 1].broadcast_to([D2, 3]), wslice[half_of, :], start=True, stop=True)
            last.then_inc(S["wc_ps"], 1)
            pe.wait_ge(S["wc_sb"], 1)
            pe.sem_inc(S["multiplied"], RING)

            def groups(n, *js):
                for j in js:
                    for u in range(2):
                        q = 2 * j + u
                        seen(gathered[q], 16 * n + 16)
                        seen(S["hot_ready"], RING * n + q + 1)
                        if u == 0:
                            seen(S["added"], n * STEP + j + 1)
                        mm(ps[:, j % 2, 0:C], onehot[:, q % HOT, :], gath[:, q, :], start=u == 0, stop=u == 1).then_inc(S["multiplied"], 1)

            def turn(n, t):
                seen(S["xt_sb"], n + 1)
                seen(S["cur_sb"], n + 1)
                for c in range(2):
                    last = pe.transpose(ps[:, 2, c * P:(c + 1) * P], xcur[:, c * P:(c + 1) * P], identf[:, :])
                last.then_inc(S["xt_ps"], 1)

            tile = lambda a, t: a[:, ds(t, 1), :].rearrange("p a c -> p (a c)")
            for g in range(2):
                mm(ps[:, 4 + g, 0:P + 1], zerob[:, 0:P], zerob[:, 0:P + 1], start=True, stop=False)

            def kv_tile(t, edge):
                turn(t, t)
                groups(t, 0, 1)
                seen(S["feat_ready"], t + 1)
                seen(S["v_sb"], t + 1)
                seen(S["xt_sb"], t + 2)
                for v in range(2):
                    for c in range(2):
                        last = mm(ps[:, 3 + 3 * v, 0:C], xT[:, c, :], wqkvT[:, c, C * (1 + v):C * (2 + v)], start=c == 0, stop=c == 1)
                last.then_inc(S["proj"], 1)
                groups(t, 2, 3)
                seen(S["feat_ready"], t + 2)
                seen(S["v_sb"], t + 2)
                r = TAIL if edge else P
                for g in range(2):
                    last = mm(ps[:, 4 + g, 0:P + 1], feat[0:r, g * P:(g + 1) * P], vone[0:r, g, :], start=False, stop=edge)
                last.then_inc(S["third"], 1)
                groups(t, 4, 5)
            with pe.Fori(0, NT - 1) as t:
                kv_tile(t, False)
            kv_tile(NT - 1, True)
            pe.wait_ge(S["third"], NT + 1)
            pe.sem_inc(S["kv_done"], 1)
            pe.wait_ge(S["kv_diag"], 1)
            with pe.Fori(0, NT) as t:
                turn(t + NT, t)
                groups(t + NT, 0, 1)
                seen(S["feat_ready"], t + NT + 1)
                seen(S["xt_sb"], t + NT + 2)
                for g in range(2):
                    for c in range(2):
                        last = mm(ps[:, 3, g * P:(g + 1) * P], wqkvT[:, c, g * P:(g + 1) * P], xT[:, c, :], start=c == 0, stop=c == 1)
                last.then_inc(S["proj"], 1)
                groups(t + NT, 2, 3)
                seen(S["res"], t + 1)
                seen(S["feat_ready"], t + NT + 2)
                for g in range(2):
                    last = mm(ps[:, 6 + g, 0:132], feat[:, g * P:(g + 1) * P], kvd[:, g, :], start=True, stop=True)
                last.then_inc(S["third"], 1)
                groups(t + NT, 4, 5)
            with pe.Fori(0, NT) as t:
                n = t + 2 * NT
                turn(n, t)
                groups(n, 0, 1)
                seen(S["feat_ready"], n + 1)
                seen(S["xt_sb"], n + 2)
                for g in range(2):
                    for c in range(2):
                        last = mm(ps[:, 3, g * P:(g + 1) * P], w1T[:, c, g * P:(g + 1) * P], xT[:, c, :], start=c == 0, stop=c == 1)
                last.then_inc(S["proj"], 1)
                groups(n, 2, 3)
                seen(S["res"], t + NT + 1)
                seen(S["feat_ready"], n + 2)
                for g in range(2):
                    mm(ps[:, 6, 0:C], feat[:, g * P:(g + 1) * P], w2T[:, g, :], start=g == 0, stop=False)
                mm(ps[:, 6, 0:C], onesb[0:3, :], bias2[:, :], start=False, stop=True).then_inc(S["third"], 1)
                groups(n, 4, 5)
            for k in range((REST + RING - 1) // RING):
                groups(3 * NT + k, *range(min(STEP, REST // 2 - k * STEP)))

            def ffn_step(t, h):
                if live(t, 0):
                    seen(S["f_norm"], t + 1)
                    for c in range(2):
                        last = pe.transpose(ps[:, 2, c * P:(c + 1) * P], xs[:, h, c * P:(c + 1) * P], identf[:, :])
                    last.then_inc(S["f_xT"], 1)
                if live(t, 2):
                    k = (h - 2) % 4
                    edge = isinstance(t, int) and t - 2 == NT - 1
                    r = TAIL if edge else P
                    seen(S["f_slice"], t - 1)
                    for m in range(4):
                        mm(ps[:, 4 + m, 0:C + 1], slices[0:r, k, m * P:(m + 1) * P], xs[0:r, k, :], start=False, stop=edge)
                    seen(S["f_sTsb"], t - 1)
                    for m in range(4):
                        last = pe.transpose(ps[:, 3, m * P:(m + 1) * P], slices[:, k, m * P:(m + 1) * P], identf[:, :])
                    last.then_inc(S["f_pair"], 1)
                if live(t, 0):
                    seen(S["f_xsT"], t + 1)
                    for c in range(2):
                        mm(ps[:, h % 2, :], xsT[:, c, :], wc[:, c, :], start=c == 0, stop=False)
                    mm(ps[:, h % 2, :], onesb[0:3, :], bias_logit[:, :], start=False, stop=True).then_inc(S["f_logit"], 1)
            pe.wait_ge(S["rstd_root"], 3)
            for m in range(4):
                mm(ps[:, 4 + m, 0:C + 1], zerob[:, 0:P], zerob[:, 0:C + 1], start=True, stop=False)
            pe.sem_inc(S["f_pair"], 1)
            pipeline(pe, ffn_step)
            pe.wait_ge(S["f_pair"], NT + 2)
            pe.sem_inc(S["tok_ps"], 1)
            pe.wait_ge(S["tok_sb"], 1)
            pe.wait_ge(S["late_loaded"], 16)
            for m in range(4):
                for c in range(2):
                    pe.transpose(ps[:, c, m * P:(m + 1) * P], token[:, m, c * P:(c + 1) * P], identf[:, :])
                last = pe.transpose(ps[0:1, 2, m * P:(m + 1) * P], token[:, m, C:C + 1], identf[:, :])
            last.then_inc(S["tok_ps"], 1)
            pe.wait_ge(S["tok_sb"], 2)
            pe.wait_ge(S["f_sTsb"], NT + 1)
            for h in range(8):
                hh = slice(h * D2, (h + 1) * D2)
                for c in range(2):
                    mm(ps[0:D2, 3, hh], wfx[:, c, hh], tokenT[:, c, hh], start=c == 0, stop=False)
                last = mm(ps[0:D2, 3, hh], bfx[:, hh], ratio[:, hh], start=False, stop=True)
            last.then_inc(S["tok_ps"], 1)
            pe.wait_ge(S["tok_sb"], 3)
            mm(ps[0:D2, 0, :], wq, tokf, start=True, stop=True)
            mm(ps[0:D2, 1, :], wk, tokf, start=True, stop=True)
            for h in range(8):
                hh = slice(h * D2, (h + 1) * D2)
                last = mm(ps[0:D2, 2, hh], tokf[:, hh], wv, start=True, stop=True)
            last.then_inc(S["tok_ps"], 1)
            pe.wait_ge(S["tok_sb"], 4)
            for h in range(8):
                hh = slice(h * D2, (h + 1) * D2)
                last = mm(ps[0:D2, 3, hh], qk[:, 0, hh], qk[:, 1, hh], start=True, stop=True)
            last.then_inc(S["tok_ps"], 1)
            pe.wait_ge(S["tok_sb"], 11)
            for h in range(8):
                hh = slice(h * D2, (h + 1) * D2)
                last = pe.transpose(ps[0:D2, 0, hh], att[:, hh], identf[0:D2, 0:D2])
            last.then_inc(S["tok_ps"], 1)
            pe.wait_ge(S["tok_sb"], 12)
            for h in range(8):
                hh = slice(h * D2, (h + 1) * D2)
                last = mm(ps[0:D2, 1, hh], vtok[:, hh], attT[:, hh], start=True, stop=True)
            last.then_inc(S["tok_ps"], 1)
            pe.wait_ge(S["tok_sb"], 13)
            for h in range(8):
                last = mm(ps[h % 2 * D2:h % 2 * D2 + D2, 4 + h // 2, 0:C], outT[:, h * D2:(h + 1) * D2], wout[:, h, :], start=True, stop=True)
            last.then_inc(S["tok_ps"], 1)
            pe.wait_ge(S["tok_sb"], 14)

            def project(t, h):
                seen(S["sl_sb"], t + 1)
                for m in range(4):
                    mm(ps[:, h, 0:C], slcur[:, h, m, :], mout[:, m, :], start=m == 0, stop=False)
                mm(ps[:, h, 0:C], onesb[0:3, :], biaso[:, :], start=False, stop=True).then_inc(S["out_ps"], 1)
            with pe.Fori(0, NT // 4) as i:
                for h in range(4):
                    seen(S["out_sum"], 4 * i + h + 1)
                    project(4 * i + h, h)
            seen(S["out_sum"], NT)
            project(NT - 1, 0)


_INS = ["x", "src", "dst", "edge_weight", "L0_mix_Wqkv", "L0_mix_ln1_g", "L0_mix_ln1_b", "L0_mix_W1", "L0_mix_b1",
        "L0_mix_W2", "L0_mix_b2", "L0_mix_ln2_g", "L0_mix_ln2_b", "L0_ffn_W_fx", "L0_ffn_b_fx", "L0_ffn_W_x",
        "L0_ffn_b_x", "L0_ffn_W_slice", "L0_ffn_b_slice", "L0_ffn_W_q", "L0_ffn_W_k", "L0_ffn_W_v", "L0_ffn_W_out",
        "L0_ffn_b_out", "L0_ffn_temperature"]


def kernel(**inputs):
    import numpy as np
    import concourse.bacc as bacc
    from concourse.bass_utils import run_bass_kernel_spmd

    nc = bacc.Bacc("TRN2", target_bir_lowering=False, num_devices=1)
    arrays, args = {}, []
    for name in _INS:
        a = np.ascontiguousarray(inputs[name])
        arrays[f"in_{name}"] = a
        args.append(nc.dram_tensor(f"in_{name}", a.shape, mybir.dt.from_np(a.dtype), kind="ExternalInput").ap())
    args.append(nc.dram_tensor("out_rows", (N, C), F32, kind="ExternalOutput").ap())
    program(nc, *args)
    result = run_bass_kernel_spmd(nc, [arrays], core_ids=[0])
    return result.results[0]["out_rows"]
```

```python
import concourse.bass as bass
from concourse import mybir
from contextlib import ExitStack

F32, I32, BF16 = mybir.dt.float32, mybir.dt.int32, mybir.dt.bfloat16
ALU = mybir.AluOpType
ACT = mybir.ActivationFunctionType
AX = mybir.AxisListType
ds = bass.ds

P = 128
N, C, E = 6250, 256, 206250
NT = (N + P - 1) // P
TAIL = N - (NT - 1) * P
COLS = 1620
LASTC = E - (P - 1) * COLS
SUPC = 60
NSUP = COLS // SUPC
BAT = 5
NBAT = SUPC // BAT
SCAT = 3
HRING = 3
SHARE = dict(dve=slice(0, 1), pool=slice(1, 3), act=slice(3, 5))
REC = 2
BLK = 8
BW = BLK * REC
NG8 = 8
GRP = 2 * P // BLK
NGRP = 896
NCHUNK = 2 * NGRP
RING = 12
IDX = 2 * RING
HOT = 6
STEP = RING // 2
BACK = NCHUNK // P
ROUNDS = [range(k, min(BACK, k + 4)) for k in range(0, BACK, 4)]
USED = (E + NSUP * NT * (BLK - 1) + NT * (2 * P - BLK)) // (2 * P)
REST = 2 * USED - 3 * NT * RING
assert USED <= NGRP and REST > 0
NBLK = NGRP * GRP
TRASH = NBLK
NREC = NBLK + NSUP * NG8 * P
assert NSUP * SUPC == COLS and (P * SUPC + NT * (BLK - 1)) <= NG8 * P * BLK
TURN = 7
assert NT % TURN == 0
BY_ACT = 4
PIPE = (NT - 4) // 4
D2 = 64
INNER = 512
QN = 4
QW = -(-NSUP // QN) * SUPC
BANKS = [(k, k * QW, min(COLS, (k + 1) * QW)) for k in range(QN)]
WB = 3
WHOLE = WB * QW // SUPC
CW = NT * NSUP // 3
ARENA = NT * C + 3 * (NCHUNK + 4) + 5 * COLS


def wide(ap, shape, axis):
    names = list("abcd"[:len(ap.shape)])
    split, new = list(names), list(names)
    if axis == len(names):
        split[-1] = f"({names[-1]} z)"
    else:
        split[axis] = f"(z {names[axis]})"
    new.insert(axis, "z")
    return ap.rearrange(f"{' '.join(split)} -> {' '.join(new)}", z=1).broadcast_to(shape)


class Steps:

    def __init__(self, eng, sem):
        self.eng, self.sem, self.base, self.off, self.reg = eng, sem, 0, 0, 0

    def loop(self, i, per):
        self.reg, self.off, self.per = i * per, 0, per

    def leave(self, count):
        assert self.off == self.per, (self.off, self.per)
        self.base, self.reg, self.off = self.base + count * self.per, 0, 0

    def freeze(self):
        self.base, self.off = self.base + self.off, 0

    def __call__(self, ins):
        self.off += 1
        ins.then_inc(self.sem, 1)
        self.eng.wait_ge(self.sem, self.base + self.reg + self.off)


def pipeline(eng, body, steps=None, per=0):
    for t in range(2):
        body(t, t)
    if steps:
        steps.freeze()
    with eng.Fori(0, PIPE) as i:
        if steps:
            steps.loop(i, 4 * per)
        for u in range(4):
            body(4 * i + 2 + u, (2 + u) % 4)
    if steps:
        steps.leave(PIPE)
    for t in range(2 + 4 * PIPE, NT + 2):
        body(t, t % 4)


def over_superchunks(eng, body, steps=None, per=0):
    body(0)
    body(1)
    if steps:
        steps.freeze()
    with eng.Fori(0, NSUP - 2) as i:
        if steps:
            steps.loop(i, per)
        body(i + 2)
    if steps:
        steps.leave(NSUP - 2)


def is_first(n, count):
    return isinstance(n, int) and n < count


def live(t, back):
    return not isinstance(t, int) or 0 <= t - back < NT


def program(nc, x, src, dst, edge_weight, Wqkv, ln1_g, ln1_b, W1, b1, W2, b2, ln2_g, ln2_b,
            W_fx, b_fx, W_x, b_x, W_slice, b_slice, W_q, W_k, W_v, W_out, b_out, temperature, out):
    ctx = ExitStack()
    with ctx:
        def sb(name, shape, dt=F32):
            return ctx.enter_context(nc.sbuf_tensor(name, shape, dt))

        def sem(name):
            return ctx.enter_context(nc.semaphore(name))

        rec = nc.dram_tensor("edge_records", (NREC, BW), F32).ap()
        xg = nc.dram_tensor("normed_rows", (N + 1, C), F32).ap()
        bucket_dram = nc.dram_tensor("group_buckets", (P, NGRP // P), I32).ap()

        ps = ctx.enter_context(nc.psum_tensor("ps", [P, 8, 512], F32))
        acc = sb("acc", [P, NT, C])
        iota = sb("iota", [P, P])
        identf = sb("identf", [P, P])
        identb = sb("identb", [P, P], BF16)
        before = sb("before", [P, P], BF16)
        onesb = sb("onesb", [P, P], BF16)
        zerob = sb("zerob", [P, QW], BF16)
        block_no = sb("block_no", [P, NG8])
        group_no = sb("group_no", [P, NGRP // P])
        stats = sb("stats", [P, NT, 6])
        mean = sb("mean", [P, NT])
        half = sb("half", [P, NT])
        rstd = sb("rstd", [P, NT])
        arena = sb("arena", [P, ARENA])
        bench = sb("bench", [P, HRING * BAT * 320])

        def view(at, shape, dt=F32):
            n = 1
            for d in shape:
                n *= d
            v = arena[:, at:at + n]
            if dt is not F32:
                v = v.bitcast(dt)
            if len(shape) == 2:
                v = v.rearrange("p (a b) -> p a b", b=shape[1])
            return v

        xn = view(0, [NT, C])
        tables = [NT, NSUP]
        tables_s = [NSUP, NT + 1]
        tw = NSUP * (NT + 1)
        tabi = view(0, [NT * NSUP], I32)
        nbi = view(tw, [NT * NSUP], I32)
        nb = view(tw, tables)
        nbs = view(2 * tw, tables_s)
        rstb = view(3 * tw, tables_s)
        rsts = view(4 * tw, tables)
        blocks_before = view(5 * tw, tables)
        blocks_through = view(6 * tw, tables)
        delta = view(7 * tw, tables_s)
        base = view(8 * tw, tables)
        base_part = [view((5 + n) * tw, [NT * (NSUP - WHOLE) // 2 + 1]).bitcast(BF16)[:, 0:NT * (NSUP - WHOLE)].rearrange("p (b s) -> p b s", b=NT) for n in range(2)]
        started = view(9 * tw, [NGRP // P, NT])
        e0, ew = NT * C, NCHUNK + 4
        srci = view(e0, [COLS], I32)
        dsti = view(e0 + ew, [COLS], I32)
        loi = view(e0 + 2 * ew, [COLS], I32)
        posi = srci
        gidx = view(e0, [NCHUNK], I32)
        slo = view(e0 + ew, [NCHUNK + 4])
        sw = view(e0 + 2 * ew, [NCHUNK + 4])
        v0 = e0 + 3 * ew
        vals = view(v0, [COLS, REC])
        based_at = (view(v0 + 2 * COLS, [COLS]), bench[:, COLS // 2:COLS // 2 + COLS])
        base_float = view(v0 + 2 * COLS, [COLS])
        based = [a[:, 0:WB * QW] for a in based_at]
        based_part = [a[:, WB * QW:COLS].bitcast(BF16).rearrange("p (n c) -> p n c", n=2) for a in based_at]
        gath = view(v0, [RING, C])
        back = view(v0, [BACK, P * REC])
        geti = view(v0 + BACK * P * REC, [4 * P], I32)
        getl = view(v0 + BACK * P * REC + 4 * P, [4 * P], I32)
        onehot = view(v0 + RING * C, [HOT, P])
        w0 = v0 + 3 * COLS
        wraw = view(w0, [COLS])
        slotp = wraw
        restart = view(w0 + COLS, [NSUP, SUPC])
        slotc = view(w0 + COLS, [COLS])
        group_bucket = view(w0 + COLS, [COLS], I32)[0:1, 0:NGRP]
        bucket, mask0, running0, ranked0, running1 = (bench[:, k * COLS // 2:(k + 1) * COLS // 2].bitcast(BF16) for k in range(5))
        hw = HRING * BAT * 64
        hot_part = bench[:, 0:2 * hw].rearrange("p (h u a) -> p h u a", h=HRING, u=BAT)
        hot_col = bench[:, 2 * hw:3 * hw].rearrange("p (h u a) -> p h u a", h=HRING, u=BAT)
        hot_rec = bench[:, 3 * hw:5 * hw].rearrange("p (h u a v) -> p h u a v", h=HRING, u=BAT, v=REC)
        tabs = sb("tabs", [P, 4096])
        cnt = tabs[:, 0:NT * NSUP // 2 + 1].bitcast(BF16)[:, 0:NT * NSUP].rearrange("p (b s) -> p b s", s=NSUP)
        lstart = tabs[:, 672:672 + tw].rearrange("p (s b) -> p s b", s=NSUP)
        jump = tabs[:, 672 + tw:672 + 2 * tw].rearrange("p (s b) -> p s b", s=NSUP)
        mask1, ranked1 = (tabs[:, 672 + k * COLS // 2:672 + (k + 1) * COLS // 2].bitcast(BF16) for k in range(2))
        mask, running, ranked = (mask0, mask1), (running0, running1), (ranked0, ranked1)
        bucket_int = sb("bucket_int", [P, NT], I32)
        bucket_blocks = sb("bucket_blocks", [P, NT])
        bucket_start = sb("bucket_start", [P, NT])
        unit_row = sb("unit_row", [P, NT])
        group_bucket_f = sb("group_bucket_f", [P, NGRP // P])
        group_bucket_i = sb("group_bucket_i", [P, NGRP // P], I32)
        passed = tabs[:, 672 + 2 * tw:672 + 2 * tw + NG8 * (NT + 1)].rearrange("p (g b) -> p g b", g=NG8)
        moved = sb("moved", [P, NG8])
        dest = sb("dest", [P, NG8], I32)
        raw_qkv = view(0, [6, C])
        raw_w1 = view(6 * C, [2, C])
        raw_w2 = view(8 * C, [2, C])
        zerof = view(5 * tw, [512])
        raw_wx = bench[:, 0:2 * INNER].rearrange("p (k o) -> p k o", o=INNER)
        wxT = bench[:, 2 * INNER:4 * INNER].rearrange("p (m c) -> p m c", c=C)
        xT = bench[:, 0:C].rearrange("p (k t) -> p k t", t=P)
        low = bench[:, C:2 * C]
        grown = bench[:, 2 * C:3 * C]
        feat = bench[:, 3 * C:4 * C]
        vone = bench[:, 4 * C:4 * C + 2 * (P + 1)].rearrange("p (g m) -> p g m", m=P + 1)
        tmp = bench[:, 5 * C + 4:6 * C + 4]
        zden = bench[:, 6 * C + 4:6 * C + 12].rearrange("p (g h) -> p g h", h=4)
        xcur = bench[:, 6 * C + 12:7 * C + 12]
        slcur = bench[:, 0:4 * INNER].rearrange("p (h m t) -> p h m t", h=4, t=P)
        wmix = sb("wmix", [P, 2824])
        wqkvT = wmix[:, 0:6 * C].rearrange("p (k o) -> p k o", o=3 * C)
        w1T = wmix[:, 6 * C:8 * C].rearrange("p (k o) -> p k o", o=C)
        w2T = wmix[:, 8 * C:10 * C].rearrange("p (k o) -> p k o", o=C)
        kvd = wmix[:, 10 * C:10 * C + 264].rearrange("p (g m) -> p g m", m=132)
        wout = wmix[0:D2, 0:8 * C].rearrange("p (h c) -> p h c", c=C)
        wc = tabs[:, 0:2 * INNER].rearrange("p (k o) -> p k o", o=INNER)
        mout = tabs[:, 0:4 * C].rearrange("p (m c) -> p m c", c=C)
        wfx = tabs[:, 2 * INNER:4 * INNER].rearrange("p (k o) -> p k o", o=INNER)
        rows = tabs[:, 4 * INNER:4 * INNER + 4 * C].rearrange("p (n c) -> p n c", c=C)
        small = tabs[:, 3072:4096]
        wslice = small[:, 0:64]
        wq, wk, wv = (small[0:D2, 64 + 64 * n:128 + 64 * n] for n in range(3))
        bxc = small[:, 256:260]
        b1c = small[:, 260:262]
        rtemp = small[:, 262:270]
        bsl = small[0:3, 270:334]
        spread, root, middle, off = (small[:, 880 + n:881 + n] for n in range(4))
        bfx = small[0:1, 350:862]
        biasf = arena[0:3, w0:w0 + 3 * INNER].rearrange("p (n c) -> p n c", c=INNER)
        bias_logit = sb("bias_logit", [3, INNER], BF16)
        bias2 = sb("bias2", [3, C], BF16)
        biaso = sb("biaso", [3, C], BF16)
        xs = bench[:, 0:4 * (C + 1)].rearrange("p (h c) -> p h c", c=C + 1)
        xsT = bench[:, 1028:1028 + C].rearrange("p (k t) -> p k t", t=P)
        slices = bench[:, 1284:1284 + 4 * INNER].rearrange("p (h o) -> p h o", h=4)
        fmax = bench[:, 3332:3348].rearrange("p (h o) -> p h o", h=2)
        fsum = bench[:, 3348:3380].rearrange("p (h o) -> p h o", h=4)
        sliceT = view(0, [4, NT * P])
        token = bench[:, 0:4 * (C + 1)].rearrange("p (m c) -> p m c", c=C + 1)
        tokenT = bench[:, 1028:1028 + 2 * INNER].rearrange("p (k o) -> p k o", o=INNER)
        ratio = bench[0:1, 2052:2052 + INNER]
        tokf = bench[0:D2, 2564:2564 + INNER]
        tden = bench[:, 3076:3080]
        qk = tabs[0:D2, 4 * INNER:6 * INNER].rearrange("p (n o) -> p n o", o=INNER)
        vtok = bench[0:D2, 0:INNER]
        att = bench[0:D2, INNER:2 * INNER]
        attT = bench[0:D2, 1028:1028 + INNER]
        outT = bench[0:D2, 1540:1540 + INNER]
        amax = small[0:D2, 334:342]
        asum = small[0:D2, 342:350]
        local = sb("local", [P, NG8 * BW])
        iring = sb("iring", [P, 2, IDX], I32)

        names = """
            consts pad_set zero_rows
            src_loaded dst_loaded w_loaded x_loaded raw_loaded
            zeroed xn_stored bucket_stored bucket_loaded fold_loaded rows_loaded wx_loaded late_loaded out_stored
            trans_ps trans_sb
            masked scan_ready prod_even prod_odd prod_used count_copied
            count_sums sums_read bucket_ready based_ready based_used
            row_stats var_ready rstd_root shift_ready normed
            col_hot pair_ready hot_pool hot_act sorted_batches local_sorted local_copied dest_ready
            wxT_ps wxT_sb wc_ps wc_sb transposed unpacked w_copied vone_set
            ring_ready hot_ready multiplied added
            cur_sb xt_ps xt_sb proj feat_low feat_exp feat_ready v_sb third res kv_done kv_diag mixed row_var row_root
            f_norm f_xT f_xsT f_logit f_low f_exp f_sum f_slice f_pair f_sTsb
            tok_ps tok_sb sl_sb out_ps out_sum
            step_dve pace pace_sp pace_pe pace_act""".split()
        S = {n: sem(n) for n in names}
        START_AT_ONE = """third proj xt_ps out_ps prod_even prod_odd count_copied prod_used based_used pair_ready f_pair f_exp local_copied xt_sb feat_ready v_sb res f_sTsb out_sum""".split()
        scattered = [sem(f"scattered{g}") for g in range(NG8)]
        gathered = [sem(f"gathered{g}") for g in range(RING)]
        loaded_back = [sem(f"loaded_back{g}") for g in range(len(ROUNDS))]
        block = ctx.enter_context(nc.Block())

        @block.sync
        def _(sp):
            for name in START_AT_ONE:
                sp.sem_inc(S[name], 1)
            sp.sem_inc(S["out_ps"], 3)
            sp.sem_inc(S["out_sum"], 3)
            sp.dma_start(raw_qkv, Wqkv.rearrange("(o p) c -> p o c", p=P)).then_inc(S["raw_loaded"], 16)
            sp.dma_start(raw_w1, W1.rearrange("(o p) c -> p o c", p=P)).then_inc(S["raw_loaded"], 16)
            sp.dma_start(raw_w2, W2.rearrange("(o p) c -> p o c", p=P)).then_inc(S["raw_loaded"], 16)
            sp.wait_ge(S["pad_set"], 4)
            sp.dma_start(srci[0:112, :], src[0:112 * COLS].rearrange("(p c) -> p c", c=COLS)).then_inc(S["src_loaded"], 16)
            sp.dma_start(srci[112:127, :], src[112 * COLS:127 * COLS].rearrange("(p c) -> p c", c=COLS)).then_inc(S["src_loaded"], 16)
            sp.dma_start(srci[127:128, 0:LASTC], src[127 * COLS:E].rearrange("(p c) -> p c", p=1)).then_inc(S["src_loaded"], 16)
            sp.dma_start(dsti[0:112, :], dst[0:112 * COLS].rearrange("(p c) -> p c", c=COLS)).then_inc(S["dst_loaded"], 16)
            sp.dma_start(dsti[112:127, :], dst[112 * COLS:127 * COLS].rearrange("(p c) -> p c", c=COLS)).then_inc(S["dst_loaded"], 16)
            sp.dma_start(dsti[127:128, 0:LASTC], dst[127 * COLS:E].rearrange("(p c) -> p c", p=1)).then_inc(S["dst_loaded"], 16)
            sp.dma_start(wraw[0:112, :], edge_weight[0:112 * COLS].rearrange("(p c) -> p c", c=COLS)).then_inc(S["w_loaded"], 16)
            sp.dma_start(wraw[112:127, :], edge_weight[112 * COLS:127 * COLS].rearrange("(p c) -> p c", c=COLS)).then_inc(S["w_loaded"], 16)
            sp.dma_start(wraw[127:128, 0:LASTC], edge_weight[127 * COLS:E].rearrange("(p c) -> p c", p=1)).then_inc(S["w_loaded"], 16)
            sp.dma_start(acc[:, 0:NT - 1, :], x[0:(NT - 1) * P, :].rearrange("(t p) c -> p t c", p=P)).then_inc(S["x_loaded"], 16)
            sp.dma_start(acc[0:TAIL, NT - 1, :], x[(NT - 1) * P:N, :]).then_inc(S["x_loaded"], 16)
            sp.wait_ge(S["zero_rows"], 2)
            zr = NBLK * BW // (P * 512)
            for k in range(zr):
                sp.dma_start(rec[0:NBLK, :].rearrange("(k p a) w -> k p (a w)", k=zr, p=P)[k], zerof[:, :]).then_inc(S["zeroed"], 16)
            sp.dma_start(xg[0:1, :], zerof[0:1, 0:C]).then_inc(S["zeroed"], 16)
            sp.wait_ge(S["normed"], NT)
            sp.dma_start(xg[1:1 + (NT - 1) * P, :].rearrange("(t p) c -> p t c", p=P), xn[:, 0:NT - 1, :]).then_inc(S["xn_stored"], 16)
            sp.dma_start(xg[1 + (NT - 1) * P:N + 1, :], xn[0:TAIL, NT - 1, :]).then_inc(S["xn_stored"], 16)
            sp.wait_ge(S["bucket_ready"], 1)
            sp.dma_start(bucket_dram, group_bucket_i[:, :]).then_inc(S["bucket_stored"], 16)
            sp.wait_ge(S["bucket_stored"], 16)
            sp.wait_ge(S["local_sorted"], NSUP)
            sp.dma_start(group_bucket[0:1, :], bucket_dram.rearrange("p q -> (p q)").rearrange("(a n) -> a n", a=1)).then_inc(S["bucket_loaded"], 16)
            sp.dma_start(raw_wx, W_x.rearrange("(k p) o -> p k o", p=P)).then_inc(S["wx_loaded"], 16)
            sp.wait_ge(S["dest_ready"], NSUP)
            for h in range(2):
                sp.dma_start(wslice[h * D2:(h + 1) * D2, :], W_slice).then_inc(S["fold_loaded"], 16)
            sp.dma_start(bxc, b_x.rearrange("(m p) -> p m", p=P), allow_slow_non_contiguous=True).then_inc(S["fold_loaded"], 16)
            sp.dma_start(wfx, W_fx.rearrange("(k p) o -> p k o", p=P)).then_inc(S["rows_loaded"], 16)
            for n, v in enumerate((ln1_g, ln1_b, ln2_g, ln2_b)):
                sp.dma_start(rows[:, n, :], v.rearrange("(a c) -> a c", a=1).broadcast_to([P, C])).then_inc(S["rows_loaded"], 16)
            for t, v in ((wq, W_q), (wk, W_k), (wv, W_v)):
                sp.dma_start(t, v).then_inc(S["rows_loaded"], 16)
            sp.dma_start(b1c, b1.rearrange("(m p) -> p m", p=P), allow_slow_non_contiguous=True).then_inc(S["rows_loaded"], 16)
            sp.dma_start(rtemp, temperature.rearrange("a h b c -> (b c) (a h)").broadcast_to([P, 8])).then_inc(S["rows_loaded"], 16)
            sp.dma_start(bsl, b_slice.rearrange("(a c) -> a c", a=1).broadcast_to([3, D2])).then_inc(S["rows_loaded"], 16)
            sp.dma_start(bfx, b_fx.rearrange("(a c) -> a c", a=1)).then_inc(S["rows_loaded"], 16)
            sp.dma_start(biasf[:, 1, 0:C], b2.rearrange("(a c) -> a c", a=1).broadcast_to([3, C])).then_inc(S["rows_loaded"], 16)
            sp.dma_start(biasf[:, 1, C:2 * C], b_out.rearrange("(a c) -> a c", a=1).broadcast_to([3, C])).then_inc(S["rows_loaded"], 16)
            for g in range(NG8):
                sp.wait_ge(scattered[g], 16 * NSUP)
            recs = rec[0:NBLK, :].rearrange("(k p a) w -> p k (a w)", p=P, a=P // BLK)
            for n, ks in enumerate(ROUNDS):
                sp.dma_start(back[:, ks[0]:ks[-1] + 1, :], recs[:, ks[0]:ks[-1] + 1, :]).then_inc(loaded_back[n], 16)
            sp.wait_ge(S["third"], 3 * NT + 1)
            sp.dma_start(wout, W_out.rearrange("(h p) c -> p h c", p=D2)).then_inc(S["late_loaded"], 16)
            with sp.Fori(0, NT // 4) as i:
                sp.wait_ge(S["out_sum"], 4 * i + 8)
                sp.sem_inc(S["pace_sp"], 1)
                sp.dma_start(out[ds(i * 4 * P, 4 * P), :].rearrange("(t p) c -> p t c", p=P), acc[:, ds(i * 4, 4), :]).then_inc(S["out_stored"], 16)
            sp.wait_ge(S["out_sum"], NT + 4)
            sp.dma_start(out[(NT - 1) * P:N, :], acc[0:TAIL, NT - 1, :]).then_inc(S["out_stored"], 16)
            sp.wait_ge(S["out_stored"], 16 * (NT // 4 + 1))

        @block.gpsimd
        def _(pool):
            def seen(s, v):
                pool.wait_ge(s, v)
                pool.sem_inc(S["pace"], 1)
            pool.memset(identf[:, :], 0.0).then_inc(S["consts"], 1)
            pool.memset(identb[:, :], 0.0).then_inc(S["consts"], 1)
            pool.memset(onesb[:, :], 1.0).then_inc(S["consts"], 1)
            pool.memset(zerob[:, :], 0.0).then_inc(S["consts"], 1)
            pool.memset(zerof[:, :], 0.0).then_inc(S["zero_rows"], 2)
            pool.iota(iota[:, :], pattern=[[1, P]], base=0, channel_multiplier=0, allow_small_or_imprecise_dtypes=True).then_inc(S["consts"], 1)
            pool.iota(block_no[:, :], pattern=[[P, NG8]], base=0, channel_multiplier=1, allow_small_or_imprecise_dtypes=True).then_inc(S["consts"], 1)
            pool.iota(group_no[:, :], pattern=[[GRP, NGRP // P]], base=0, channel_multiplier=GRP * (NGRP // P), allow_small_or_imprecise_dtypes=True).then_inc(S["consts"], 1)
            pool.wait_ge(S["consts"], 7)
            pool.affine_select(out=identf[:, :], in_=identf[:, :], compare_op=ALU.not_equal, fill=1.0, base=0, pattern=[[-1, P]], channel_multiplier=1).then_inc(S["consts"], 1)
            pool.affine_select(out=identb[:, :], in_=identb[:, :], compare_op=ALU.not_equal, fill=1.0, base=0, pattern=[[-1, P]], channel_multiplier=1).then_inc(S["consts"], 1)
            pool.affine_select(out=before[:, :], in_=onesb[:, :], compare_op=ALU.is_gt, fill=0.0, base=0, pattern=[[1, P]], channel_multiplier=-1).then_inc(S["consts"], 1)
            with pool.Fori(0, NT // 2) as i:
                pool.wait_ge(S["prod_used"], 2 * i + 2)
                seen(S["scan_ready"], 2 * i + 2)
                pool.tensor_tensor(ranked[1][:, :], running[1][:, :], mask[1][:, :], ALU.mult).then_inc(S["prod_odd"], 1)
            pool.wait_ge(S["zeroed"], 16 * (NBLK * BW // (P * 512) + 1))

            def weigh_columns(i, q):
                n, c = i * NBAT + q, SHARE["pool"]
                count = c.stop - c.start
                pool.wait_ge(S["sorted_batches"], n + 1)
                seen(S["col_hot"], n + 1)
                pool.tensor_tensor(hot_rec[:, q % HRING, c, :, :], wide(hot_col[:, q % HRING, c, :], [P, count, 64, REC], 3), wide(vals[:, ds(i * SUPC + q * BAT + c.start, count), :], [P, count, 64, REC], 2), ALU.mult).then_inc(S["hot_pool"], 1)

            def scatter(i, g):
                if g == 0:
                    pool.wait_ge(S["dest_ready"], i + 1)
                    seen(S["local_copied"], i + 2)
                pool.indirect_dma_start(rec, bass.IndirectOffsetOnAxis(ap=dest[:, g:g + 1], axis=0), local[:, g * BW:(g + 1) * BW], None).then_inc(scattered[g], 16)

            def superchunk(n):
                for q in range(NBAT):
                    weigh_columns(n, q)
                    if 0 <= q - SCAT < NG8 and not is_first(n, 1):
                        scatter(n - 1, q - SCAT)
            over_superchunks(pool, superchunk)
            for g in range(NG8):
                scatter(NSUP - 1, g)
            pool.wait_ge(S["xn_stored"], 32)
            pool.wait_ge(S["unpacked"], len(ROUNDS))

            def set_out(k, h, count):
                pool.tensor_copy(iring[:, h, 0:count], gidx[:, ds(k * IDX, count)]).then_inc(S["ring_ready"], 1)

            def fetch(k, h, count, after):
                seen(S["ring_ready"], k + 1)
                for j in range(count):
                    seen(S["multiplied"], k * IDX + j + 1)
                    if j == RING and after:
                        set_out(k + 1, 1 - h, after)
                    pool.indirect_dma_start(gath[:, j % RING, :], None, xg, bass.IndirectOffsetOnAxis(ap=iring[:, h, j:j + 1], axis=0)).then_inc(gathered[j % RING], 16)
            set_out(0, 0, IDX)
            pairs = (2 * USED // IDX - 1) // 2
            with pool.Fori(0, pairs) as i:
                for h in range(2):
                    fetch(2 * i + h, h, IDX, IDX)
            left = lambda k: max(0, min(IDX, 2 * USED - k * IDX))
            for k in range(2 * pairs, -(-2 * USED // IDX)):
                fetch(k, k % 2, left(k), left(k + 1))

            def weigh(t, h):
                if live(t, 1):
                    seen(S["f_sum"], t)
                    k = (h - 1) % 4
                    pool.tensor_tensor(slices[:, k, :].rearrange("p (n g) -> p n g", g=D2), slices[:, k, :].rearrange("p (n g) -> p n g", g=D2), wide(fsum[:, k, :], [P, 8, D2], 2), ALU.mult).then_inc(S["f_slice"], 1)
            pipeline(pool, weigh)

        @block.scalar
        def _(act):
            def seen(s, v):
                act.wait_ge(s, v)
                act.sem_inc(S["pace_act"], 1)
            for k in range(10):
                act.wait_ge(S["trans_ps"], k + 1)
                to = wqkvT[:, :, k * P:(k + 1) * P] if k < 6 else (w1T if k < 8 else w2T)[:, :, k % 2 * P:k % 2 * P + P]
                act.copy(to, ps[:, 6 + k % 2, 0:2 * P].rearrange("p (k o) -> p k o", k=2)).then_inc(S["trans_sb"], 1)

            def keep_counts(b, h):
                seen(S["scan_ready"], b + 1)
                act.copy(cnt[:, ds(b, 1), :], running[h][:, SUPC - 1::SUPC].rearrange("p (a s) -> p a s", a=1)).then_inc(S["count_copied"], 1)
            with act.Fori(0, NT // 2) as i:
                for h in range(2):
                    keep_counts(2 * i + h, h)
            keep_counts(NT - 1, 0)
            act.wait_ge(S["var_ready"], 1)
            act.activation(rstd[:, :], rstd[:, :], ACT.Sqrt).then_inc(S["rstd_root"], 1)
            act.wait_ge(S["shift_ready"], 1)
            act.wait_ge(S["based_ready"], NT)
            tile = lambda a, t: a[:, ds(t, 1), :].rearrange("p a c -> p (a c)")
            with act.Fori(0, BY_ACT) as i:
                for u in range(TURN):
                    t = i * TURN + u
                    act.activation(tile(xn, t), tile(acc, t), ACT.Identity, bias=half[:, ds(t, 1)], scale=rstd[:, ds(t, 1)]).then_inc(S["normed"], 1)

            def weigh_columns(i, q):
                n, c = i * NBAT + q, SHARE["act"]
                act.wait_ge(S["sorted_batches"], n + 1)
                seen(S["col_hot"], n + 1)
                for u in range(c.start, c.stop):
                    for v in range(REC):
                        last = act.mul(hot_rec[:, q % HRING, u, :, v], hot_col[:, q % HRING, u, :], vals[:, ds(i * SUPC + q * BAT + u, 1), v])
                last.then_inc(S["hot_act"], 1)

            def copy_local(i):
                if not is_first(i, 1):
                    for g in range(NG8):
                        act.wait_ge(scattered[g], 16 * i)
                seen(S["local_sorted"], i + 1)
                act.copy(local[:, :], ps[:, 7, 0:P]).then_inc(S["local_copied"], 1)

            def superchunk(n):
                for q in range(NBAT):
                    weigh_columns(n, q)
                    if q == 0 and not is_first(n, 1):
                        copy_local(n - 1)
            over_superchunks(act, superchunk)
            copy_local(NSUP - 1)
            for m in range(4):
                act.wait_ge(S["wxT_ps"], m + 1)
                act.copy(wxT[:, m, :], ps[:, 2 + m % 2, 0:C]).then_inc(S["wxT_sb"], 1)
            for n, ks in enumerate(ROUNDS):
                act.wait_ge(S["transposed"], n + 1)
                act.copy(sw[:, ks[0] * P:(ks[-1] + 1) * P], ps[:, 6 + n % 2, 0:len(ks) * P]).then_inc(S["w_copied"], 1)

            tile = lambda a, t: a[:, ds(t, 1), :].rearrange("p a c -> p (a c)")

            def stage(n, t):
                seen(S["xt_ps"], n + 1)
                act.copy(xcur, tile(xn, t)).then_inc(S["cur_sb"], 1)

            def copy_xT(n):
                act.wait_ge(S["proj"], n + 1)
                seen(S["xt_ps"], n + 2)
                act.copy(xT[:, :, :], ps[:, 2, 0:C].rearrange("p (k t) -> p k t", k=2)).then_inc(S["xt_sb"], 1)

            def grow(n):
                seen(S["feat_low"], n + 1)
                act.activation(grown, low, ACT.Exp).then_inc(S["feat_exp"], 1)

            act.wait_ge(S["wc_ps"], 1)
            act.wait_ge(S["vone_set"], 1)
            with act.Fori(0, NT) as t:
                stage(t, t)
                copy_xT(t)
                act.wait_ge(S["third"], t + 1)
                seen(S["proj"], t + 2)
                act.copy(vone[:, :, 0:P], ps[:, 6, 0:C].rearrange("p (g m) -> p g m", g=2)).then_inc(S["v_sb"], 1)
                grow(t)
            with act.Fori(0, NT) as t:
                stage(t + NT, t)
                copy_xT(t + NT)
                grow(t + NT)
            act.wait_ge(S["var_ready"], 2)
            act.activation(rstd[:, :], rstd[:, :], ACT.Sqrt).then_inc(S["rstd_root"], 1)

            def second_layer(t, more):
                n = t + 2 * NT
                copy_xT(n)
                act.wait_ge(S["third"], n + 1)
                seen(S["proj"], n + 2)
                act.activation(feat[:, 0:P], ps[:, 3, 0:P], ACT.Gelu, bias=b1c[:, 0:1])
                act.activation(feat[:, P:2 * P], ps[:, 3, P:2 * P], ACT.Gelu, bias=b1c[:, 1:2]).then_inc(S["feat_ready"], 1)
                if more:
                    act.wait_ge(S["mixed"], t + 2)
                    stage(n + 1, t + 1)
                seen(S["row_var"], t + 1)
                act.activation(root, spread, ACT.Sqrt).then_inc(S["row_root"], 1)
            act.wait_ge(S["mixed"], 1)
            stage(2 * NT, 0)
            with act.Fori(0, NT - 1) as t:
                second_layer(t, True)
            second_layer(NT - 1, False)
            act.wait_ge(S["var_ready"], 3)
            act.activation(rstd[:, :], rstd[:, :], ACT.Sqrt).then_inc(S["rstd_root"], 1)

            def ffn_step(t, h):
                if live(t, 0):
                    if live(t, 1):
                        act.wait_ge(S["f_logit"], t)
                    seen(S["f_xT"], t + 1)
                    act.copy(xsT[:, :, :], ps[:, 2, 0:C].rearrange("p (k t) -> p k t", k=2)).then_inc(S["f_xsT"], 1)
                if live(t, 1):
                    seen(S["f_low"], t)
                    k = (h - 1) % 4
                    act.activation(slices[:, k, :], slices[:, k, :], ACT.Exp).then_inc(S["f_exp"], 1)
                if live(t, 2):
                    seen(S["f_pair"], t + 1)
                    act.copy(sliceT[:, :, ds((t - 2) * P, P)], ps[:, 3, 0:INNER].rearrange("p (m t) -> p m t", m=4)).then_inc(S["f_sTsb"], 1)
            pipeline(act, ffn_step)
            act.wait_ge(S["tok_sb"], 9)
            act.activation(att, att, ACT.Exp, scale=D2 ** -0.5).then_inc(S["tok_sb"], 1)
            act.wait_ge(S["tok_sb"], 14)

            def stage_slices(t, h):
                act.copy(slcur[:, h, :, :], sliceT[:, :, ds(t * P, P)]).then_inc(S["sl_sb"], 1)
            with act.Fori(0, NT // 4) as i:
                for h in range(4):
                    seen(S["out_ps"], 4 * i + h + 1)
                    stage_slices(4 * i + h, h)
            seen(S["out_ps"], NT)
            stage_slices(NT - 1, 0)

        def split_bias(step, to, frm, width):
            dve = nc.vector
            hi, rest, mid = biasf[:, 0, 0:width], biasf[:, 2, 0:width], frm
            step(dve.tensor_copy(to[:, 0:width], frm))
            step(dve.tensor_copy(hi, to[:, 0:width]))
            step(dve.tensor_tensor(rest, frm, hi, ALU.subtract))
            step(dve.tensor_copy(to[:, 0:width], rest))
            step(dve.tensor_copy(mid, to[:, 0:width]))
            step(dve.tensor_tensor(rest, rest, mid, ALU.subtract))
            step(dve.tensor_scalar(hi, hi, identf[0:3, 0:1], None, ALU.mult))
            step(dve.scalar_tensor_tensor(hi, mid, identf[0:3, 1:2], hi, ALU.mult, ALU.add))
            step(dve.scalar_tensor_tensor(to[:, 0:width], rest, identf[0:3, 2:3], hi, ALU.mult, ALU.add))

        def var_of_stats(step):
            dve = nc.vector
            dve.tensor_tensor(mean[:, :], stats[:, :, 1], stats[:, :, 4], ALU.add)
            dve.tensor_tensor(half[:, :], stats[:, :, 1], stats[:, :, 4], ALU.subtract)
            step(dve.tensor_tensor(rstd[:, :], stats[:, :, 2], stats[:, :, 5], ALU.add))
            dve.tensor_scalar(mean[:, :], mean[:, :], 0.5, None, ALU.mult)
            dve.scalar_tensor_tensor(half[:, :], half[:, :], 0.25, half[:, :], ALU.mult, ALU.mult)
            step(dve.tensor_scalar(rstd[:, :], rstd[:, :], 1.0 / C, 1e-5, ALU.mult, ALU.add))
            step(dve.tensor_tensor(rstd[:, :], rstd[:, :], half[:, :], ALU.add))

        @block.vector
        def _(dve):
            step = Steps(dve, S["step_dve"])
            dve.memset(srci[96:P, LASTC:COLS], NT * P).then_inc(S["pad_set"], 1)
            dve.memset(dsti[96:P, LASTC:COLS], -1).then_inc(S["pad_set"], 1)
            dve.memset(wraw[96:P, LASTC:COLS], 0.0).then_inc(S["pad_set"], 1)
            dve.memset(acc[96:P, NT - 1, :], 0.0).then_inc(S["pad_set"], 1)
            step(dve.memset(restart[:, :, :], 1.0))
            step(dve.memset(restart[:, :, 0:1], 0.0))
            dve.memset(rstb[:, :, :], 1.0)
            step(dve.memset(rsts[:, :, :], 1.0))
            dve.memset(rstb[:, :, 0:1], 0.0)
            step(dve.memset(rsts[:, :, 0:1], 0.0))
            dve.memset(unit_row[:, :], 1.0)
            dve.memset(slo[:, NCHUNK:], 0.0)
            dve.memset(sw[:, NCHUNK:], 0.0)
            step(dve.memset(nbs[:, :, :], 0.0))
            dve.wait_ge(S["consts"], 10)
            dve.wait_ge(S["src_loaded"], 48)
            dve.wait_ge(S["dst_loaded"], 48)
            dve.wait_ge(S["w_loaded"], 48)
            step(dve.tensor_scalar(loi[:, :], srci[:, :], 7, None, ALU.logical_shift_right))
            step(dve.tensor_copy(bucket[:, :], loi[:, :]))
            step(dve.tensor_scalar(loi[:, :], srci[:, :], P - 1, None, ALU.bitwise_and))
            step(dve.tensor_scalar(base_float[:, :], dsti[:, :], 1.0, float(P), ALU.add, ALU.mult))
            dve.tensor_tensor(vals[:, :, 0], base_float[:, :], loi[:, :], ALU.add)
            step(dve.tensor_copy(vals[:, :, 1], wraw[:, :]))

            def find(b, h):
                dve.tensor_scalar(mask[h][:, :], bucket[:, :], iota[:, ds(b, 1)], None, ALU.is_equal).then_inc(S["masked"], 1)

            def count(b, pair, h, more):
                dve.wait_ge(S["masked"], b + 1)
                dve.wait_ge(S["prod_odd" if h else "prod_even"], pair + 1)
                dve.wait_ge(S["count_copied"], b + 1)
                dve.tensor_tensor_scan(running[h][:, :], restart[:, :, :].rearrange("p s c -> p (s c)"), mask[h][:, :], 0.0, ALU.mult, ALU.add).then_inc(S["scan_ready"], 1)
                if h == 0:
                    dve.wait_ge(S["scan_ready"], b + 1)
                    dve.wait_ge(S["prod_used"], b + 1)
                    dve.tensor_tensor(ranked[0][:, :], running[0][:, :], mask[0][:, :], ALU.mult).then_inc(S["prod_even"], 1)
                    if more:
                        dve.wait_ge(S["prod_odd"], pair + 1)
                        find(b + 1, 1)
                else:
                    dve.wait_ge(S["prod_even"], pair + 2)
                    find(b + 1, 0)
            dve.sem_inc(S["prod_used"], 1)
            dve.sem_inc(S["count_copied"], 1)
            find(0, 0)
            with dve.Fori(0, NT // 2) as i:
                for h in range(2):
                    count(2 * i + h, i, h, True)
            count(NT - 1, NT // 2, 0, False)
            dve.wait_ge(S["prod_used"], NT + 2)
            dve.wait_ge(S["zeroed"], 16 * (NBLK * BW // (P * 512) + 1))
            dve.wait_ge(S["trans_ps"], 10)
            dve.wait_ge(S["count_sums"], 1)
            step(dve.tensor_copy(base[:, :, :].rearrange("p b s -> p (b s)").rearrange("p (k c) -> p k c", k=3), ps[:, 4:7, 0:CW]))
            dve.engine_nop().then_inc(S["sums_read"], 1)
            dve.wait_ge(S["count_sums"], 2)
            step(dve.tensor_scalar(tabi[:, :].rearrange("p (k c) -> p k c", k=3), ps[:, 4:7, 0:CW], float(BLK - 1), None, ALU.add))
            step(dve.tensor_scalar(tabi[:, :], tabi[:, :], 3, None, ALU.logical_shift_right))
            step(dve.tensor_copy(nb[:, :, :].rearrange("p b s -> p (b s)"), tabi[:, :]))
            step(dve.tensor_copy(nbs[:, :, 0:NT].rearrange("p s b -> p b s"), nb[:, :, :]))
            flat = lambda t: t[:, :, :].rearrange("p a b -> p (a b)")
            step(dve.tensor_tensor_scan(flat(lstart), flat(rstb), flat(nbs), 0.0, ALU.mult, ALU.add))
            step(dve.tensor_tensor(flat(lstart), flat(lstart), flat(nbs), ALU.subtract))
            step(dve.tensor_tensor_scan(flat(blocks_through), flat(rsts), flat(nb), 0.0, ALU.mult, ALU.add))
            step(dve.tensor_tensor(flat(blocks_before), flat(blocks_through), flat(nb), ALU.subtract))
            step(dve.tensor_scalar(bucket_int[:, :], blocks_through[:, :, NSUP - 1], float(GRP - 1), None, ALU.add))
            step(dve.tensor_scalar(bucket_int[:, :], bucket_int[:, :], 5, 5, ALU.logical_shift_right, ALU.logical_shift_left))
            step(dve.tensor_copy(bucket_blocks[:, :], bucket_int[:, :]))
            step(dve.tensor_tensor_scan(bucket_start[:, :], unit_row[:, :], bucket_blocks[:, :], 0.0, ALU.mult, ALU.add))
            step(dve.tensor_tensor(bucket_start[:, :], bucket_start[:, :], bucket_blocks[:, :], ALU.subtract))
            step(dve.tensor_tensor(blocks_before[:, :, :], blocks_before[:, :, :], bucket_start[:, :].rearrange("p (b s) -> p b s", s=1).broadcast_to([P, NT, NSUP]), ALU.add))
            step(dve.tensor_tensor(delta[:, :, 0:NT].rearrange("p s b -> p b s"), blocks_before[:, :, :], lstart[:, :, 0:NT].rearrange("p s b -> p b s"), ALU.subtract))
            step(dve.tensor_scalar(delta[:, :, NT], iota[:, 0:NSUP], float(NG8 * P), float(TRASH), ALU.mult, ALU.add))
            step(dve.tensor_tensor(jump[:, :, 1:NT + 1], delta[:, :, 1:NT + 1], delta[:, :, 0:NT], ALU.subtract))
            step(dve.tensor_copy(jump[:, :, 0:1], delta[:, :, 0:1]))
            step(dve.scalar_tensor_tensor(base[:, :, :], lstart[:, :, 0:NT].rearrange("p s b -> p b s"), float(BLK), base[:, :, :], ALU.mult, ALU.add))
            step(dve.tensor_copy(tabi[:, :], flat(base)))
            step(dve.tensor_scalar(nbi[:, :], tabi[:, :], 7, 7, ALU.logical_shift_right, ALU.logical_shift_left))
            step(dve.tensor_copy(base_part[0], nbi[:, :].rearrange("p (b s) -> p b s", b=NT)[:, :, WHOLE:]))
            step(dve.tensor_scalar(nbi[:, :], tabi[:, :], P - 1, None, ALU.bitwise_and))
            step(dve.tensor_copy(base_part[1], nbi[:, :].rearrange("p (b s) -> p b s", b=NT)[:, :, WHOLE:]))
            step(dve.tensor_tensor(started[:, :, :], group_no[:, :].rearrange("p (q b) -> p q b", b=1).broadcast_to([P, NGRP // P, NT]), bucket_start[:, :].rearrange("p (q b) -> p q b", q=1).broadcast_to([P, NGRP // P, NT]), ALU.is_ge))
            step(dve.tensor_reduce(group_bucket_f[:, :], started[:, :, :], AX.X, ALU.add))
            dve.tensor_scalar(group_bucket_i[:, :], group_bucket_f[:, :], 1.0, None, ALU.subtract).then_inc(S["bucket_ready"], 1)
            dve.wait_ge(S["x_loaded"], 32)
            tile = lambda a, t: a[:, ds(t, 1), :].rearrange("p a c -> p (a c)")
            with dve.Fori(0, NT // TURN) as i:
                for u in range(TURN):
                    t = i * TURN + u
                    dve.bn_stats(tile(stats, t), tile(acc, t)).then_inc(S["row_stats"], 1)
            dve.wait_ge(S["row_stats"], NT)
            var_of_stats(step)
            dve.engine_nop().then_inc(S["var_ready"], 1)
            dve.wait_ge(S["rstd_root"], 1)
            step(dve.reciprocal(rstd[:, :], rstd[:, :]))
            dve.scalar_tensor_tensor(half[:, :], mean[:, :], -1.0, rstd[:, :], ALU.mult, ALU.mult).then_inc(S["shift_ready"], 1)
            by_super = lambda a: a.rearrange("p (s c) -> p s c", c=SUPC)

            def add_base(b, h):
                dve.wait_ge(S["based_used"], b + 1)
                for n in range(2):
                    cols = slice(WHOLE * SUPC, COLS)
                    dve.scalar_tensor_tensor(by_super(based_part[h][:, n, :]), by_super(bucket[:, cols]), iota[:, ds(b, 1)], base_part[n][:, ds(b, 1), :].rearrange("p a s -> p s a").broadcast_to([P, NSUP - WHOLE, SUPC]), ALU.is_equal, ALU.mult)
                dve.scalar_tensor_tensor(by_super(based[h]), by_super(bucket[:, 0:WHOLE * SUPC]), iota[:, ds(b, 1)], base[:, ds(b, 1), 0:WHOLE].rearrange("p a s -> p s a").broadcast_to([P, WHOLE, SUPC]), ALU.is_equal, ALU.mult).then_inc(S["based_ready"], 1)
            dve.sem_inc(S["based_used"], 1)
            with dve.Fori(0, NT // 2) as i:
                for h in range(2):
                    add_base(2 * i + h, h)
            add_base(NT - 1, 0)
            dve.wait_ge(S["based_used"], NT + 3)
            for k, c0, c1 in BANKS:
                last = dve.tensor_scalar(posi[:, c0:c1], ps[:, k, 0:c1 - c0], 1.0, None, ALU.subtract)
            step(last)
            step(dve.tensor_scalar(loi[:, :], posi[:, :], 3, P - 1, ALU.logical_shift_right, ALU.bitwise_and))
            step(dve.tensor_copy(slotp[:, :], loi[:, :]))
            step(dve.tensor_scalar(loi[:, :], posi[:, :], 10, 3, ALU.logical_shift_right, ALU.logical_shift_left))
            step(dve.tensor_scalar(dsti[:, :], posi[:, :], BLK - 1, None, ALU.bitwise_and))
            step(dve.tensor_tensor(loi[:, :], loi[:, :], dsti[:, :], ALU.bitwise_or))
            step(dve.tensor_copy(slotc[:, :], loi[:, :]))
            with dve.Fori(BY_ACT, NT // TURN) as i:
                for u in range(TURN):
                    t = i * TURN + u
                    dve.tensor_scalar(tile(xn, t), tile(acc, t), mean[:, ds(t, 1)], rstd[:, ds(t, 1)], ALU.subtract, ALU.mult).then_inc(S["normed"], 1)
            step.freeze()

            def make_hot(n, q):
                b, h, col, m = n * NBAT + q, q % HRING, n * SUPC + q * BAT, SHARE["dve"].stop
                c = ds(col, BAT)
                dve.wait_ge(S["sorted_batches"], b + 1)
                dve.tensor_tensor(hot_col[:, h, :, :], wide(iota[:, 0:64], [P, BAT, 64], 1), wide(slotc[:, c], [P, BAT, 64], 2), ALU.is_equal).then_inc(S["col_hot"], 1)
                dve.tensor_tensor(hot_part[:, h, :, :], wide(iota[:, :], [P, BAT, P], 1), wide(slotp[:, c], [P, BAT, P], 2), ALU.is_equal)
                dve.wait_ge(S["col_hot"], b + 1)
                dve.tensor_tensor(hot_rec[:, h, 0:m, :, :], wide(hot_col[:, h, 0:m, :], [P, m, 64, REC], 3), wide(vals[:, ds(col, m), :], [P, m, 64, REC], 2), ALU.mult).then_inc(S["pair_ready"], 1)

            def destinations(i):
                if not is_first(i, 1):
                    for g in range(NG8):
                        dve.wait_ge(scattered[g], 16 * i)
                at = ds(i, 1)
                shape = [P, NG8, NT + 1]
                step(dve.tensor_tensor(passed[:, :, :], block_no[:, :].rearrange("p (g b) -> p g b", b=1).broadcast_to(shape), lstart[:, at, :].broadcast_to(shape), ALU.is_ge))
                step(dve.tensor_tensor(passed[:, :, :], passed[:, :, :], jump[:, at, :].broadcast_to(shape), ALU.mult))
                step(dve.tensor_reduce(moved[:, :], passed[:, :, :], AX.X, ALU.add))
                dve.tensor_tensor(dest[:, :], moved[:, :], block_no[:, :], ALU.add).then_inc(S["dest_ready"], 1)

            def superchunk(n):
                for q in range(NBAT):
                    make_hot(n, q)
                    if q == 1 and not is_first(n, 1):
                        destinations(n - 1)
            over_superchunks(dve, superchunk, step, 3)
            destinations(NSUP - 1)
            def low_part(n):
                dve.wait_ge(S["proj"], n + 2)
                dve.tensor_scalar(low, ps[:, 3, 0:C], 0.0, None, ALU.min).then_inc(S["feat_low"], 1)

            def high_part(n):
                dve.wait_ge(S["third"], n + 1)
                dve.wait_ge(S["feat_exp"], n + 1)
                dve.scalar_tensor_tensor(feat, ps[:, 3, 0:C], 0.0, grown, ALU.max, ALU.add).then_inc(S["feat_ready"], 1)

            tile = lambda a, t: a[:, ds(t, 1), :].rearrange("p a c -> p (a c)")
            for n, ks in enumerate(ROUNDS):
                w, at = len(ks) * P, slice(ks[0] * P, (ks[-1] + 1) * P)
                dve.wait_ge(S["transposed"], n + 1)
                step(dve.tensor_copy(geti[:, 0:w], ps[:, n % 2, 0:w]))
                step(dve.tensor_scalar(getl[:, 0:w], geti[:, 0:w], P - 1, None, ALU.bitwise_and))
                dve.tensor_scalar(gidx[:, at], geti[:, 0:w], 7, None, ALU.logical_shift_right)
                step(dve.tensor_copy(slo[:, at], getl[:, 0:w]))
                dve.engine_nop().then_inc(S["unpacked"], 1)
            dve.wait_ge(S["w_copied"], len(ROUNDS))
            dve.wait_ge(S["bucket_loaded"], 16)
            dve.sem_inc(S["added"], 2)

            def hot(q, u):
                dve.wait_ge(S["multiplied"], q + RING + 1 - HOT)
                dve.tensor_scalar(onehot[:, u, :], iota[:, :], slo[:, ds(q, 1)], sw[:, ds(q, 1)], ALU.is_equal, ALU.mult).then_inc(S["hot_ready"], 1)

            def buckets(n, count=STEP):
                return nc.values_load_multi_w_load_instructions(
                    group_bucket[0:1, ds(n * STEP, count)], engines=[mybir.EngineType.DVE], min_val=0, max_val=NT - 1,
                    skip_runtime_bounds_check_because="a count of NT comparisons less one, the first of which holds")[1]

            def groups(n, at, *js):
                for j in js:
                    g = n * STEP + j
                    for u in range(2):
                        hot(2 * g + 4 + u, (2 * j + 4 + u) % HOT)
                    b = at[j]
                    dve.wait_ge(S["multiplied"], RING + 2 * g + 2)
                    dve.wait_ge(S["added"], 2 + g)
                    dve.tensor_tensor(tile(acc, b), tile(acc, b), ps[:, j % 2, 0:C], ALU.add).then_inc(S["added"], 1)
            for q in range(4):
                hot(q, q)
            step.freeze()
            dve.wait_ge(S["rows_loaded"], 16 * 14)
            step(dve.tensor_scalar(rtemp, rtemp, 0.1, 5.0, ALU.max, ALU.min))
            step(dve.reciprocal(rtemp, rtemp))
            dve.wait_ge(S["wc_ps"], 1)
            parity = lambda a, e: a.rearrange("p (m e g) -> p e m g", e=2, g=D2)[:, e]
            for e in range(2):
                for k in range(2):
                    dve.tensor_tensor(parity(wc[:, k, :], e), parity(ps[:, 2 + k + 2 * e, :], e), wide(rtemp.rearrange("p (m e) -> p e m", e=2)[:, e, :], [P, 4, D2], 2), ALU.mult)
            three = lambda a: a.rearrange("p (n g) -> p n g", g=D2)
            split_bias(step, bias2[:, :], biasf[:, 1, 0:C], C)
            split_bias(step, biaso[:, :], biasf[:, 1, C:2 * C], C)
            for e in range(2):
                step(dve.tensor_tensor(parity(biasf[:, 1, :], e), parity(ps[0:3, 2 + 2 * e, :], 1 - e), wide(bsl, [3, 4, D2], 1), ALU.add))
            step(dve.tensor_tensor(three(biasf[:, 1, :]), three(biasf[:, 1, :]), wide(rtemp[0:3, :], [3, 8, D2], 2), ALU.mult))
            split_bias(step, bias_logit[:, :], biasf[:, 1, :], INNER)
            step(dve.memset(vone[:, :, P:P + 1], 1.0))
            step(dve.memset(kvd[:, :, :], 0.0))
            dve.engine_nop().then_inc(S["vone_set"], 1)
            dve.engine_nop().then_inc(S["wc_sb"], 1)

            step.freeze()
            with dve.Fori(0, NT) as t:
                at = buckets(t)
                groups(t, at, 0, 1)
                low_part(t)
                groups(t, at, 2)
                high_part(t)
                groups(t, at, 3, 4, 5)
            dve.wait_ge(S["kv_done"], 1)
            for g in range(2):
                for h in range(4):
                    rr = slice(32 * h, 32 * h + 32)
                    dve.tensor_copy(kvd[rr, g, 32 * h:32 * h + 32], ps[rr, 4 + g, 32 * h:32 * h + 32])
                    last = dve.tensor_copy(kvd[rr, g, P + h:P + h + 1], ps[rr, 4 + g, P:P + 1])
            step(last)
            dve.engine_nop().then_inc(S["kv_diag"], 1)
            step.freeze()
            with dve.Fori(0, NT) as t:
                step.loop(t, 4)
                at = buckets(t + NT)
                groups(t + NT, at, 0, 1)
                low_part(t + NT)
                groups(t + NT, at, 2)
                high_part(t + NT)
                groups(t + NT, at, 3, 4)
                dve.wait_ge(S["third"], t + NT + 2)
                heads = ps[:, 6:8, 0:132]
                step(dve.tensor_scalar(zden, heads[:, :, P:P + 4], 1e-6, None, ALU.add))
                step(dve.reciprocal(zden, zden))
                dve.tensor_tensor(tmp.rearrange("p (g h m) -> p g h m", g=2, h=4), heads[:, :, 0:P].rearrange("p g (h m) -> p g h m", h=4), wide(zden, [P, 2, 4, 32], 3), ALU.mult).then_inc(S["res"], 1)
                dve.wait_ge(S["res"], t + 2)
                step(dve.tensor_tensor(tile(xn, t), tmp, tile(xn, t), ALU.add))
                step(dve.bn_stats(tile(stats, t), tile(xn, t)))
                groups(t + NT, at, 5)
            step.leave(NT)
            var_of_stats(step)
            dve.engine_nop().then_inc(S["var_ready"], 1)
            dve.wait_ge(S["rstd_root"], 2)
            step(dve.reciprocal(rstd[:, :], rstd[:, :]))

            def affine(t, n, to, center, scale):
                step(dve.scalar_tensor_tensor(tmp, tile(xn, t), center, rows[:, n, :], ALU.subtract, ALU.mult))
                return dve.scalar_tensor_tensor(to, tmp, scale, rows[:, n + 1, :], ALU.mult, ALU.add)
            step.freeze()
            def second(t):
                affine(t, 0, tile(xn, t), mean[:, ds(t, 1)], rstd[:, ds(t, 1)]).then_inc(S["mixed"], 1)

            def last_norm(t, more):
                n = t + 2 * NT
                at = buckets(n)
                groups(n, at, 0, 1, 2)
                if more:
                    second(t + 1)
                groups(n, at, 3)
                dve.wait_ge(S["third"], n + 2)
                dve.tensor_tensor(tile(xn, t), ps[:, 6, 0:C], tile(xn, t), ALU.add).then_inc(S["res"], 1)
                dve.wait_ge(S["res"], NT + t + 2)
                step(dve.bn_stats(tile(stats, t), tile(xn, t)))
                col = lambda k: tile(stats, t)[:, k:k + 1]
                dve.tensor_tensor(middle, col(1), col(4), ALU.add)
                dve.tensor_tensor(off, col(1), col(4), ALU.subtract)
                step(dve.tensor_tensor(spread, col(2), col(5), ALU.add))
                dve.tensor_scalar(middle, middle, 0.5, None, ALU.mult)
                dve.scalar_tensor_tensor(off, off, 0.25, off, ALU.mult, ALU.mult)
                step(dve.tensor_scalar(spread, spread, 1.0 / C, 1e-5, ALU.mult, ALU.add))
                dve.tensor_tensor(spread, spread, off, ALU.add).then_inc(S["row_var"], 1)
                groups(n, at, 4, 5)
                dve.wait_ge(S["row_root"], t + 1)
                step(dve.reciprocal(root, root))
                step(affine(t, 2, tile(xn, t), middle, root))
                dve.wait_ge(S["added"], 2 + n * STEP + STEP)
                step(dve.tensor_tensor(tile(acc, t), tile(acc, t), tile(xn, t), ALU.add))
            second(0)
            step.freeze()
            with dve.Fori(0, NT // 2) as i:
                step.loop(i, 16)
                for u in range(2):
                    last_norm(2 * i + u, True)
            step.leave(NT // 2)
            last_norm(NT - 1, False)
            step.freeze()
            for k in range((REST + RING - 1) // RING):
                count = min(STEP, REST // 2 - k * STEP)
                groups(3 * NT + k, buckets(3 * NT + k, count), *range(count))
            dve.wait_ge(S["added"], 2 + USED)
            with dve.Fori(0, NT // TURN) as i:
                for u in range(TURN):
                    t = i * TURN + u
                    dve.bn_stats(tile(stats, t), tile(acc, t)).then_inc(S["row_stats"], 1)
            dve.wait_ge(S["row_stats"], 2 * NT)
            var_of_stats(step)
            dve.engine_nop().then_inc(S["var_ready"], 1)
            dve.wait_ge(S["rstd_root"], 3)
            step(dve.reciprocal(rstd[:, :], rstd[:, :]))
            step(dve.memset(xs[:, :, C:C + 1], 1.0))

            def normed(t, h):
                dve.tensor_scalar(xs[:, h, 0:C], tile(acc, t), mean[:, ds(t, 1)], rstd[:, ds(t, 1)], ALU.subtract, ALU.mult).then_inc(S["f_norm"], 1)

            def soften(t, h):
                if live(t, 1):
                    k = (h - 1) % 4
                    dve.wait_ge(S["f_exp"], t + 1)
                    step(dve.tensor_reduce(fsum[:, k, :], three(slices[:, k, :]), AX.X, ALU.add))
                    dve.reciprocal(fsum[:, k, :], fsum[:, k, :]).then_inc(S["f_sum"], 1)
                if live(t, 0):
                    dve.wait_ge(S["f_logit"], t + 1)
                    step(dve.tensor_reduce(fmax[:, h % 2, :], three(ps[:, h % 2, :]), AX.X, ALU.max))
                    dve.tensor_tensor(three(slices[:, h, :]), three(ps[:, h % 2, :]), wide(fmax[:, h % 2, :], [P, 8, D2], 2), ALU.subtract).then_inc(S["f_low"], 1)
                if live(t, -2):
                    if live(t, 2):
                        dve.wait_ge(S["f_pair"], t + 1)
                    normed(t + 2, (h + 2) % 4)
            step.freeze()
            normed(0, 0)
            normed(1, 1)
            pipeline(dve, soften, step, 2)
            dve.wait_ge(S["tok_ps"], 1)
            step(dve.tensor_scalar(tden, ps[:, 4:8, C], 1e-5, None, ALU.add))
            step(dve.reciprocal(tden, tden))
            step(dve.tensor_tensor(token[:, :, :], ps[:, 4:8, 0:C + 1], wide(tden, [P, 4, C + 1], 2), ALU.mult))
            dve.engine_nop().then_inc(S["tok_sb"], 1)
            dve.wait_ge(S["tok_ps"], 2)
            dve.tensor_copy(tokenT[:, 0, :], ps[:, 0, :])
            dve.tensor_copy(tokenT[:, 1, :], ps[:, 1, :])
            step(dve.tensor_copy(ratio, ps[0:1, 2, :]))
            dve.engine_nop().then_inc(S["tok_sb"], 1)
            dve.wait_ge(S["tok_ps"], 3)
            step(dve.tensor_copy(tokf, ps[0:D2, 3, :]))
            dve.engine_nop().then_inc(S["tok_sb"], 1)
            dve.wait_ge(S["tok_ps"], 4)
            dve.tensor_copy(qk[:, 0, :], ps[0:D2, 0, :])
            dve.tensor_copy(qk[:, 1, :], ps[0:D2, 1, :])
            step(dve.tensor_copy(vtok, ps[0:D2, 2, :]))
            dve.engine_nop().then_inc(S["tok_sb"], 1)
            dve.wait_ge(S["tok_ps"], 5)
            step(dve.tensor_reduce(amax, three(ps[0:D2, 3, :]), AX.X, ALU.max))
            step(dve.tensor_tensor(three(att), three(ps[0:D2, 3, :]), wide(amax, [D2, 8, D2], 2), ALU.subtract))
            for k in range(5):
                dve.engine_nop().then_inc(S["tok_sb"], 1)
            dve.wait_ge(S["tok_sb"], 10)
            step(dve.tensor_reduce(asum, three(att), AX.X, ALU.add))
            step(dve.reciprocal(asum, asum))
            step(dve.tensor_tensor(three(att), three(att), wide(asum, [D2, 8, D2], 2), ALU.mult))
            dve.engine_nop().then_inc(S["tok_sb"], 1)
            dve.wait_ge(S["tok_ps"], 6)
            step(dve.tensor_copy(attT, ps[0:D2, 0, :]))
            dve.engine_nop().then_inc(S["tok_sb"], 1)
            dve.wait_ge(S["tok_ps"], 7)
            step(dve.tensor_copy(outT, ps[0:D2, 1, :]))
            dve.engine_nop().then_inc(S["tok_sb"], 1)
            dve.wait_ge(S["tok_ps"], 8)
            for m in range(4):
                last = dve.tensor_copy(mout[:, m, :], ps[:, 4 + m, 0:C])
            step(last)
            dve.engine_nop().then_inc(S["tok_sb"], 1)

            def add_out(t, h):
                dve.wait_ge(S["out_ps"], t + 5)
                dve.tensor_tensor(tile(acc, t), tile(acc, t), ps[:, h, 0:C], ALU.add).then_inc(S["out_sum"], 1)
            with dve.Fori(0, NT // 4) as i:
                for h in range(4):
                    add_out(4 * i + h, h)
            add_out(NT - 1, 0)

        @block.tensor
        def _(pe):
            def seen(s, v):
                pe.wait_ge(s, v)
                pe.sem_inc(S["pace_pe"], 1)
            pe.wait_ge(S["consts"], 10)
            mm = pe.matmul
            for k in range(QN):
                mm(ps[:, k, 0:QW], zerob[:, 0:P], zerob[:, :], start=True, stop=False)
            pe.wait_ge(S["raw_loaded"], 48)
            for k in range(10):
                raw = raw_qkv[:, k, :] if k < 6 else (raw_w1 if k < 8 else raw_w2)[:, k % 2, :]
                if k >= 2:
                    pe.wait_ge(S["trans_sb"], k - 1)
                for c in range(2):
                    last = pe.transpose(ps[:, 6 + k % 2, c * P:(c + 1) * P], raw[:, c * P:(c + 1) * P], identf[:, :])
                last.then_inc(S["trans_ps"], 1)
            pe.wait_ge(S["trans_sb"], 10)

            def add_ranks(pair, h):
                seen(S["prod_odd" if h else "prod_even"], pair + 2)
                for k, c0, c1 in BANKS:
                    last = mm(ps[:, k, 0:c1 - c0], identb[:, :], ranked[h][:, c0:c1], start=False, stop=False)
                last.then_inc(S["prod_used"], 1)
            with pe.Fori(0, NT // 2) as i:
                for h in range(2):
                    add_ranks(i, h)
            add_ranks(NT // 2, 0)
            pe.wait_ge(S["count_copied"], NT + 2)
            flat = cnt[:, :, :].rearrange("p b s -> p (b s)")
            for k in range(3):
                last = mm(ps[:, 4 + k, 0:CW], before[:, :], flat[:, k * CW:(k + 1) * CW], start=True, stop=True)
            last.then_inc(S["count_sums"], 1)
            pe.wait_ge(S["sums_read"], 1)
            for k in range(3):
                last = mm(ps[:, 4 + k, 0:CW], onesb[:, :], flat[:, k * CW:(k + 1) * CW], start=True, stop=True)
            last.then_inc(S["count_sums"], 1)

            def add_bases(b, h):
                seen(S["based_ready"], b + 1)
                for k, c0, c1 in BANKS[0:WB]:
                    mm(ps[:, k, 0:c1 - c0], identf[:, :], based[h][:, c0:c1], start=False, stop=False)
                for k, c0, c1 in BANKS[WB:]:
                    for n in range(2):
                        last = mm(ps[:, k, 0:c1 - c0], identb[:, :], based_part[h][:, n, c0 - WB * QW:c1 - WB * QW], start=False, stop=False)
                last.then_inc(S["based_used"], 1)
            with pe.Fori(0, NT // 2) as i:
                for h in range(2):
                    add_bases(2 * i + h, h)
            add_bases(NT - 1, 0)
            for k, c0, c1 in BANKS:
                last = mm(ps[:, k, 0:c1 - c0], zerob[:, 0:P], zerob[:, 0:c1 - c0], start=False, stop=True)
            last.then_inc(S["based_used"], 1)
            pe.sem_inc(S["sorted_batches"], HRING)
            with pe.Fori(0, NSUP) as i:
                seen(S["local_copied"], i + 1)
                mm(ps[:, 7, 0:P], zerob[:, 0:P], zerob[:, 0:P], start=True, stop=False)
                with pe.Fori(0, NBAT // HRING) as j:
                    for h in range(HRING):
                        seen(S["pair_ready"], i * NBAT + j * HRING + h + 2)
                        seen(S["hot_pool"], i * NBAT + j * HRING + h + 1)
                        seen(S["hot_act"], i * NBAT + j * HRING + h + 1)
                        for u in range(BAT):
                            last = mm(ps[:, 7, 0:P], hot_part[:, h, u, :], hot_rec[:, h, u, :, :].rearrange("p a v -> p (a v)"), start=False, stop=False)
                        last.then_inc(S["sorted_batches"], 1)
                mm(ps[:, 7, 0:P], zerob[:, 0:P], zerob[:, 0:P], start=False, stop=True).then_inc(S["local_sorted"], 1)
            pe.wait_ge(S["wx_loaded"], 16)
            for m in range(4):
                if m >= 2:
                    pe.wait_ge(S["wxT_sb"], m - 1)
                for c in range(2):
                    last = pe.transpose(ps[:, 2 + m % 2, c * P:(c + 1) * P], raw_wx[:, c, m * P:(m + 1) * P], identf[:, :])
                last.then_inc(S["wxT_ps"], 1)
            pe.wait_ge(S["wxT_sb"], 4)
            pe.wait_ge(S["fold_loaded"], 48)
            for h in range(8):
                half_of = slice(h % 2 * D2, h % 2 * D2 + D2)
                for k in range(2):
                    mm(ps[:, 2 + k + 2 * (h % 2), h * D2:(h + 1) * D2], wxT[half_of, h // 2, k * P:(k + 1) * P], wslice[half_of, :], start=True, stop=True)
                free = h + 1 - 2 * (h % 2)
                last = mm(ps[0:3, 2 + 2 * (h % 2), free * D2:(free + 1) * D2], bxc[half_of, h // 2:h // 2 + 1].broadcast_to([D2, 3]), wslice[half_of, :], start=True, stop=True)
            last.then_inc(S["wc_ps"], 1)
            for n, ks in enumerate(ROUNDS):
                pe.wait_ge(loaded_back[n], 16)
                if n >= 2:
                    pe.wait_ge(S["unpacked"], n - 1)
                    pe.wait_ge(S["w_copied"], n - 1)
                for j, k in enumerate(ks):
                    for v in range(REC):
                        last = pe.transpose(ps[:, 6 * v + n % 2, j * P:(j + 1) * P], back[:, k, v::REC], identf[:, :])
                last.then_inc(S["transposed"], 1)
            pe.wait_ge(S["unpacked"], len(ROUNDS))
            pe.wait_ge(S["w_copied"], len(ROUNDS))
            pe.sem_inc(S["multiplied"], RING)
            pe.wait_ge(S["wc_sb"], 1)

            def groups(n, *js):
                for j in js:
                    for u in range(2):
                        q = 2 * j + u
                        seen(gathered[q], 16 * n + 16)
                        seen(S["hot_ready"], RING * n + q + 1)
                        if u == 0:
                            seen(S["added"], n * STEP + j + 1)
                        mm(ps[:, j % 2, 0:C], onehot[:, q % HOT, :], gath[:, q, :], start=u == 0, stop=u == 1).then_inc(S["multiplied"], 1)

            def turn(n, t):
                seen(S["xt_sb"], n + 1)
                seen(S["cur_sb"], n + 1)
                for c in range(2):
                    last = pe.transpose(ps[:, 2, c * P:(c + 1) * P], xcur[:, c * P:(c + 1) * P], identf[:, :])
                last.then_inc(S["xt_ps"], 1)

            tile = lambda a, t: a[:, ds(t, 1), :].rearrange("p a c -> p (a c)")
            for g in range(2):
                mm(ps[:, 4 + g, 0:P + 1], zerob[:, 0:P], zerob[:, 0:P + 1], start=True, stop=False)

            def kv_tile(t, edge):
                turn(t, t)
                groups(t, 0, 1)
                seen(S["feat_ready"], t + 1)
                seen(S["v_sb"], t + 1)
                seen(S["xt_sb"], t + 2)
                for v in range(2):
                    for c in range(2):
                        last = mm(ps[:, 3 + 3 * v, 0:C], xT[:, c, :], wqkvT[:, c, C * (1 + v):C * (2 + v)], start=c == 0, stop=c == 1)
                last.then_inc(S["proj"], 1)
                groups(t, 2, 3)
                seen(S["feat_ready"], t + 2)
                seen(S["v_sb"], t + 2)
                r = TAIL if edge else P
                for g in range(2):
                    last = mm(ps[:, 4 + g, 0:P + 1], feat[0:r, g * P:(g + 1) * P], vone[0:r, g, :], start=False, stop=edge)
                last.then_inc(S["third"], 1)
                groups(t, 4, 5)
            with pe.Fori(0, NT - 1) as t:
                kv_tile(t, False)
            kv_tile(NT - 1, True)
            pe.wait_ge(S["third"], NT + 1)
            pe.sem_inc(S["kv_done"], 1)
            pe.wait_ge(S["kv_diag"], 1)
            with pe.Fori(0, NT) as t:
                turn(t + NT, t)
                groups(t + NT, 0, 1)
                seen(S["feat_ready"], t + NT + 1)
                seen(S["xt_sb"], t + NT + 2)
                for g in range(2):
                    for c in range(2):
                        last = mm(ps[:, 3, g * P:(g + 1) * P], wqkvT[:, c, g * P:(g + 1) * P], xT[:, c, :], start=c == 0, stop=c == 1)
                last.then_inc(S["proj"], 1)
                groups(t + NT, 2, 3)
                seen(S["res"], t + 1)
                seen(S["feat_ready"], t + NT + 2)
                for g in range(2):
                    last = mm(ps[:, 6 + g, 0:132], feat[:, g * P:(g + 1) * P], kvd[:, g, :], start=True, stop=True)
                last.then_inc(S["third"], 1)
                groups(t + NT, 4, 5)
            with pe.Fori(0, NT) as t:
                n = t + 2 * NT
                turn(n, t)
                groups(n, 0, 1)
                seen(S["feat_ready"], n + 1)
                seen(S["xt_sb"], n + 2)
                for g in range(2):
                    for c in range(2):
                        last = mm(ps[:, 3, g * P:(g + 1) * P], w1T[:, c, g * P:(g + 1) * P], xT[:, c, :], start=c == 0, stop=c == 1)
                last.then_inc(S["proj"], 1)
                groups(n, 2, 3)
                seen(S["res"], t + NT + 1)
                seen(S["feat_ready"], n + 2)
                for g in range(2):
                    mm(ps[:, 6, 0:C], feat[:, g * P:(g + 1) * P], w2T[:, g, :], start=g == 0, stop=False)
                mm(ps[:, 6, 0:C], onesb[0:3, :], bias2[:, :], start=False, stop=True).then_inc(S["third"], 1)
                groups(n, 4, 5)
            for k in range((REST + RING - 1) // RING):
                groups(3 * NT + k, *range(min(STEP, REST // 2 - k * STEP)))

            def ffn_step(t, h):
                if live(t, 0):
                    seen(S["f_norm"], t + 1)
                    for c in range(2):
                        last = pe.transpose(ps[:, 2, c * P:(c + 1) * P], xs[:, h, c * P:(c + 1) * P], identf[:, :])
                    last.then_inc(S["f_xT"], 1)
                if live(t, 2):
                    k = (h - 2) % 4
                    edge = isinstance(t, int) and t - 2 == NT - 1
                    r = TAIL if edge else P
                    seen(S["f_slice"], t - 1)
                    for m in range(4):
                        mm(ps[:, 4 + m, 0:C + 1], slices[0:r, k, m * P:(m + 1) * P], xs[0:r, k, :], start=False, stop=edge)
                    seen(S["f_sTsb"], t - 1)
                    for m in range(4):
                        last = pe.transpose(ps[:, 3, m * P:(m + 1) * P], slices[:, k, m * P:(m + 1) * P], identf[:, :])
                    last.then_inc(S["f_pair"], 1)
                if live(t, 0):
                    seen(S["f_xsT"], t + 1)
                    for c in range(2):
                        mm(ps[:, h % 2, :], xsT[:, c, :], wc[:, c, :], start=c == 0, stop=False)
                    mm(ps[:, h % 2, :], onesb[0:3, :], bias_logit[:, :], start=False, stop=True).then_inc(S["f_logit"], 1)
            pe.wait_ge(S["rstd_root"], 3)
            for m in range(4):
                mm(ps[:, 4 + m, 0:C + 1], zerob[:, 0:P], zerob[:, 0:C + 1], start=True, stop=False)
            pe.sem_inc(S["f_pair"], 1)
            pipeline(pe, ffn_step)
            pe.wait_ge(S["f_pair"], NT + 2)
            pe.sem_inc(S["tok_ps"], 1)
            pe.wait_ge(S["tok_sb"], 1)
            pe.wait_ge(S["late_loaded"], 16)
            for m in range(4):
                for c in range(2):
                    pe.transpose(ps[:, c, m * P:(m + 1) * P], token[:, m, c * P:(c + 1) * P], identf[:, :])
                last = pe.transpose(ps[0:1, 2, m * P:(m + 1) * P], token[:, m, C:C + 1], identf[:, :])
            last.then_inc(S["tok_ps"], 1)
            pe.wait_ge(S["tok_sb"], 2)
            pe.wait_ge(S["f_sTsb"], NT + 1)
            for h in range(8):
                hh = slice(h * D2, (h + 1) * D2)
                for c in range(2):
                    mm(ps[0:D2, 3, hh], wfx[:, c, hh], tokenT[:, c, hh], start=c == 0, stop=False)
                last = mm(ps[0:D2, 3, hh], bfx[:, hh], ratio[:, hh], start=False, stop=True)
            last.then_inc(S["tok_ps"], 1)
            pe.wait_ge(S["tok_sb"], 3)
            mm(ps[0:D2, 0, :], wq, tokf, start=True, stop=True)
            mm(ps[0:D2, 1, :], wk, tokf, start=True, stop=True)
            for h in range(8):
                hh = slice(h * D2, (h + 1) * D2)
                last = mm(ps[0:D2, 2, hh], tokf[:, hh], wv, start=True, stop=True)
            last.then_inc(S["tok_ps"], 1)
            pe.wait_ge(S["tok_sb"], 4)
            for h in range(8):
                hh = slice(h * D2, (h + 1) * D2)
                last = mm(ps[0:D2, 3, hh], qk[:, 0, hh], qk[:, 1, hh], start=True, stop=True)
            last.then_inc(S["tok_ps"], 1)
            pe.wait_ge(S["tok_sb"], 11)
            for h in range(8):
                hh = slice(h * D2, (h + 1) * D2)
                last = pe.transpose(ps[0:D2, 0, hh], att[:, hh], identf[0:D2, 0:D2])
            last.then_inc(S["tok_ps"], 1)
            pe.wait_ge(S["tok_sb"], 12)
            for h in range(8):
                hh = slice(h * D2, (h + 1) * D2)
                last = mm(ps[0:D2, 1, hh], vtok[:, hh], attT[:, hh], start=True, stop=True)
            last.then_inc(S["tok_ps"], 1)
            pe.wait_ge(S["tok_sb"], 13)
            for h in range(8):
                last = mm(ps[h % 2 * D2:h % 2 * D2 + D2, 4 + h // 2, 0:C], outT[:, h * D2:(h + 1) * D2], wout[:, h, :], start=True, stop=True)
            last.then_inc(S["tok_ps"], 1)
            pe.wait_ge(S["tok_sb"], 14)

            def project(t, h):
                seen(S["sl_sb"], t + 1)
                for m in range(4):
                    mm(ps[:, h, 0:C], slcur[:, h, m, :], mout[:, m, :], start=m == 0, stop=False)
                mm(ps[:, h, 0:C], onesb[0:3, :], biaso[:, :], start=False, stop=True).then_inc(S["out_ps"], 1)
            with pe.Fori(0, NT // 4) as i:
                for h in range(4):
                    seen(S["out_sum"], 4 * i + h + 1)
                    project(4 * i + h, h)
            seen(S["out_sum"], NT)
            project(NT - 1, 0)


_INS = ["x", "src", "dst", "edge_weight", "L0_mix_Wqkv", "L0_mix_ln1_g", "L0_mix_ln1_b", "L0_mix_W1", "L0_mix_b1",
        "L0_mix_W2", "L0_mix_b2", "L0_mix_ln2_g", "L0_mix_ln2_b", "L0_ffn_W_fx", "L0_ffn_b_fx", "L0_ffn_W_x",
        "L0_ffn_b_x", "L0_ffn_W_slice", "L0_ffn_b_slice", "L0_ffn_W_q", "L0_ffn_W_k", "L0_ffn_W_v", "L0_ffn_W_out",
        "L0_ffn_b_out", "L0_ffn_temperature"]


def kernel(**inputs):
    import numpy as np
    import concourse.bacc as bacc
    from concourse.bass_utils import run_bass_kernel_spmd

    nc = bacc.Bacc("TRN2", target_bir_lowering=False, num_devices=1)
    arrays, args = {}, []
    for name in _INS:
        a = np.ascontiguousarray(inputs[name])
        arrays[f"in_{name}"] = a
        args.append(nc.dram_tensor(f"in_{name}", a.shape, mybir.dt.from_np(a.dtype), kind="ExternalInput").ap())
    args.append(nc.dram_tensor("out_rows", (N, C), F32, kind="ExternalOutput").ap())
    program(nc, *args)
    result = run_bass_kernel_spmd(nc, [arrays], core_ids=[0])
    return result.results[0]["out_rows"]
```
